# Optimizing a Trainium2 kernel written in Bass

```python
import numpy as np
import jax
import jax.numpy as jnp

def _softmax(x, axis=-1):
    return jax.nn.softmax(x, axis=axis)

def _gelu(x):
    return jax.nn.gelu(x, approximate=True)

def _silu(x):
    return jax.nn.silu(x)

def _sigmoid(x):
    return jax.nn.sigmoid(x)

def _layernorm(x, axis=-1, eps=1e-05):
    m = jnp.mean(x, axis=axis, keepdims=True)
    v = jnp.var(x, axis=axis, keepdims=True)
    return (x - m) / jnp.sqrt(v + eps)

def _scatter_add(tgt, idx, src, axis=0):
    return tgt.at[idx].add(src)

def _segment_sum(src, seg, n):
    return jax.ops.segment_sum(src, seg, n)
kernel_name = 'mk_adaln_ffn_d2_seqx_r8_9c0ee9'

def setup_inputs(seed: int=0):
    np.random.seed(seed)
    _w = jnp.asarray

    def _rec_inputs():
        import jax
        import jax.numpy as jnp
        _rk = jax.random.key(seed)
        x = -7.109e-05 + 0.9999 * jax.random.normal(jax.random.fold_in(_rk, 1), (32, 32, 256), jnp.float32)
        _lenS = 32 - jax.random.randint(jax.random.fold_in(_rk, 7), (32,), 0, max(1, 32 // 4) + 1, jnp.int32)
        _lenS2 = 32 - jax.random.randint(jax.random.fold_in(_rk, 8), (32,), 0, max(1, 32 // 4) + 1, jnp.int32)
        itok_B_1_198 = jax.random.randint(jax.random.fold_in(_rk, 11), (32,), 1, 199, jnp.int32)
        itok_B_0_6 = jax.random.randint(jax.random.fold_in(_rk, 12), (32,), 0, 7, jnp.int32)
        return (x, itok_B_1_198, itok_B_0_6)
    x, itok_B_1_198, itok_B_0_6 = _rec_inputs()

    def _L0_cond_setup():
        import jax, jax.numpy as jnp
        import numpy as np
        B, C, T = (128, 32, 256)
        S, D = (200, 32)
        key = jax.random.key(seed)
        k1, k2, k3 = jax.random.split(key, 3)
        x = jax.random.normal(k1, (B, C, T), dtype=jnp.float32)
        conditions = jax.random.randint(k2, (B,), 0, S, dtype=jnp.int64)
        weights = jax.random.normal(k3, (S, C, D), dtype=jnp.float32) / jnp.sqrt(jnp.float32(C))
        return {'x': x, 'conditions': conditions, 'weights': weights}
    _L0_cond_all = _L0_cond_setup()
    _L0_cond_in = {k: v for k, v in _L0_cond_all.items() if k in ('weights',)}
    del _L0_cond_all

    def _L0_ffn_setup():
        import jax, jax.numpy as jnp
        import numpy as np
        B_, S, D = (2, 256, 256)
        F_ = 1024
        R = 16
        H = 16
        HD = D // H
        MOD_SCALE = 0.1
        EPS = 1e-06

        def _rmsnorm(x, w):
            v = jnp.mean(x * x, axis=-1, keepdims=True)
            return x * jax.lax.rsqrt(v + EPS) * w

        def _attention(x, Wq, Wk, Wv, Wo):
            b, s, d = x.shape
            q = (x @ Wq.T).reshape(b, s, H, HD)
            k = (x @ Wk.T).reshape(b, s, H, HD)
            v = (x @ Wv.T).reshape(b, s, H, HD)
            scores = jnp.einsum('bqhd,bkhd->bhqk', q, k) / np.sqrt(HD).astype(np.float32)
            causal = jnp.tril(jnp.ones((s, s), bool))
            scores = jnp.where(causal, scores, jnp.finfo(scores.dtype).min)
            probs = jax.nn.softmax(scores, axis=-1)
            out = jnp.einsum('bhqk,bkhd->bqhd', probs, v).reshape(b, s, d)
            return out @ Wo.T
        key = jax.random.key(seed)
        ks = jax.random.split(key, 12)
        sd = 0.02
        return {'hidden_states': jax.random.normal(ks[0], (B_, S, D), jnp.float32), 'ln1_w': jnp.ones((D,), jnp.float32), 'ln2_w': jnp.ones((D,), jnp.float32), 'Wq': jax.random.normal(ks[1], (D, D), jnp.float32) * sd, 'Wk': jax.random.normal(ks[2], (D, D), jnp.float32) * sd, 'Wv': jax.random.normal(ks[3], (D, D), jnp.float32) * sd, 'Wo': jax.random.normal(ks[4], (D, D), jnp.float32) * sd, 'A': jax.random.normal(ks[5], (D, R), jnp.float32) * (0.01 / np.sqrt(D)), 'B': jax.random.normal(ks[6], (R, F_), jnp.float32) * (0.01 / np.sqrt(R)), 'W_in_base': jax.random.normal(ks[7], (F_, D), jnp.float32) * sd, 'W_up_base': jax.random.normal(ks[8], (F_, D), jnp.float32) * sd, 'W_down': jax.random.normal(ks[9], (D, F_), jnp.float32) * sd}
    _L0_ffn_all = _L0_ffn_setup()
    _L0_ffn_in = {k: v for k, v in _L0_ffn_all.items() if k in ('ln1_w', 'ln2_w', 'Wq', 'Wk', 'Wv', 'Wo', 'A', 'B', 'W_in_base', 'W_up_base', 'W_down')}
    del _L0_ffn_all

    def _L1_cond_setup():
        import jax, jax.numpy as jnp
        import numpy as np
        B, T, D_IN, D_OUT = (16, 256, 256, 256)
        N_ADAPTERS, RANK = (8, 16)
        key = jax.random.key(seed)
        k_x, k_w, k_a, k_b, k_s, k_idx = jax.random.split(key, 6)
        x = jax.random.normal(k_x, (B, T, D_IN), dtype=jnp.float32)
        W = jax.random.normal(k_w, (D_OUT, D_IN), dtype=jnp.float32) * (1.0 / np.sqrt(D_IN))
        A = jax.random.normal(k_a, (N_ADAPTERS, RANK, D_IN), dtype=jnp.float32) * 0.02
        Bm = jax.random.normal(k_b, (N_ADAPTERS, D_OUT, RANK), dtype=jnp.float32) * 0.02
        scalings = jnp.ones((N_ADAPTERS,), dtype=jnp.float32)
        adapter_idx = jax.random.randint(k_idx, (B,), 0, N_ADAPTERS, dtype=jnp.int32)
        return {'x': x, 'W': W, 'A': A, 'Bm': Bm, 'scalings': scalings, 'adapter_idx': adapter_idx}
    _L1_cond_all = _L1_cond_setup()
    _L1_cond_in = {k: v for k, v in _L1_cond_all.items() if k in ('W', 'A', 'Bm', 'scalings')}
    del _L1_cond_all

    def _L1_ffn_setup():
        import jax, jax.numpy as jnp
        import numpy as np
        B, S, H = (2, 256, 256)
        E, K = (16, 4)
        I_MOE, I_SH = (176, 704)
        key = jax.random.key(seed)
        ks = jax.random.split(key, 9)

        def w(k, shape, fan_in):
            return jax.random.normal(k, shape, jnp.float32) * fan_in ** (-0.5)
        return {'hidden_states': jax.random.normal(ks[0], (B, S, H), jnp.float32), 'router_w': w(ks[1], (E, H), H), 'w_gate': w(ks[2], (E, H, I_MOE), H), 'w_up': w(ks[3], (E, H, I_MOE), H), 'w_down': w(ks[4], (E, I_MOE, H), I_MOE), 'sh_gate': w(ks[5], (H, I_SH), H), 'sh_up': w(ks[6], (H, I_SH), H), 'sh_down': w(ks[7], (I_SH, H), I_SH), 'sh_gate_w': w(ks[8], (H, 1), H)}
    _L1_ffn_all = _L1_ffn_setup()
    _L1_ffn_in = {k: v for k, v in _L1_ffn_all.items() if k in ('router_w', 'w_gate', 'w_up', 'w_down', 'sh_gate', 'sh_up', 'sh_down', 'sh_gate_w')}
    del _L1_ffn_all
    return {'x': x, 'itok_B_1_198': itok_B_1_198, 'itok_B_0_6': itok_B_0_6, 'L0_cond_weights': _L0_cond_in['weights'], 'L0_ffn_ln1_w': _L0_ffn_in['ln1_w'], 'L0_ffn_ln2_w': _L0_ffn_in['ln2_w'], 'L0_ffn_Wq': _L0_ffn_in['Wq'], 'L0_ffn_Wk': _L0_ffn_in['Wk'], 'L0_ffn_Wv': _L0_ffn_in['Wv'], 'L0_ffn_Wo': _L0_ffn_in['Wo'], 'L0_ffn_A': _L0_ffn_in['A'], 'L0_ffn_B': _L0_ffn_in['B'], 'L0_ffn_W_in_base': _L0_ffn_in['W_in_base'], 'L0_ffn_W_up_base': _L0_ffn_in['W_up_base'], 'L0_ffn_W_down': _L0_ffn_in['W_down'], 'L1_cond_W': _L1_cond_in['W'], 'L1_cond_A': _L1_cond_in['A'], 'L1_cond_Bm': _L1_cond_in['Bm'], 'L1_cond_scalings': _L1_cond_in['scalings'], 'L1_ffn_router_w': _L1_ffn_in['router_w'], 'L1_ffn_w_gate': _L1_ffn_in['w_gate'], 'L1_ffn_w_up': _L1_ffn_in['w_up'], 'L1_ffn_w_down': _L1_ffn_in['w_down'], 'L1_ffn_sh_gate': _L1_ffn_in['sh_gate'], 'L1_ffn_sh_up': _L1_ffn_in['sh_up'], 'L1_ffn_sh_down': _L1_ffn_in['sh_down'], 'L1_ffn_sh_gate_w': _L1_ffn_in['sh_gate_w']}

def reference(x, itok_B_1_198, itok_B_0_6, L0_cond_weights, L0_ffn_ln1_w, L0_ffn_ln2_w, L0_ffn_Wq, L0_ffn_Wk, L0_ffn_Wv, L0_ffn_Wo, L0_ffn_A, L0_ffn_B, L0_ffn_W_in_base, L0_ffn_W_up_base, L0_ffn_W_down, L1_cond_W, L1_cond_A, L1_cond_Bm, L1_cond_scalings, L1_ffn_router_w, L1_ffn_w_gate, L1_ffn_w_up, L1_ffn_w_down, L1_ffn_sh_gate, L1_ffn_sh_up, L1_ffn_sh_down, L1_ffn_sh_gate_w):
    import jax
    import jax.numpy as jnp

    def _L0_cond_ref(x, conditions, weights):
        import jax, jax.numpy as jnp
        import numpy as np
        B, C, T = (128, 32, 256)
        S, D = (200, 32)
        w = weights[conditions]
        return jnp.einsum('bct,bcd->bdt', x, w)

    def _L0_ffn_ref(hidden_states, ln1_w, ln2_w, Wq, Wk, Wv, Wo, A, B, W_in_base, W_up_base, W_down):
        import jax, jax.numpy as jnp
        import numpy as np
        B_, S, D = (2, 256, 256)
        F_ = 1024
        R = 16
        H = 16
        HD = D // H
        MOD_SCALE = 0.1
        EPS = 1e-06

        def _rmsnorm(x, w):
            v = jnp.mean(x * x, axis=-1, keepdims=True)
            return x * jax.lax.rsqrt(v + EPS) * w

        def _attention(x, Wq, Wk, Wv, Wo):
            b, s, d = x.shape
            q = (x @ Wq.T).reshape(b, s, H, HD)
            k = (x @ Wk.T).reshape(b, s, H, HD)
            v = (x @ Wv.T).reshape(b, s, H, HD)
            scores = jnp.einsum('bqhd,bkhd->bhqk', q, k) / np.sqrt(HD).astype(np.float32)
            causal = jnp.tril(jnp.ones((s, s), bool))
            scores = jnp.where(causal, scores, jnp.finfo(scores.dtype).min)
            probs = jax.nn.softmax(scores, axis=-1)
            out = jnp.einsum('bhqk,bkhd->bqhd', probs, v).reshape(b, s, d)
            return out @ Wo.T
        residual = hidden_states
        x = _rmsnorm(hidden_states, ln1_w)
        attn = _attention(x, Wq, Wk, Wv, Wo)
        mod = MOD_SCALE * jnp.tanh(attn @ A)
        h = _rmsnorm(residual, ln2_w)
        gate_pre = h @ W_in_base.T + mod * (h @ A) @ B
        gate = jax.nn.silu(gate_pre)
        up = h @ W_up_base.T
        mlp_out = gate * up @ W_down.T
        return residual + mlp_out

    def _L1_cond_ref(x, W, A, Bm, scalings, adapter_idx):
        import jax, jax.numpy as jnp
        import numpy as np
        B, T, D_IN, D_OUT = (16, 256, 256, 256)
        N_ADAPTERS, RANK = (8, 16)
        H = jnp.einsum('btd,od->bto', x, W)
        A_b = A[adapter_idx]
        B_b = Bm[adapter_idx]
        s_b = scalings[adapter_idx]
        xa = jnp.einsum('btd,brd->btr', x, A_b)
        delta = jnp.einsum('btr,bor->bto', xa, B_b)
        delta = jax.lax.stop_gradient(delta * s_b[:, None, None])
        return H + delta

    def _L1_ffn_ref(hidden_states, router_w, w_gate, w_up, w_down, sh_gate, sh_up, sh_down, sh_gate_w):
        import jax, jax.numpy as jnp
        import numpy as np
        B, S, H = (2, 256, 256)
        E, K = (16, 4)
        I_MOE, I_SH = (176, 704)
        orig = hidden_states.shape
        h = hidden_states.reshape(-1, orig[-1])
        N = h.shape[0]
        logits = h @ router_w.T
        probs = jax.nn.softmax(logits.astype(jnp.float32), axis=-1)
        top_vals, top_idx = jax.lax.top_k(probs, K)
        top_vals = top_vals / jnp.maximum(top_vals.sum(-1, keepdims=True), 1e-09)
        top_vals = top_vals.astype(h.dtype)
        comb = jnp.zeros((N, E), h.dtype).at[jnp.arange(N)[:, None], top_idx].add(top_vals)
        g = jnp.einsum('nh,ehi->eni', h, w_gate)
        u = jnp.einsum('nh,ehi->eni', h, w_up)
        y = jnp.einsum('eni,eih->enh', jax.nn.silu(g) * u, w_down)
        routed = jnp.einsum('enh,ne->nh', y, comb)
        shared = jax.nn.silu(h @ sh_gate) * (h @ sh_up) @ sh_down
        sg = jax.nn.sigmoid(h @ sh_gate_w)
        return (routed + sg * shared).reshape(orig)
    x = x + _L0_ffn_ref(_L0_cond_ref(x, itok_B_1_198, L0_cond_weights), L0_ffn_ln1_w, L0_ffn_ln2_w, L0_ffn_Wq, L0_ffn_Wk, L0_ffn_Wv, L0_ffn_Wo, L0_ffn_A, L0_ffn_B, L0_ffn_W_in_base, L0_ffn_W_up_base, L0_ffn_W_down)
    x = x + _L1_ffn_ref(_L1_cond_ref(x, L1_cond_W, L1_cond_A, L1_cond_Bm, L1_cond_scalings, itok_B_0_6), L1_ffn_router_w, L1_ffn_w_gate, L1_ffn_w_up, L1_ffn_w_down, L1_ffn_sh_gate, L1_ffn_sh_up, L1_ffn_sh_down, L1_ffn_sh_gate_w)
    return x

_drawn_inputs = setup_inputs


def setup_inputs(seed=0):
    import zlib

    import numpy as np

    out = dict(_drawn_inputs(seed))
    spreads = {'L0_ffn_ln1_w': (1.0, 0.6), 'L0_ffn_ln2_w': (1.0, 0.6), 'L1_cond_scalings': (1.0, 0.6)}
    factors = {'L0_ffn_Wq': 200.0,
     'L0_ffn_Wk': 200.0,
     'L0_ffn_Wv': 200.0,
     'L0_ffn_Wo': 200.0,
     'L0_ffn_A': 193.095,
     'L0_ffn_B': 187.498}
    for name, (base, spread) in spreads.items():
        noise = np.random.default_rng([zlib.crc32(name.encode()), seed]).standard_normal(out[name].shape)
        drawn = base * np.exp(spread * noise) if base else spread * noise
        out[name] = jnp.asarray(drawn.astype(out[name].dtype))
    for name, factor in factors.items():
        out[name] = (out[name] * factor).astype(out[name].dtype)
    return out
```

```python
from contextlib import ExitStack

import numpy as np

import concourse.bass as bass
from concourse import mybir

F32 = mybir.dt.float32
BF16 = mybir.dt.bfloat16
I32 = mybir.dt.int32
U32 = mybir.dt.uint32
ALU = mybir.AluOpType
ACT = mybir.ActivationFunctionType
AX = mybir.AxisListType

P = 128
BATCH, SEQ, D = 32, 32, 256
TOK = BATCH * SEQ
TILES = TOK // P
HALF = TOK // 2
KC = D // P
HEADS, HD = 16, 16
FF = 1024
FC = FF // P
RANK = 16
COND = 200
EPS = 1e-6
NEG = -3.0e38
ADAPT = 8
EXP, TOPK = 16, 4
IM = 176
IH = IM // 2
SH = 704
SHC = [(f * P, min(P, SH - f * P)) for f in range((SH + P - 1) // P)]
SLOT_TILES = (TOK * TOPK + EXP * (P - 1)) // P
SLOTS = SLOT_TILES * P
ROW = D + 2 * EXP
NOWHERE = 1.0e6
PIPE0, RING = 2, 4
STEADY = range(PIPE0, SLOT_TILES - 1)
assert len(STEADY) % RING == 0 and PIPE0 % RING == 2

CONSTS = {}


def const_columns():
    at = 0
    for name, n in (("ident", P), ("batch_of", 4), ("head_of", 4), ("causal", 32), ("adapter_of", 1),
                    ("pos_of", 1), ("before", P), ("iota_e", EXP), ("tile_edge", TILES),
                    ("lower_e", EXP * EXP), ("iota_s", SLOT_TILES), ("dest", TILES * TOPK)):
        CONSTS[name] = (at, n)
        at += n
    return at


NCONST = const_columns()


def constants():
    p = np.arange(P)
    c = np.zeros((P, NCONST), np.float32)

    def put(name, a):
        at, n = CONSTS[name]
        c[:, at:at + n] = a

    put("ident", np.eye(P))
    put("batch_of", p[:, None] // SEQ == np.arange(4)[None])
    put("head_of", 0.25 * ((p[:, None] % 64) // HD == np.arange(4)[None]))
    put("causal", np.where(np.arange(SEQ)[None] <= p[:, None] % SEQ, 0.0, NEG))
    put("adapter_of", p[:, None] // RANK)
    put("pos_of", p[:, None] % SEQ)
    put("before", p[:, None] < p[None])
    put("iota_e", np.arange(EXP)[None])
    put("tile_edge", P * np.arange(TILES)[None])
    put("lower_e", (np.arange(EXP)[None] < np.arange(EXP)[:, None]).reshape(1, -1))
    put("iota_s", np.arange(SLOT_TILES)[None])
    n = np.arange(TILES)[None, :, None] * P + p[:, None, None]
    put("dest", (TOPK * n + np.arange(TOPK)[None, None]).reshape(P, -1))
    return c


def spread(ap, axis, n):
    v = ap.unsqueeze(axis)
    shape = list(v.shape)
    shape[axis] = n
    return v.broadcast_to(shape)


def program(nc, t):
    ctx = ExitStack()
    with ctx:
        top = [0]
        base = (nc.sbuf_base + 63) // 64 * 64
        nbytes = {F32: 4, BF16: 2, I32: 4, U32: 4}

        def sb(name, shape, dt=F32, at=None):
            size = int(np.prod(shape[1:])) * nbytes[dt]
            size = (size + 31) // 32 * 32
            if at is None:
                at = top[0]
                top[0] += size
            assert base + at + size <= nc.sbuf_usable_end, name
            h = nc.alloc_sbuf_tensor_at(name, shape, dt, offset=base + at)
            h_at[name] = (at, size)
            return h

        h_at = {}

        def after(name):
            return h_at[name][0] + h_at[name][1]

        def sem(name):
            return ctx.enter_context(nc.semaphore(name))

        consts = sb("consts", [P, NCONST])
        K = {n: consts[:, a:a + w] for n, (a, w) in CONSTS.items()}
        ident_b = sb("ident_b", [P, P], BF16)
        causal_b = sb("causal_b", [P, SEQ], BF16)
        before_b = sb("before_b", [P, P], BF16)
        ones_b = sb("ones_b", [P, P], BF16)
        cond_b = sb("cond_b", [P, TILES], I32)
        cond_rows = sb("cond_rows", [P, TILES], I32)
        norm_w = sb("norm_w", [P, 2, KC])
        ssq = sb("ssq", [P, TILES])
        msq = sb("msq", [P, TILES])
        rms = sb("rms", [P, TILES])
        rstd = sb("rstd", [P, TILES])
        peak = sb("peak", [P, 8, 16])
        total = sb("total", [P, 8, 16])
        rtotal = sb("rtotal", [P, 8, 16])
        adapter_b = sb("adapter_b", [P, BATCH], I32)
        scale_p = sb("scale_p", [P, 1])
        adapter_sel = sb("adapter_sel", [P, BATCH])
        res = sb("res", [P, TILES, D])
        zone_a = top[0]
        qx = sb("qx", [P, KC, BATCH, 4, SEQ])
        hn = sb("hn", [P, TILES, D], at=h_at["qx"][0])
        vbd = sb("vbd", [P, BATCH, 4, 64])
        xn1 = sb("xn1", [P, KC, TOK])
        kT = sb("kT", [P, KC, TOK])
        square = sb("square", [P, TILES, D], at=h_at["kT"][0])
        v_sb = sb("v_sb", [P, TILES, D])
        wqkv = sb("wqkv", [P, 3, KC, D])
        ex = sb("ex", [P, 4, 512])
        exT = sb("exT", [P, 2, 512])
        zone_a_end = top[0]
        xn2 = sb("xn2", [P, KC, TOK])
        attnT = sb("attnT", [P, KC, TOK])
        up = sb("up", [P, FC, TOK])
        wgath = sb("wgath", [P, TILES, SEQ], at=h_at["up"][0])
        wbd = sb("wbd", [P, TILES, 4, SEQ], at=after("wgath"))
        w_gu = sb("w_gu", [P, 2, KC, FF])
        w_dn = sb("w_dn", [P, FC, D])
        wo = sb("wo", [P, KC, D])
        a_sb = sb("a_sb", [P, KC, RANK])
        woa = sb("woa", [P, KC, RANK])
        b_sb = sb("b_sb", [RANK, FF])
        thm = sb("thm", [RANK, TOK], at=h_at["ex"][0])
        m_sb = sb("m_sb", [RANK, TOK], at=h_at["ex"][0] + 4096)
        e_gu = sb("e_gu", [P, EXP, KC, 2 * IM], at=zone_a)
        e_dn = sb("e_dn", [IH, EXP, 2, D], at=after("e_gu"))
        s_gu = sb("s_gu", [P, KC, 2 * SH], at=after("e_dn"))
        s_dn = sb("s_dn", [P, len(SHC), D], at=after("s_gu"))
        assert after("s_dn") <= h_at["ex"][0]
        w1 = sb("w1", [P, KC, D])
        bm = sb("bm", [P, D])
        aT = sb("aT", [P, KC, P])
        rw = sb("rw", [P, KC, EXP + 1])
        g_sb = sb("g_sb", [P, 2, 512], at=h_at["exT"][0])
        x1T = sb("x1T", [P, KC, TOK], at=h_at["attnT"][0])
        h1T = sb("h1T", [P, KC, TOK], at=h_at["xn2"][0])
        rows = sb("rows", [P, TILES, ROW], at=h_at["w_gu"][0])
        xam = sb("xam", [P, TOK], at=after("rows"))
        s_sil = sb("s_sil", [P, 2, 512], at=after("xam"))
        s_act = sb("s_act", [P, len(SHC), 512], at=h_at["up"][0])
        lgx = sb("lgx", [P, TILES, EXP], at=after("s_act"))
        lgm = sb("lgm", [P, 3, TILES], at=after("lgx"))
        top_v = sb("top_v", [P, TILES, 8], at=after("lgm"))
        top_i = sb("top_i", [P, TILES, 8], U32, at=after("top_v"))
        top_f = sb("top_f", [P, TILES, TOPK], at=after("top_i"))
        wts = sb("wts", [P, TILES, TOPK], at=after("top_f"))
        hot = sb("hot", [P, TILES, TOPK, EXP], at=after("wts"))
        prod = sb("prod", [P, TILES, TOPK, EXP], at=after("hot"))
        member = sb("member", [P, TILES, EXP], BF16, at=after("prod"))
        over = sb("over", [P, EXP, TILES], at=after("member"))
        ntile = sb("ntile", [P, EXP], at=after("over"))
        first = sb("first", [P, EXP], at=after("ntile"))
        last = sb("last", [P, EXP], at=after("first"))
        pairs = sb("pairs", [P, EXP, EXP], at=after("last"))
        where = sb("where", [P, TILES, EXP], at=after("pairs"))
        slot_f = sb("slot_f", [P, TILES * TOPK], at=after("where"))
        slot = sb("slot", [P, TILES * TOPK], I32, at=after("slot_f"))
        hot_s = sb("hot_s", [P, SLOT_TILES, EXP], at=after("slot"))
        hot_t = sb("hot_t", [P, SLOT_TILES, EXP], at=after("hot_s"))
        who_f = sb("who_f", [P, SLOT_TILES], at=after("hot_t"))
        who = sb("who", [P, SLOT_TILES], I32, at=after("who_f"))
        lg_sb = sb("lg_sb", [P, TILES, EXP + 1], at=after("who"))
        sgate = sb("sgate", [P, TILES], at=after("lg_sb"))
        assert after("sgate") <= after("up")
        fill = sb("fill", [P, ROW])
        slot_rows = sb("slot_rows", [P, RING, ROW])
        hT = sb("hT", [P, 2, KC, P], at=after("s_sil"))
        sil = sb("sil", [P, 2, IM], at=after("hT"))
        act = sb("act", [P, 2, IM], at=after("sil"))
        actT = sb("actT", [IH, 2, 2, P], at=after("act"))
        y = sb("y", [P, RING, D], at=after("actT"))
        pick = sb("pick", [P, RING, 2, EXP], at=after("y"))
        wd = sb("wd", [P, RING, 2], at=after("pick"))
        dest = sb("dest", [P, RING], I32, at=after("wd"))
        assert after("dest") <= after("b_sb")
        yk = sb("yk", [P, TILES, TOPK * D], at=zone_a)
        ysum = sb("ysum", [P, TILES, 2 * D], at=after("yk"))

        bank = [ctx.enter_context(nc.psum_tensor(f"bank{i}", [P, 512], F32)) for i in range(8)]

        slots_d = nc.dram_tensor("slots_d", (SLOTS, ROW), F32).ap()
        yk_d = nc.dram_tensor("yk_d", (TOK * TOPK, D), F32).ap()

        ld_const, ld_cond, ld_wqkv, ld_norm, ld_small = map(sem, ("ld_const", "ld_cond", "ld_wqkv", "ld_norm", "ld_small"))
        ld_x = [sem(f"ld_x{h}") for h in range(2)]
        ld_up, ld_gate, ld_down = map(sem, ("ld_up", "ld_gate", "ld_down"))
        ld_l1, ld_shared, ld_exp, ld_adapt = map(sem, ("ld_l1", "ld_shared", "ld_exp", "ld_adapt"))
        filled, fill_set = sem("filled"), sem("fill_set")
        dve_step = sem("dve_step")
        gathered, wbd_ready, hid_ready, ssq_ready, msq_ready = map(sem, ("gathered", "wbd_ready", "hid_ready", "ssq_ready", "msq_ready"))
        cond_ready, rms_ready, hn_ready, res_ready = map(sem, ("cond_ready", "rms_ready", "hn_ready", "res_ready"))
        bf_ready = sem("bf_ready")
        hid_kept, hnT_ready, xn_act, xn_dve = map(sem, ("hid_kept", "hnT_ready", "xn_act", "xn_dve"))
        qk_ready, v_ready, qx_ready, k_ready, v_kept = map(sem, ("qk_ready", "v_ready", "qx_ready", "k_ready", "v_kept"))
        vbd_zero, vbd_act, vbd_dve = sem("vbd_zero"), sem("vbd_act"), sem("vbd_dve")
        scored, shifted, exped, summed, normed, exT_ready, pv_ready, attn_ready = map(
            sem, ("scored", "shifted", "exped", "summed", "normed", "exT_ready", "pv_ready", "attn_ready"))
        woa_mm, woa_ready, up_mm, up_ready, ha_mm, mod_mm, th_ready, m_ready = map(
            sem, ("woa_mm", "woa_ready", "up_mm", "up_ready", "ha_mm", "mod_mm", "th_ready", "m_ready"))
        gate_mm, silu_ready, act_ready, down_mm, x1_ready = map(
            sem, ("gate_mm", "silu_ready", "act_ready", "down_mm", "x1_ready"))
        x1T_mm, x1T_act, x1T_dve, xa_mm, xam_ready, h1_mm, h1_ready = map(
            sem, ("x1T_mm", "x1T_act", "x1T_dve", "xa_mm", "xam_ready", "h1_mm", "h1_ready"))
        h1T_mm, h1T_act, h1T_dve, lg_mm, lg_ready = map(sem, ("h1T_mm", "h1T_act", "h1T_dve", "lg_mm", "lg_ready"))
        lgx_ready, lge_ready, sg_ready, member_ready, rank_mm, slot_ready, who_ready, scattered = map(
            sem, ("lgx_ready", "lge_ready", "sg_ready", "member_ready", "rank_mm", "slot_ready", "who_ready", "scattered"))
        sgu_mm, s_sil_ready, s_act_ready, sdn_mm, shared_added = map(
            sem, ("sgu_mm", "s_sil_ready", "s_act_ready", "sdn_mm", "shared_added"))
        r_loaded = [sem(f"r_loaded{i}") for i in range(RING)]
        r_sent = [sem(f"r_sent{i}") for i in range(RING)]
        r_in, r_hT, r_gu, r_sil, r_act, r_ta, r_actT, r_dn, r_wd, r_y, r_pick = map(
            sem, ("r_in", "r_hT", "r_gu", "r_sil", "r_act", "r_ta", "r_actT", "r_dn", "r_wd", "r_y", "r_pick"))
        yk_loaded = [sem(f"yk_loaded{i}") for i in range(TILES)]
        out_ready, stored = sem("out_ready"), sem("stored")

        def ring_count(s, r):
            return 4 * (s - r) + 16

        def spread_v(copy, h, b4s, done):
            for b4 in b4s:
                for h4 in range(4):
                    src = v_sb[32 * b4:32 * b4 + 32, 4 * h:4 * h + 4, :].rearrange(
                        "p t (a c) -> p t a c", a=4)[:, :, :, HD * h4:HD * h4 + HD]
                    dst = vbd[32 * h4:32 * h4 + 32, 16 * h:16 * h + 16].rearrange(
                        "p (t b) a c -> p t b a c", t=4)[:, :, b4, :, HD * h4:HD * h4 + HD]
                    ins = copy(dst, src)
            ins.then_inc(done, 1)

        block = ctx.enter_context(nc.Block())

        @block.sync
        def _(sp):
            sp.dma_start(cond_b[:, :], t["cond_b"]).then_inc(ld_cond, 16)
            sp.dma_start(consts[:, :], t["consts"]).then_inc(ld_const, 16)
            xt = t["x"].rearrange("(t p) d -> p t d", p=P)
            for h in range(2):
                sp.dma_start(res[:, 4 * h:4 * h + 4, :], xt[:, 4 * h:4 * h + 4, :]).then_inc(ld_x[h], 16)
            sp.dma_start(norm_w[:].rearrange("p i k -> p (i k)"), t["norms"]).then_inc(ld_norm, 16)
            for i, n in enumerate(("WqT", "WkT", "WvT")):
                sp.dma_start(wqkv[:, i], t[n].rearrange("(k p) n -> p k n", p=P)).then_inc(ld_wqkv, 16)
            sp.dma_start(wo[:], t["Wo"].rearrange("(k p) n -> p k n", p=P)).then_inc(ld_small, 16)
            sp.dma_start(a_sb[:], t["A"].rearrange("(k p) n -> p k n", p=P)).then_inc(ld_small, 16)
            sp.dma_start(b_sb[:], t["B"]).then_inc(ld_small, 16)
            sp.dma_start(w_gu[:, 1], t["WupT"].rearrange("(k p) n -> p k n", p=P)).then_inc(ld_up, 16)
            sp.dma_start(w_gu[:, 0], t["WinT"].rearrange("(k p) n -> p k n", p=P)).then_inc(ld_gate, 16)
            sp.dma_start(w_dn[:], t["WdT"].rearrange("(k p) n -> p k n", p=P)).then_inc(ld_down, 16)
            sp.dma_start(adapter_b[:], t["adapter_b"]).then_inc(ld_adapt, 16)
            sp.dma_start(scale_p[:], t["scale_p"]).then_inc(ld_adapt, 16)
            sp.wait_ge(fill_set, 2)
            for s in range(SLOT_TILES):
                sp.dma_start(slots_d[s * P:(s + 1) * P, :], fill[:]).then_inc(filled, 16)
            sp.wait_ge(pv_ready, 4)
            sp.dma_start(aT[:], t["AT"].rearrange("(k p) n -> p k n", p=P)).then_inc(ld_l1, 16)
            sp.dma_start(w1[:], t["W1T"].rearrange("(k p) n -> p k n", p=P)).then_inc(ld_l1, 16)
            sp.dma_start(bm[:], t["BmT"]).then_inc(ld_l1, 16)
            sp.dma_start(rw[:], t["router"].rearrange("(k p) n -> p k n", p=P)).then_inc(ld_l1, 16)
            sp.dma_start(s_gu[:], t["s_gu"].rearrange("(k p) n -> p k n", p=P)).then_inc(ld_shared, 16)
            for f, (a, n) in enumerate(SHC):
                sp.dma_start(s_dn[0:n, f], t["s_dn"][a:a + n, :]).then_inc(ld_shared, 16)
            for e in range(EXP):
                sp.dma_start(e_gu[:, e], t["e_gu"][e].rearrange("(k p) n -> p k n", p=P)).then_inc(ld_exp, 16)
                sp.dma_start(e_dn[:, e], t["e_dn"][e].rearrange("(k p) n -> p k n", p=IH)).then_inc(ld_exp, 16)

            def load(s, r, first_round):
                if not first_round:
                    sp.wait_ge(r_in, s - 3)
                    sp.wait_ge(r_wd, s - 3)
                sp.dma_start(slot_rows[:, r, :], slots_d[bass.ds(s * P, P), :]).then_inc(r_loaded[r], 16)

            sp.wait_ge(scattered, 16 * TILES * TOPK)
            head = 4 + (SLOT_TILES - 4) % RING
            for s in range(head):
                load(s, s % RING, s < RING)
            with sp.Fori(head, SLOT_TILES - RING + 1, RING) as i:
                for j in range(RING):
                    load(i + j, (head + j) % RING, False)
            for r in range(RING):
                sp.wait_ge(r_sent[r], 16 * len(range(r, SLOT_TILES, RING)))
            ykt = yk_d.rearrange("(t p k) d -> t p (k d)", p=P, k=TOPK)
            for i in range(TILES):
                sp.dma_start(yk[:, i], ykt[i]).then_inc(yk_loaded[i], 16)
            ot = t["out"].rearrange("(t p) d -> t p d", p=P)
            for i in range(TILES):
                sp.wait_ge(out_ready, i + 1)
                sp.dma_start(ot[i], res[:, i]).then_inc(stored, 16)
            sp.wait_ge(stored, 16 * TILES)

        @block.gpsimd
        def _(pool):
            nc.gpsimd.memset(fill[:, 0:D + EXP], 0.0).then_inc(fill_set, 1)
            nc.gpsimd.memset(fill[:, D + EXP:ROW], NOWHERE).then_inc(fill_set, 1)
            pool.wait_ge(cond_ready, 1)
            wrows = t["cond_w"].rearrange("s c d -> (s c) d")
            for i in range(TILES):
                pool.indirect_dma_start(wgath[:, i, :], None, wrows,
                                        bass.IndirectOffsetOnAxis(cond_rows[:, i:i + 1], 0),
                                        bounds_check=COND * SEQ - 1).then_inc(gathered, 16)
            nc.gpsimd.memset(vbd[:], 0.0).then_inc(vbd_zero, 1)
            def norm(u):
                pool.wait_ge(summed, u + 1)
                e3 = ex[:, u % 4, :].rearrange("p (a k) -> p a k", k=SEQ)
                nc.gpsimd.tensor_tensor(e3, e3, spread(rtotal[:, u, :], 2, SEQ), ALU.mult).then_inc(normed, 1)

            for u in range(8):
                norm(u)

            pool.wait_ge(filled, 16 * SLOT_TILES)
            pool.wait_ge(slot_ready, 1)
            pool.wait_ge(h1_ready, 4)
            for i in range(TILES):
                for k in range(TOPK):
                    pool.indirect_dma_start(slots_d, bass.IndirectOffsetOnAxis(slot[:, i * TOPK + k:i * TOPK + k + 1], 0),
                                            rows[:, i, :], None, bounds_check=SLOTS - 1).then_inc(scattered, 16)

            within = pool.to_reg(TOK * TOPK - 1)

            def send(s, r):
                pool.wait_ge(r_y, s + 1)
                pool.indirect_dma_start(yk_d, bass.IndirectOffsetOnAxis(dest[:, r:r + 1], 0), y[:, r, :], None,
                                        bounds_check=within, oob_is_err=False).then_inc(r_sent[r], 16)

            for s in range(SLOT_TILES):
                send(s, s % RING)

        @block.scalar
        def _(act_e):
            A = nc.scalar.activation
            for h in range(2):
                for g in range(2 * h, 2 * h + 2):
                    act_e.wait_ge(hid_ready, 2 * g + 2)
                    A(hn[:, 2 * g:2 * g + 2].rearrange("p t d -> p (t d)"), bank[g][:, :], ACT.Copy).then_inc(hid_kept, 1)
                for i in range(4 * h, 4 * h + 4):
                    act_e.wait_ge(hid_kept, i // 2 + 1)
                    A(square[:, i], hn[:, i], ACT.Square, accum_out=ssq[:, i:i + 1]).then_inc(ssq_ready, 1)
            for h in range(2):
                act_e.wait_ge(msq_ready, h + 1)
                A(rms[:, 4 * h:4 * h + 4], msq[:, 4 * h:4 * h + 4], ACT.Sqrt).then_inc(rms_ready, 1)
            act_e.wait_ge(ld_norm, 16)
            for h in range(2):
                act_e.wait_ge(hnT_ready, 4 * h + 4)
                for n, xn in enumerate((xn1, xn2)):
                    A(xn[:, 0, HALF * h:HALF * h + HALF], bank[4 + 2 * h][:, :], ACT.Copy,
                      scale=norm_w[:, n, 0:1]).then_inc(xn_act, 1)

            def keep_kv(h):
                for c in range(KC):
                    act_e.wait_ge(qk_ready, 4 * h + 3 + c)
                    A(kT[:, c, HALF * h:HALF * h + HALF], bank[2 + c][:, :], ACT.Copy).then_inc(k_ready, 1)
                for g in range(2 * h, 2 * h + 2):
                    act_e.wait_ge(v_ready, g + 1)
                    A(v_sb[:, 2 * g:2 * g + 2].rearrange("p t d -> p (t d)"), bank[4 + g % 2][:, :],
                      ACT.Copy).then_inc(v_kept, 1)

            def keep_up(i):
                act_e.wait_ge(up_mm, i + 1)
                A(up[:, i // 2, HALF * (i % 2):HALF * (i % 2) + HALF], bank[6 + i % 2][:, :],
                  ACT.Copy).then_inc(up_ready, 1)

            def exp(u):
                act_e.wait_ge(shifted, u + 1)
                A(ex[:, u % 4, :], ex[:, u % 4, :], ACT.Exp).then_inc(exped, 1)

            def keep_attn(g):
                act_e.wait_ge(pv_ready, g + 1)
                A(attnT[:, :, 256 * g:256 * g + 256], bank[4 + g % 2][:, :].rearrange("p (c n) -> p c n", c=2),
                  ACT.Copy).then_inc(attn_ready, 1)

            def copy(dst, src):
                return A(dst, src, ACT.Copy)

            act_e.wait_ge(vbd_zero, 1)
            for h in range(2):
                keep_kv(h)
                act_e.wait_ge(v_kept, 2 * h + 2)
                spread_v(copy, h, (2, 3), vbd_act)
            act_e.wait_ge(woa_mm, 1)
            A(woa[:].rearrange("p k r -> p (k r)"), bank[6][:, 0:KC * RANK], ACT.Copy).then_inc(woa_ready, 1)
            for g in range(4):
                exp(2 * g), exp(2 * g + 1)
                for i in range(4 * g, 4 * g + 4):
                    keep_up(i)
                if g:
                    keep_attn(g - 1)
            keep_attn(3)
            for h in range(2):
                act_e.wait_ge(mod_mm, h + 1)
                A(thm[:, HALF * h:HALF * h + HALF], bank[4 + h][0:RANK, :], ACT.Tanh).then_inc(th_ready, 1)
            for i in range(2 * FC):
                act_e.wait_ge(gate_mm, i + 1)
                if i >= 2:
                    act_e.wait_ge(act_ready, i - 1)
                A(g_sb[:, i % 2, :], bank[6 + i % 2][:, :], ACT.Silu).then_inc(silu_ready, 1)
            for h in range(2):
                act_e.wait_ge(x1T_mm, 4 * h + 4)
                A(x1T[:, 0, HALF * h:HALF * h + HALF], bank[4 + 2 * h][:, :], ACT.Copy).then_inc(x1T_act, 1)
            for g in range(4):
                act_e.wait_ge(h1_mm, g + 1)
                A(rows[:, 2 * g:2 * g + 2, 0:D], bank[2 + g][:, :].rearrange("p (t d) -> p t d", t=2),
                  ACT.Copy).then_inc(h1_ready, 1)
            for h in range(2):
                act_e.wait_ge(h1T_mm, 4 * h + 4)
                A(h1T[:, 0, HALF * h:HALF * h + HALF], bank[(6, 0)[h]][:, :], ACT.Copy).then_inc(h1T_act, 1)
            act_e.wait_ge(lgx_ready, 1)
            A(lgx[:], lgx[:], ACT.Exp).then_inc(lge_ready, 1)
            act_e.wait_ge(lg_ready, 1)
            A(sgate[:], lg_sb[:, :, EXP], ACT.Sigmoid).then_inc(sg_ready, 1)
            for i in range(2 * len(SHC)):
                n = SHC[i % len(SHC)][1]
                act_e.wait_ge(sgu_mm, i + 1)
                if i >= 2:
                    act_e.wait_ge(s_act_ready, i - 1)
                A(s_sil[0:n, i % 2, :], bank[(6, 0)[i % 2]][0:n, :], ACT.Silu).then_inc(s_sil_ready, 1)

            def keep_hT(s, q):
                act_e.wait_ge(r_in, s + 1)
                A(hT[:, q], bank[2 + q][:, 0:D].rearrange("p (k n) -> p k n", k=KC), ACT.Copy).then_inc(r_hT, 1)

            def silu(s, q):
                act_e.wait_ge(r_gu, s + 1)
                A(sil[:, q], bank[q][:, 0:IM], ACT.Silu).then_inc(r_sil, 1)

            def weigh(s, q, r, again):
                act_e.wait_ge(r_dn, s + 1)
                act_e.wait_ge(r_wd, s + 1)
                if again:
                    act_e.wait_ge(r_sent[r], ring_count(s, r) - 16)
                A(y[:, r, :], bank[6 + q][:, 0:D], ACT.Copy, scale=wd[:, r, 0:1]).then_inc(r_y, 1)

            keep_hT(0, 0)
            for s in range(PIPE0):
                if s >= 2:
                    act_e.wait_ge(r_act, s - 1)
                silu(s, s % 2)
                keep_hT(s + 1, (s + 1) % 2)

            def step(s, j, again):
                q = (PIPE0 + j) % 2
                act_e.wait_ge(r_act, s - 1)
                silu(s, q)
                act_e.wait_ge(r_gu, s)
                keep_hT(s + 1, 1 - q)
                weigh(s - 2, q, (PIPE0 + j - 2) % RING, again)

            for j in range(RING):
                step(PIPE0 + j, j, False)
            with act_e.Fori(PIPE0 + RING, SLOT_TILES - RING, RING) as i:
                for j in range(RING):
                    step(i + j, j, True)
            s = SLOT_TILES - 1
            act_e.wait_ge(r_act, s - 1)
            silu(s, s % 2)
            for s in range(SLOT_TILES - 3, SLOT_TILES):
                weigh(s, s % 2, s % RING, True)

        @block.vector
        def _(dve):
            V = nc.vector
            steps = [0]

            def link(ins):
                steps[0] += 1
                ins.then_inc(dve_step, 1)
                dve.wait_ge(dve_step, steps[0])

            dve.wait_ge(ld_cond, 16)
            dve.wait_ge(ld_const, 16)
            V.tensor_scalar(cond_rows[:], cond_b[:], float(SEQ), K["pos_of"], ALU.mult, ALU.add).then_inc(cond_ready, 1)
            V.tensor_copy(ident_b[:], K["ident"]).then_inc(bf_ready, 1)
            V.tensor_copy(causal_b[:], K["causal"]).then_inc(bf_ready, 1)
            V.tensor_copy(before_b[:], K["before"]).then_inc(bf_ready, 1)
            V.memset(ones_b[:], 1.0).then_inc(bf_ready, 1)
            for i in range(TILES):
                if i == 0:
                    dve.wait_ge(gathered, 16 * TILES)
                V.tensor_tensor(wbd[:, i], spread(wgath[:, i], 1, 4), spread(K["batch_of"], 2, SEQ),
                                ALU.mult).then_inc(wbd_ready, 1)
            for h in range(2):
                dve.wait_ge(ld_x[h], 16)
                dve.wait_ge(ssq_ready, 4 * h + 4)
                V.tensor_scalar(msq[:, 4 * h:4 * h + 4], ssq[:, 4 * h:4 * h + 4], 1.0 / D, EPS, ALU.mult, ALU.add).then_inc(msq_ready, 1)
                dve.wait_ge(hid_ready, 4 * h + 4)
                V.tensor_tensor(res[:, 4 * h:4 * h + 4], hn[:, 4 * h:4 * h + 4], res[:, 4 * h:4 * h + 4], ALU.add).then_inc(res_ready, 1)
                dve.wait_ge(rms_ready, h + 1)
                link(V.reciprocal(rstd[:, 4 * h:4 * h + 4], rms[:, 4 * h:4 * h + 4]))
                for i in range(4 * h, 4 * h + 4):
                    V.tensor_scalar(hn[:, i], hn[:, i], rstd[:, i:i + 1], None, ALU.mult).then_inc(hn_ready, 1)
            dve.wait_ge(ld_norm, 16)
            for h in range(2):
                dve.wait_ge(hnT_ready, 4 * h + 4)
                for n, xn in enumerate((xn1, xn2)):
                    V.tensor_scalar(xn[:, 1, HALF * h:HALF * h + HALF], bank[5 + 2 * h][:, :],
                                    norm_w[:, n, 1:2], None, ALU.mult).then_inc(xn_dve, 1)

            def mask_q(h):
                for c in range(KC):
                    dve.wait_ge(qk_ready, 4 * h + 1 + c)
                    q3 = bank[c][:, :].rearrange("p (b q) -> p b q", q=SEQ)
                    V.tensor_tensor(qx[:, c, 16 * h:16 * h + 16], spread(q3, 2, 4),
                                    spread(spread(K["head_of"], 2, SEQ), 1, 16), ALU.mult).then_inc(qx_ready, 1)

            def shift(u):
                dve.wait_ge(scored, u + 1)
                s3 = bank[u % 4][:, :].rearrange("p (a k) -> p a k", k=SEQ)
                link(V.reduce_max(peak[:, u, :], s3, AX.X))
                if u >= 4:
                    dve.wait_ge(exT_ready, u - 3)
                V.tensor_tensor(ex[:, u % 4, :].rearrange("p (a k) -> p a k", k=SEQ), s3,
                                spread(peak[:, u, :], 2, SEQ), ALU.subtract).then_inc(shifted, 1)

            def sums(u):
                dve.wait_ge(exped, u + 1)
                link(V.reduce_sum(total[:, u, :], ex[:, u % 4, :].rearrange("p (a k) -> p a k", k=SEQ), AX.X))
                V.reciprocal(rtotal[:, u, :], total[:, u, :]).then_inc(summed, 1)

            def turn(u):
                dve.wait_ge(normed, u + 1)
                if u >= 2:
                    dve.wait_ge(pv_ready, (u - 2) // 2 + 1)
                V.transpose(exT[:, u % 2, :], ex[:, u % 4, :]).then_inc(exT_ready, 1)

            dve.wait_ge(vbd_zero, 1)
            for h in range(2):
                mask_q(h)
                dve.wait_ge(v_kept, 2 * h + 2)
                spread_v(V.tensor_copy, h, (0, 1), vbd_dve)
            for g in range(4):
                for u in (2 * g, 2 * g + 1):
                    shift(u)
                if g:
                    turn(2 * g - 2), turn(2 * g - 1)
                for u in (2 * g, 2 * g + 1):
                    sums(u)
            turn(6), turn(7)
            for h in range(2):
                dve.wait_ge(th_ready, h + 1)
                dve.wait_ge(ha_mm, h + 1)
                V.scalar_tensor_tensor(m_sb[:, HALF * h:HALF * h + HALF], thm[:, HALF * h:HALF * h + HALF], 0.1,
                                       bank[h][0:RANK, :], ALU.mult, ALU.mult).then_inc(m_ready, 1)
            for i in range(2 * FC):
                dve.wait_ge(silu_ready, i + 1)
                dve.wait_ge(up_ready, i + 1)
                u2 = up[:, i // 2, HALF * (i % 2):HALF * (i % 2) + HALF]
                V.tensor_tensor(u2, g_sb[:, i % 2, :], u2, ALU.mult).then_inc(act_ready, 1)
            for i in range(4):
                dve.wait_ge(down_mm, i + 1)
                r2 = res[:, 2 * i:2 * i + 2].rearrange("p t d -> p (t d)")
                V.tensor_tensor(r2, bank[i][:, :], r2, ALU.add).then_inc(x1_ready, 1)
            dve.wait_ge(ld_adapt, 32)
            link(V.tensor_scalar(adapter_sel[:], adapter_b[:], K["adapter_of"], scale_p[:, 0:1], ALU.is_equal, ALU.mult))
            for h in range(2):
                dve.wait_ge(x1T_mm, 4 * h + 4)
                V.tensor_copy(x1T[:, 1, HALF * h:HALF * h + HALF], bank[5 + 2 * h][:, :]).then_inc(x1T_dve, 1)
            for h in range(2):
                dve.wait_ge(xa_mm, h + 1)
                V.tensor_tensor(xam[:, HALF * h:HALF * h + HALF].rearrange("p (b s) -> p b s", s=SEQ),
                                bank[h][:, :].rearrange("p (b s) -> p b s", s=SEQ),
                                spread(adapter_sel[:, 16 * h:16 * h + 16], 2, SEQ), ALU.mult).then_inc(xam_ready, 1)
            for h in range(2):
                dve.wait_ge(h1T_mm, 4 * h + 4)
                V.tensor_copy(h1T[:, 1, HALF * h:HALF * h + HALF], bank[(7, 1)[h]][:, :]).then_inc(h1T_dve, 1)

            dve.wait_ge(lg_mm, 1)
            V.tensor_copy(lg_sb[:].rearrange("p t e -> p (t e)"), bank[2][:, 0:TILES * (EXP + 1)]).then_inc(lg_ready, 1)
            dve.wait_ge(lg_ready, 1)
            lg = lg_sb[:, :, 0:EXP]
            link(V.reduce_max(lgm[:, 0, :], lg, AX.X))
            V.tensor_tensor(lgx[:], lg, spread(lgm[:, 0, :], 2, EXP), ALU.subtract).then_inc(lgx_ready, 1)
            dve.wait_ge(lge_ready, 1)
            link(V.reduce_sum(lgm[:, 1, :], lgx[:], AX.X))
            link(V.reciprocal(lgm[:, 2, :], lgm[:, 1, :]))
            link(V.tensor_tensor(lgx[:], lgx[:], spread(lgm[:, 2, :], 2, EXP), ALU.mult))
            for i in range(TILES):
                ins = V.max(top_v[:, i], lgx[:, i])
            link(ins)
            for i in range(TILES):
                ins = V.max_index(top_i[:, i], top_v[:, i], lgx[:, i])
            link(ins)
            link(V.tensor_copy(top_f[:], top_i[:, :, 0:TOPK]))
            link(V.tensor_tensor(hot[:], spread(top_f[:], 3, EXP),
                                 spread(spread(K["iota_e"], 1, TOPK), 1, TILES), ALU.is_equal))
            with nc.allow_low_precision(reason="zeros and ones"):
                V.tensor_reduce(member[:], hot[:].rearrange("p t k e -> p t e k"), AX.X, ALU.add).then_inc(member_ready, 1)
            link(V.reduce_sum(lgm[:, 0, :], top_v[:, :, 0:TOPK], AX.X))
            link(V.tensor_scalar(lgm[:, 1, :], lgm[:, 0, :], 1e-9, None, ALU.max))
            link(V.reciprocal(lgm[:, 2, :], lgm[:, 1, :]))
            link(V.tensor_tensor(wts[:], top_v[:, :, 0:TOPK], spread(lgm[:, 2, :], 2, TOPK), ALU.mult))
            def find_slots():
                dve.wait_ge(rank_mm, 1)
                rank = bank[3][:, 0:P].rearrange("p (t e) -> p t e", e=EXP)
                count = bank[3][:, P:P + EXP]
                link(V.tensor_tensor(over[:], spread(count, 2, TILES), spread(K["tile_edge"], 1, EXP), ALU.is_gt))
                link(V.reduce_sum(ntile[:], over[:], AX.X))
                link(V.tensor_tensor(pairs[:], spread(ntile[:], 1, EXP), K["lower_e"].rearrange("p (a b) -> p a b", a=EXP), ALU.mult))
                link(V.reduce_sum(first[:], pairs[:], AX.X))
                link(V.scalar_tensor_tensor(where[:], spread(first[:], 1, TILES), float(P), rank, ALU.mult, ALU.add))
                link(V.tensor_tensor(prod[:], hot[:], spread(where[:], 2, TOPK), ALU.mult))
                link(V.reduce_sum(slot_f[:], prod[:].rearrange("p t k e -> p (t k) e"), AX.X))
                link(V.tensor_copy(slot[:], slot_f[:]))
                dve.wait_ge(h1_ready, 4)
                link(V.tensor_tensor(prod[:], hot[:], spread(wts[:], 3, EXP), ALU.mult))
                link(V.tensor_reduce(rows[:, :, D:D + EXP], prod[:].rearrange("p t k e -> p t e k"), AX.X, ALU.add))
                link(V.tensor_tensor(prod[:], hot[:], spread(K["dest"].rearrange("p (t k) -> p t k", k=TOPK), 3, EXP), ALU.mult))
                V.tensor_reduce(rows[:, :, D + EXP:ROW], prod[:].rearrange("p t k e -> p t e k"), AX.X, ALU.add).then_inc(slot_ready, 1)

            def find_experts():
                link(V.tensor_tensor(last[:], first[:], ntile[:], ALU.add))
                link(V.memset(last[:, EXP - 1:EXP], float(SLOT_TILES)))
                link(V.tensor_tensor(hot_s[:], spread(K["iota_s"], 2, EXP), spread(first[:], 1, SLOT_TILES), ALU.is_ge))
                link(V.tensor_tensor(hot_t[:], spread(K["iota_s"], 2, EXP), spread(last[:], 1, SLOT_TILES), ALU.is_lt))
                link(V.tensor_tensor(hot_s[:], hot_s[:], hot_t[:], ALU.mult))
                link(V.tensor_tensor(hot_t[:], hot_s[:], spread(K["iota_e"], 1, SLOT_TILES), ALU.mult))
                link(V.reduce_sum(who_f[:], hot_t[:], AX.X))
                V.tensor_copy(who[:], who_f[:]).then_inc(who_ready, 1)

            for h in range(2):
                for f, (a, n) in enumerate(SHC):
                    i = h * len(SHC) + f
                    dve.wait_ge(s_sil_ready, i + 1)
                    if h:
                        dve.wait_ge(sdn_mm, 2)
                    V.tensor_tensor(s_act[0:n, f, :], s_sil[0:n, i % 2, :], bank[(7, 1)[i % 2]][0:n, :],
                                    ALU.mult).then_inc(s_act_ready, 1)
                    if i == 1:
                        find_slots()
                    if i == 3:
                        find_experts()
                dve.wait_ge(sg_ready, 1)
                for j in range(2):
                    dve.wait_ge(sdn_mm, 2 * h + j + 1)
                    for tt in range(2):
                        i = 4 * h + 2 * j + tt
                        V.scalar_tensor_tensor(res[:, i], bank[4 + j][:, D * tt:D * tt + D], sgate[:, i:i + 1],
                                               res[:, i], ALU.mult, ALU.add).then_inc(shared_added, 1)

            def mul(s, q):
                dve.wait_ge(r_sil, s + 1)
                V.tensor_tensor(act[:, q], sil[:, q], bank[q][:, IM:2 * IM], ALU.mult).then_inc(r_act, 1)

            def keep_actT(s, q):
                dve.wait_ge(r_ta, s + 1)
                V.tensor_copy(actT[:, q], bank[4 + q][0:IH, 0:2 * P].rearrange("p (k n) -> p k n", k=2)).then_inc(r_actT, 1)

            def pick_row(s, r, again):
                dve.wait_ge(r_loaded[r], ring_count(s, r))
                V.tensor_tensor(pick[:, r], slot_rows[:, r, D:ROW].rearrange("p (a e) -> p a e", a=2),
                                spread(hot_s[:, bass.ds(s, 1), :].rearrange("p s e -> p (s e)"), 1, 2), ALU.mult).then_inc(r_pick, 1)
                if again:
                    dve.wait_ge(r_sent[r], ring_count(s, r) - 16)
                dve.wait_ge(r_pick, 2 * s + 1)
                V.reduce_sum(wd[:, r, :], pick[:, r], AX.X).then_inc(r_pick, 1)
                dve.wait_ge(r_pick, 2 * s + 2)
                V.tensor_copy(dest[:, r:r + 1], wd[:, r, 1:2]).then_inc(r_wd, 1)

            for s in range(PIPE0):
                mul(s, s % 2)
                if s:
                    keep_actT(s - 1, (s - 1) % 2)
                pick_row(s, s % RING, False)

            def vstep(s, j, again):
                q = (PIPE0 + j) % 2
                dve.wait_ge(r_ta, s - 1)
                mul(s, q)
                if again:
                    dve.wait_ge(r_dn, s - 2)
                keep_actT(s - 1, 1 - q)
                pick_row(s, (PIPE0 + j) % RING, again)

            for j in range(RING):
                vstep(PIPE0 + j, j, j >= 2)
            with dve.Fori(PIPE0 + RING, SLOT_TILES - RING, RING) as i:
                for j in range(RING):
                    vstep(i + j, j, True)
            s = SLOT_TILES - 1
            vstep(s, s - PIPE0, True)
            dve.wait_ge(r_dn, s - 1)
            keep_actT(s, s % 2)

            for i in range(TILES):
                dve.wait_ge(yk_loaded[i], 16)
                link(V.tensor_tensor(ysum[:, i], yk[:, i, 0:2 * D], yk[:, i, 2 * D:4 * D], ALU.add))
                link(V.tensor_tensor(ysum[:, i, 0:D], ysum[:, i, 0:D], ysum[:, i, D:2 * D], ALU.add))
                V.tensor_tensor(res[:, i], ysum[:, i, 0:D], res[:, i], ALU.add).then_inc(out_ready, 1)

        @block.tensor
        def _(pe):
            MM = nc.tensor.matmul
            TR = nc.tensor.transpose
            I = K["ident"]
            pe.wait_ge(ld_const, 16)
            for i in range(TILES):
                pe.wait_ge(wbd_ready, i + 1)
                pe.wait_ge(ld_x[i // 4], 16)
                MM(bank[i // 2][:, D * (i % 2):D * (i % 2) + D], wbd[:, i].rearrange("p b d -> p (b d)"), res[:, i],
                   start=True, stop=True).then_inc(hid_ready, 1)
            for i in range(TILES):
                pe.wait_ge(hn_ready, i + 1)
                for k in range(KC):
                    ins = TR(bank[4 + 2 * (i // 4) + k][:, P * (i % 4):P * (i % 4) + P], hn[:, i, P * k:P * k + P], I)
                ins.then_inc(hnT_ready, 1)

            def qkv(h):
                pe.wait_ge(xn_act, 2 * h + 2)
                pe.wait_ge(xn_dve, 2 * h + 2)
                for m in range(2):
                    for c in range(KC):
                        if h:
                            pe.wait_ge((qx_ready, k_ready)[m], c + 1)
                        for k in range(KC):
                            ins = MM(bank[2 * m + c][:, :], wqkv[:, m, k, P * c:P * c + P],
                                     xn1[:, k, HALF * h:HALF * h + HALF], start=(k == 0), stop=(k == KC - 1))
                        ins.then_inc(qk_ready, 1)
                for g in range(2 * h, 2 * h + 2):
                    if g >= 2:
                        pe.wait_ge(v_kept, g - 1)
                    for tt in range(2):
                        i = 2 * g + tt
                        for k in range(KC):
                            ins = MM(bank[4 + g % 2][:, D * tt:D * tt + D], xn1[:, k, P * i:P * i + P], wqkv[:, 2, k, :],
                                     start=(k == 0), stop=(k == KC - 1))
                    ins.then_inc(v_ready, 1)

            pe.wait_ge(ld_wqkv, 48)
            qkv(0)
            qkv(1)
            pe.wait_ge(ld_small, 48)
            for c in range(KC):
                for k in range(KC):
                    ins = MM(bank[6][:, RANK * c:RANK * c + RANK], wo[:, k, P * c:P * c + P], a_sb[:, k, :],
                             start=(k == 0), stop=(k == KC - 1))
            ins.then_inc(woa_mm, 1)

            def up_unit(i):
                if i == 0:
                    pe.wait_ge(ld_up, 16)
                    pe.wait_ge(woa_ready, 1)
                if i >= 2:
                    pe.wait_ge(up_ready, i - 1)
                f, h = i // 2, i % 2
                for k in range(KC):
                    ins = MM(bank[6 + i % 2][:, :], w_gu[:, 1, k, P * f:P * f + P], xn2[:, k, HALF * h:HALF * h + HALF],
                             start=(k == 0), stop=(k == KC - 1))
                ins.then_inc(up_mm, 1)

            def scores(g):
                if g == 0:
                    pe.wait_ge(bf_ready, 4)
                    pe.wait_ge(qx_ready, 4)
                    pe.wait_ge(k_ready, 4)
                for zz in range(2):
                    u = 2 * g + zz
                    if u >= 4:
                        pe.wait_ge(shifted, u - 3)
                    b_ = bank[u % 4]
                    MM(b_[:, :], ident_b[:], spread(causal_b[:], 1, 16), start=True, stop=False, skip_group_check=True)
                    for b in range(8):
                        for c in range(KC):
                            bb = 8 * g + b
                            at = SEQ * (2 * b + c)
                            ins = MM(b_[:, at:at + SEQ], qx[64 * zz:64 * zz + 64, c, bb].rearrange("p h q -> p (h q)"),
                                     kT[64 * zz:64 * zz + 64, c, SEQ * bb:SEQ * bb + SEQ], start=False,
                                     stop=True, skip_group_check=True)
                    ins.then_inc(scored, 1)

            def pv(g):
                pe.wait_ge(vbd_act, g // 2 + 1)
                pe.wait_ge(vbd_dve, g // 2 + 1)
                if g >= 2:
                    pe.wait_ge(attn_ready, g - 1)
                else:
                    pe.wait_ge(v_kept, g + 3)
                for zz in range(2):
                    u = 2 * g + zz
                    pe.wait_ge(exT_ready, u + 1)
                    for b in range(8):
                        for c in range(KC):
                            at = SEQ * (2 * b + c)
                            ins = MM(bank[4 + g % 2][64 * zz:64 * zz + 64, 256 * c + SEQ * b:256 * c + SEQ * b + SEQ],
                                     vbd[:, 8 * g + b, 2 * c + zz, :], exT[:, u % 2, at:at + SEQ], start=True, stop=True)
                ins.then_inc(pv_ready, 1)

            for g in range(4):
                scores(g)
                for i in range(4 * g, 4 * g + 4):
                    up_unit(i)
                if g:
                    pv(g - 1)
            pe.wait_ge(shifted, 8)
            for h in range(2):
                for k in range(KC):
                    ins = MM(bank[h][0:RANK, :], a_sb[:, k, :], xn2[:, k, HALF * h:HALF * h + HALF],
                             start=(k == 0), stop=(k == KC - 1))
                ins.then_inc(ha_mm, 1)
            pv(3)
            pe.wait_ge(attn_ready, 4)
            for h in range(2):
                for k in range(KC):
                    ins = MM(bank[4 + h][0:RANK, :], woa[:, k, :], attnT[:, k, HALF * h:HALF * h + HALF],
                             start=(k == 0), stop=(k == KC - 1))
                ins.then_inc(mod_mm, 1)

            def gate_unit(i):
                if i == 0:
                    pe.wait_ge(ld_gate, 16)
                pe.wait_ge(up_ready, 2 * FC) if i < 2 else pe.wait_ge(silu_ready, i - 1)
                f, h = i // 2, i % 2
                for k in range(KC):
                    MM(bank[6 + i % 2][:, :], w_gu[:, 0, k, P * f:P * f + P], xn2[:, k, HALF * h:HALF * h + HALF],
                       start=(k == 0), stop=False)
                pe.wait_ge(m_ready, h + 1) if i < 2 else None
                MM(bank[6 + i % 2][:, :], b_sb[:, P * f:P * f + P], m_sb[:, HALF * h:HALF * h + HALF],
                   start=False, stop=True).then_inc(gate_mm, 1)

            def down(f):
                if f == 0:
                    pe.wait_ge(ld_down, 16)
                pe.wait_ge(act_ready, 2 * f + 2)
                for i in range(TILES):
                    ins = MM(bank[i // 2][:, D * (i % 2):D * (i % 2) + D], up[:, f, P * i:P * i + P], w_dn[:, f, :],
                             start=(f == 0 and i % 2 == 0), stop=(f == FC - 1), skip_group_check=True)
                    if f == FC - 1 and i % 2:
                        ins.then_inc(down_mm, 1)

            gate_unit(0), gate_unit(1)
            for f in range(FC):
                if f + 1 < FC:
                    gate_unit(2 * f + 2), gate_unit(2 * f + 3)
                down(f)

            for i in range(TILES):
                pe.wait_ge(x1_ready, i // 2 + 1)
                if i == 0:
                    pe.wait_ge(th_ready, 2)
                if i == 4:
                    pe.wait_ge(silu_ready, 2 * FC)
                for k in range(KC):
                    ins = TR(bank[4 + 2 * (i // 4) + k][:, P * (i % 4):P * (i % 4) + P], res[:, i, P * k:P * k + P], I)
                ins.then_inc(x1T_mm, 1)
            pe.wait_ge(ld_l1, 64)
            pe.wait_ge(x1T_act, 2)
            pe.wait_ge(x1T_dve, 2)
            for h in range(2):
                for k in range(KC):
                    ins = MM(bank[h][:, :], aT[:, k, :], x1T[:, k, HALF * h:HALF * h + HALF],
                             start=(k == 0), stop=(k == KC - 1))
                ins.then_inc(xa_mm, 1)
            for g in range(4):
                pe.wait_ge(xam_ready, g // 2 + 1)
                for tt in range(2):
                    i = 2 * g + tt
                    o = bank[2 + g][:, D * tt:D * tt + D]
                    for k in range(KC):
                        MM(o, x1T[:, k, P * i:P * i + P], w1[:, k, :], start=(k == 0), stop=False)
                    ins = MM(o, xam[:, P * i:P * i + P], bm[:, :], start=False, stop=True)
                ins.then_inc(h1_mm, 1)
            for i in range(TILES):
                pe.wait_ge(h1_ready, i // 2 + 1)
                for k in range(KC):
                    b_ = bank[((6, 7), (0, 1))[i // 4][k]]
                    ins = TR(b_[:, P * (i % 4):P * (i % 4) + P], rows[:, i, P * k:P * k + P], I)
                ins.then_inc(h1T_mm, 1)
            for i in range(TILES):
                if i % 4 == 0:
                    pe.wait_ge(h1T_act, i // 4 + 1)
                    pe.wait_ge(h1T_dve, i // 4 + 1)
                for k in range(KC):
                    ins = MM(bank[2][:, 17 * i:17 * i + 17], h1T[:, k, P * i:P * i + P], rw[:, k, :],
                             start=(k == 0), stop=(k == KC - 1))
            ins.then_inc(lg_mm, 1)

            def ranks():
                pe.wait_ge(member_ready, 1)
                mb = member[:].rearrange("p t e -> p (t e)")
                MM(bank[3][:, 0:P], before_b[:], mb, start=True, stop=False, skip_group_check=True)
                for d in range(1, TILES):
                    MM(bank[3][:, EXP * d:P], ones_b[:], mb[:, 0:P - EXP * d], start=False, stop=False,
                       skip_group_check=True)
                for i in range(TILES):
                    ins = MM(bank[3][:, P:P + EXP], ones_b[:], mb[:, EXP * i:EXP * i + EXP], start=False,
                             stop=(i == TILES - 1), skip_group_check=True)
                ins.then_inc(rank_mm, 1)

            pe.wait_ge(ld_shared, 16 * (1 + len(SHC)))
            for h in range(2):
                for f, (a, n) in enumerate(SHC):
                    i = h * len(SHC) + f
                    if i >= 2:
                        pe.wait_ge(s_act_ready, i - 1)
                    for m in range(2):
                        for k in range(KC):
                            ins = MM(bank[((6, 7), (0, 1))[i % 2][m]][0:n, :], s_gu[:, k, SH * m + a:SH * m + a + n],
                                     h1T[:, k, HALF * h:HALF * h + HALF], start=(k == 0), stop=(k == KC - 1))
                    ins.then_inc(sgu_mm, 1)
                    if i == 1:
                        ranks()
                pe.wait_ge(s_act_ready, (h + 1) * len(SHC))
                if h:
                    pe.wait_ge(shared_added, 4)
                for j in range(2):
                    for tt in range(2):
                        i = 2 * j + tt
                        for f, (a, n) in enumerate(SHC):
                            ins = MM(bank[4 + j][:, D * tt:D * tt + D], s_act[0:n, f, P * i:P * i + P], s_dn[0:n, f, :],
                                     start=(f == 0), stop=(f == len(SHC) - 1))
                    ins.then_inc(sdn_mm, 1)

            def turn_in(s, q, r, again):
                pe.wait_ge(r_loaded[r], ring_count(s, r))
                if again:
                    pe.wait_ge(r_hT, s - 1)
                for k in range(KC):
                    ins = TR(bank[2 + q][:, P * k:P * k + P], slot_rows[:, r, P * k:P * k + P], I)
                ins.then_inc(r_in, 1)

            def expert_of(s):
                return pe.value_load(who[0:1, bass.ds(s, 1)], min_val=0, max_val=EXP - 1)

            def gate_up(s, q, again):
                e = expert_of(s)
                pe.wait_ge(r_hT, s + 1)
                if again:
                    pe.wait_ge(r_act, s - 1)
                w = e_gu[:].rearrange("p e k n -> p (e k) n")
                for k in range(KC):
                    ins = MM(bank[q][:, 0:2 * IM], hT[:, q, k, :],
                             w[:, bass.ds(e * KC + k, 1), :].rearrange("p a n -> p (a n)"),
                             start=(k == 0), stop=(k == KC - 1))
                ins.then_inc(r_gu, 1)

            def turn_act(s, q, again):
                pe.wait_ge(r_act, s + 1)
                if again:
                    pe.wait_ge(r_actT, s - 1)
                for k in range(2):
                    ins = TR(bank[4 + q][0:IH, P * k:P * k + P], act[:, q, IH * k:IH * k + IH], I)
                ins.then_inc(r_ta, 1)

            def down_e(s, q, again):
                e = expert_of(s)
                pe.wait_ge(r_actT, s + 1)
                if again:
                    pe.wait_ge(r_y, s - 1)
                w = e_dn[:].rearrange("p e k n -> p (e k) n")
                for k in range(2):
                    ins = MM(bank[6 + q][:, 0:D], actT[:, q, k, :],
                             w[:, bass.ds(e * 2 + k, 1), :].rearrange("p a n -> p (a n)"),
                             start=(k == 0), stop=(k == 1))
                ins.then_inc(r_dn, 1)

            pe.wait_ge(who_ready, 1)
            pe.wait_ge(ld_exp, 32 * EXP)
            turn_in(0, 0, 0, False)
            gate_up(0, 0, False)
            turn_in(1, 1, 1, False)
            gate_up(1, 1, False)
            pe.wait_ge(shared_added, 8)
            turn_act(0, 0, False)
            turn_in(2, 0, 2, True)

            def pstep(s, j, again):
                q = (PIPE0 + j) % 2
                gate_up(s, q, True)
                turn_act(s - 1, 1 - q, again)
                turn_in(s + 1, 1 - q, (PIPE0 + j + 1) % RING, True)
                down_e(s - 2, q, again)

            for j in range(RING):
                pstep(PIPE0 + j, j, j >= 2)
            with pe.Fori(PIPE0 + RING, SLOT_TILES - RING, RING) as i:
                for j in range(RING):
                    pstep(i + j, j, True)
            s = SLOT_TILES - 1
            gate_up(s, s % 2, True)
            turn_act(s - 1, (s - 1) % 2, True)
            down_e(s - 2, s % 2, True)
            turn_act(s, s % 2, True)
            down_e(s - 1, (s - 1) % 2, True)
            down_e(s, s % 2, True)


def kernel(**inputs):
    import numpy as _np
    import concourse.bacc as _bacc
    from concourse import mybir as _mybir
    from concourse.bass_utils import run_bass_kernel_spmd as _run

    a = {k: _np.asarray(v) for k, v in inputs.items()}
    flip = lambda w: _np.ascontiguousarray(w.T)
    arrays = {
        "x": a["x"].reshape(TOK, D), "cond": flip(a["itok_B_1_198"].reshape(TILES, 4)), "adapter": a["itok_B_0_6"],
        "cond_w": a["L0_cond_weights"], 
        "norms": flip(_np.concatenate([a["L0_ffn_ln1_w"], a["L0_ffn_ln2_w"]]).reshape(2 * KC, P)),
        "WqT": flip(a["L0_ffn_Wq"]), "WkT": flip(a["L0_ffn_Wk"]), "WvT": flip(a["L0_ffn_Wv"]),
        "Wo": a["L0_ffn_Wo"], "A": a["L0_ffn_A"], "B": a["L0_ffn_B"],
        "WinT": flip(a["L0_ffn_W_in_base"]), "WupT": flip(a["L0_ffn_W_up_base"]), "WdT": flip(a["L0_ffn_W_down"]),
        "W1T": flip(a["L1_cond_W"]), "AT": flip(a["L1_cond_A"].reshape(P, D)),
        "BmT": _np.ascontiguousarray(a["L1_cond_Bm"].transpose(0, 2, 1)).reshape(P, D),
        "scale": a["L1_cond_scalings"],
        "router": _np.concatenate([flip(a["L1_ffn_router_w"]), a["L1_ffn_sh_gate_w"]], axis=1),
        "e_gu": _np.concatenate([a["L1_ffn_w_gate"], a["L1_ffn_w_up"]], axis=2), "e_dn": a["L1_ffn_w_down"],
        "s_gu": _np.concatenate([a["L1_ffn_sh_gate"], a["L1_ffn_sh_up"]], axis=1), "s_dn": a["L1_ffn_sh_down"],
        "consts": constants(),
    }
    arrays = {f"in_{k}": _np.ascontiguousarray(v) for k, v in arrays.items()}
    nc = _bacc.Bacc("TRN2", target_bir_lowering=False, num_devices=1)
    t = {k[3:]: nc.dram_tensor(k, v.shape, _mybir.dt.from_np(v.dtype), kind="ExternalInput").ap()
         for k, v in arrays.items()}
    t["out"] = nc.dram_tensor("out", (TOK, D), F32, kind="ExternalOutput").ap()
    t["cond_b"] = bass.AP(t["cond"].tensor, 0, [[TILES, 4], [0, SEQ], [1, TILES]])
    t["adapter_b"] = bass.AP(t["adapter"].tensor, 0, [[0, P], [1, BATCH]])
    t["scale_p"] = bass.AP(t["scale"].tensor, 0, [[1, ADAPT], [0, RANK], [1, 1]])
    program(nc, t)
    r = _run(nc, [arrays], core_ids=[0])
    return r.results[0]["out"].reshape(BATCH, SEQ, D)
```

```python
from contextlib import ExitStack

import numpy as np

import concourse.bass as bass
from concourse import mybir

F32 = mybir.dt.float32
F32R = mybir.dt.float32r
BF16 = mybir.dt.bfloat16
I32 = mybir.dt.int32
U32 = mybir.dt.uint32
ALU = mybir.AluOpType
ACT = mybir.ActivationFunctionType
AX = mybir.AxisListType

P = 128
BATCH, SEQ, D = 32, 32, 256
TOK = BATCH * SEQ
TILES = TOK // P
HALF = TOK // 2
KC = D // P
HEADS, HD = 16, 16
FF = 1024
FC = FF // P
RANK = 16
COND = 200
EPS = 1e-6
NEG = -3.0e38
ADAPT = 8
EXP, TOPK = 16, 4
IM = 176
IH = IM // 2
SH = 704
SHC = [(f * P, min(P, SH - f * P)) for f in range((SH + P - 1) // P)]
SLOT_TILES = (TOK * TOPK + EXP * (P - 1)) // P
SLOTS = SLOT_TILES * P
ROW = D + 2 * EXP
NOWHERE = 1.0e6
PIPE0, RING = 2, 4
STEADY = range(PIPE0, SLOT_TILES - 1)
assert len(STEADY) % RING == 0 and PIPE0 % RING == 2

CONSTS = {}


def const_columns():
    at = 0
    for name, n in (("ident", P), ("batch_of", 4), ("head_of", 8), ("pair_of", 2), ("causal", 32), ("adapter_of", 1),
                    ("pos_of", 1), ("before", P), ("iota_e", EXP), ("tile_edge", TILES),
                    ("lower_e", EXP * EXP), ("iota_s", SLOT_TILES), ("dest", TILES * TOPK)):
        CONSTS[name] = (at, n)
        at += n
    return at


NCONST = const_columns()


def constants():
    p = np.arange(P)
    c = np.zeros((P, NCONST), np.float32)

    def put(name, a):
        at, n = CONSTS[name]
        c[:, at:at + n] = a

    put("ident", np.eye(P))
    put("batch_of", p[:, None] // SEQ == np.arange(4)[None])
    put("head_of", p[:, None] // HD == np.arange(8)[None])
    put("pair_of", p[:, None] // HD % 2 == np.arange(2)[None])
    put("causal", np.where(np.arange(SEQ)[None] <= p[:, None] % SEQ, 0.0, NEG))
    put("adapter_of", p[:, None] // RANK)
    put("pos_of", p[:, None] % SEQ)
    put("before", p[:, None] < p[None])
    put("iota_e", np.arange(EXP)[None])
    put("tile_edge", P * np.arange(TILES)[None])
    put("lower_e", (np.arange(EXP)[None] < np.arange(EXP)[:, None]).reshape(1, -1))
    put("iota_s", np.arange(SLOT_TILES)[None])
    n = np.arange(TILES)[None, :, None] * P + p[:, None, None]
    put("dest", (TOPK * n + np.arange(TOPK)[None, None]).reshape(P, -1))
    return c


def spread(ap, axis, n):
    v = ap.unsqueeze(axis)
    shape = list(v.shape)
    shape[axis] = n
    return v.broadcast_to(shape)


def program(nc, t):
    ctx = ExitStack()
    with ctx:
        top = [0]
        base = (nc.sbuf_base + 63) // 64 * 64
        nbytes = {F32: 4, F32R: 4, BF16: 2, I32: 4, U32: 4}

        def sb(name, shape, dt=F32, at=None):
            size = int(np.prod(shape[1:])) * nbytes[dt]
            size = (size + 31) // 32 * 32
            if at is None:
                at = top[0]
                top[0] += size
            assert base + at + size <= nc.sbuf_usable_end, name
            h = nc.alloc_sbuf_tensor_at(name, shape, dt, offset=base + at)
            h_at[name] = (at, size)
            return h

        h_at = {}

        def after(name):
            return h_at[name][0] + h_at[name][1]

        def sem(name):
            return ctx.enter_context(nc.semaphore(name))

        consts = sb("consts", [P, NCONST])
        K = {n: consts[:, a:a + w] for n, (a, w) in CONSTS.items()}
        ident_b = sb("ident_b", [P, P], BF16)
        causal_b = sb("causal_b", [P, SEQ], BF16)
        before_b = sb("before_b", [P, P], BF16)
        ones_b = sb("ones_b", [P, P], BF16)
        cond_b = sb("cond_b", [P, TILES], I32)
        cond_rows = sb("cond_rows", [P, TILES], I32)
        norm_w = sb("norm_w", [P, 2, KC])
        ssq = sb("ssq", [P, TILES])
        msq = sb("msq", [P, TILES])
        rms = sb("rms", [P, TILES])
        rstd = sb("rstd", [P, TILES])
        warm = sb("warm", [P, 1])
        peak = sb("peak", [P, TILES, HEADS])
        total = sb("total", [P, TILES, HEADS])
        rtotal = sb("rtotal", [P, TILES, HEADS])
        adapter_b = sb("adapter_b", [P, BATCH], I32)
        scale_p = sb("scale_p", [P, 1])
        adapter_sel = sb("adapter_sel", [P, BATCH])
        res = sb("res", [P, TILES, D])
        hT_h = sb("hT_h", [P, KC, TOK], F32R)
        hT_l = sb("hT_l", [P, KC, TOK], F32R)
        wqkv_h = sb("wqkv_h", [P, 3, KC, D], F32R)
        wqkv_l = sb("wqkv_l", [P, 3, KC, D], F32R)
        wqkv = sb("wqkv", [P, 3, KC, D], at=h_at["wqkv_l"][0])
        wg_h = sb("wg_h", [P, KC, FF], F32R)
        wg_l = sb("wg_l", [P, KC, FF], F32R)
        wg = sb("wg", [P, KC, FF], at=h_at["wg_l"][0])
        wd_h = sb("wd_h", [P, FC, D], F32R)
        wd_l = sb("wd_l", [P, FC, D], F32R)
        wd_ = sb("wd_", [P, FC, D], at=h_at["wd_l"][0])
        wu_h = sb("wu_h", [P, KC, FF], F32R)
        wu_l = sb("wu_l", [P, KC, FF], F32R)
        wu = sb("wu", [P, KC, FF], at=h_at["wu_l"][0])
        wo = sb("wo", [P, KC, D])
        a_raw = sb("a_raw", [P, KC, RANK])
        a_h = sb("a_h", [P, KC, P], F32R)
        a_l = sb("a_l", [P, KC, P], F32R)
        woa = sb("woa", [P, KC, RANK])
        b_stack = sb("b_stack", [P, FF], F32R)
        up = sb("up", [P, FC, TOK])
        act_h = sb("act_h", [P, FC, TOK], F32R, at=h_at["up"][0])
        kT = sb("kT", [P, KC, TOK], at=h_at["up"][0] + 3 * FC // 4 * TOK * 4)
        wgath = sb("wgath", [P, TILES, SEQ], at=h_at["up"][0])
        wbd = sb("wbd", [P, TILES, 4, SEQ], at=after("wgath"))
        hnorm = sb("hnorm", [P, TILES, D], at=after("wbd"))
        zone_a = top[0]
        qT = sb("qT", [P, KC, TOK])
        v_sb = sb("v_sb", [P, TILES, D])
        kx = sb("kx", [P, 2, KC, 8, 8, SEQ])
        hn = sb("hn", [P, TILES, D], at=h_at["kx"][0])
        zone_b = top[0]
        exd = sb("exd", [P, 2, HEADS, P])
        ex = sb("ex", [P, 3, 512])
        exT = sb("exT", [P, 2, 512])
        zone_end = top[0]
        b_raw = sb("b_raw", [RANK, FF], at=h_at["ex"][0])
        attnT = sb("attnT", [P, KC, TOK], at=h_at["wqkv_h"][0])
        act_l = sb("act_l", [P, 2, TOK], F32R, at=zone_b)
        g_sb = sb("g_sb", [P, 3, 512], at=after("act_l"))
        m_stack = sb("m_stack", [P, TOK], F32R, at=after("g_sb"))
        thm = sb("thm", [RANK, TOK], at=after("m_stack"))
        m_sb = sb("m_sb", [RANK, TOK], at=after("thm"))
        assert after("m_sb") <= zone_end
        e_gu = sb("e_gu", [P, EXP, KC, 2 * IM], at=zone_a)
        assert after("e_gu") <= zone_b
        e_dn = sb("e_dn", [IH, EXP, 2, D], at=h_at["wg_h"][0])
        assert after("e_dn") <= after("wd_l")
        w1_h = sb("w1_h", [P, KC, D], F32R, at=h_at["wqkv_h"][0])
        w1_l = sb("w1_l", [P, KC, D], F32R, at=after("w1_h"))
        w1 = sb("w1", [P, KC, D], at=h_at["w1_l"][0])
        bm_h = sb("bm_h", [P, D], F32R, at=after("w1_l"))
        bm_l = sb("bm_l", [P, D], F32R, at=after("bm_h"))
        bm = sb("bm", [P, D], at=h_at["bm_l"][0])
        aT_h = sb("aT_h", [P, KC, P], F32R, at=after("bm_l"))
        aT_l = sb("aT_l", [P, KC, P], F32R, at=after("aT_h"))
        aT = sb("aT", [P, KC, P], at=h_at["aT_l"][0])
        rw_h = sb("rw_h", [P, KC, P], F32R, at=after("aT_l"))
        rw_l = sb("rw_l", [P, KC, P], F32R, at=after("rw_h"))
        assert after("rw_l") <= after("wqkv_l")
        rw = sb("rw", [P, KC, EXP + 1])
        sgu_h = sb("sgu_h", [P, 2, 2, KC, P], F32R, at=h_at["wu_h"][0])
        sgu_l = sb("sgu_l", [P, 2, 2, KC, P], F32R, at=after("sgu_h"))
        sgu = sb("sgu", [P, 2, 2, KC, P], at=h_at["sgu_l"][0])
        sdn_h = sb("sdn_h", [P, 4, D], F32R, at=after("sgu_l"))
        sdn_l = sb("sdn_l", [P, 4, D], F32R, at=after("sdn_h"))
        sdn = sb("sdn", [P, 4, D], at=h_at["sdn_l"][0])
        assert after("sdn_l") <= after("wu_l")
        x1T_h = sb("x1T_h", [P, KC, TOK], F32R, at=h_at["up"][0])
        x1T_l = sb("x1T_l", [P, KC, TOK], F32R, at=after("x1T_h"))
        xam = sb("xam", [P, TOK], at=after("x1T_l"))
        xam_h = sb("xam_h", [P, TOK], F32R, at=after("xam"))
        xam_l = sb("xam_l", [P, TOK], F32R, at=after("xam_h"))
        s_act_h = sb("s_act_h", [P, 2, TOK], F32R, at=h_at["up"][0])
        s_act_l = sb("s_act_l", [P, 2, TOK], F32R, at=after("s_act_h"))
        s_g = sb("s_g", [P, 3, 512], at=after("s_act_l"))
        lgT = sb("lgT", [SEQ, TOK], at=after("s_g"))
        assert after("lgT") <= after("up") and after("xam_l") <= after("up")
        rows = sb("rows", [P, TILES, ROW], at=zone_b)
        lgx = sb("lgx", [P, TILES, EXP], at=after("rows"))
        lgm = sb("lgm", [P, 3, TILES], at=after("lgx"))
        top_v = sb("top_v", [P, TILES, 8], at=after("lgm"))
        top_i = sb("top_i", [P, TILES, 8], U32, at=after("top_v"))
        top_f = sb("top_f", [P, TILES, TOPK], at=after("top_i"))
        wts = sb("wts", [P, TILES, TOPK], at=after("top_f"))
        hot = sb("hot", [P, TILES, TOPK, EXP], at=after("wts"))
        prod = sb("prod", [P, TILES, TOPK, EXP], at=after("hot"))
        member = sb("member", [P, TILES, EXP], BF16, at=after("prod"))
        over = sb("over", [P, EXP, TILES], at=after("member"))
        ntile = sb("ntile", [P, EXP], at=after("over"))
        first = sb("first", [P, EXP], at=after("ntile"))
        last = sb("last", [P, EXP], at=after("first"))
        pairs = sb("pairs", [P, EXP, EXP], at=after("last"))
        where = sb("where", [P, TILES, EXP], at=after("pairs"))
        slot_f = sb("slot_f", [P, TILES * TOPK], at=after("where"))
        slot = sb("slot", [P, TILES * TOPK], I32, at=after("slot_f"))
        hot_s = sb("hot_s", [P, SLOT_TILES, EXP], at=after("slot"))
        hot_t = sb("hot_t", [P, SLOT_TILES, EXP], at=after("hot_s"))
        who_f = sb("who_f", [P, SLOT_TILES], at=after("hot_t"))
        who = sb("who", [P, SLOT_TILES], I32, at=after("who_f"))
        lg_sb = sb("lg_sb", [P, TILES, SEQ], at=after("who"))
        sgate = sb("sgate", [P, TILES], at=after("lg_sb"))
        assert after("sgate") <= zone_end, (after("sgate"), zone_end)
        fill = sb("fill", [P, ROW])
        slot_rows = sb("slot_rows", [P, RING, ROW], at=after("lgT"))
        assert after("slot_rows") <= after("up")
        hT = sb("hT", [P, 2, KC, P], at=h_at["up"][0])
        sil = sb("sil", [P, 2, IM], at=after("hT"))
        act = sb("act", [P, 2, IM], at=after("sil"))
        actT = sb("actT", [IH, 2, 2, P], at=after("act"))
        y = sb("y", [P, RING, D], at=after("actT"))
        pick = sb("pick", [P, RING, 2, EXP], at=after("y"))
        wd = sb("wd", [P, RING, 2], at=after("pick"))
        dest = sb("dest", [P, RING], I32, at=after("wd"))
        assert after("dest") <= after("up")
        yk = sb("yk", [P, TILES, TOPK * D], at=zone_a)
        ysum = sb("ysum", [P, TILES, 2 * D], at=h_at["wg_h"][0])
        assert after("yk") <= zone_b
        bank = [ctx.enter_context(nc.psum_tensor(f"bank{i}", [P, 512], F32)) for i in range(8)]

        slots_d = nc.dram_tensor("slots_d", (SLOTS, ROW), F32).ap()
        yk_d = nc.dram_tensor("yk_d", (TOK * TOPK, D), F32).ap()

        ld_const, ld_cond, ld_wqkv, ld_norm, ld_small = map(sem, ("ld_const", "ld_cond", "ld_wqkv", "ld_norm", "ld_small"))
        ld_x = [sem(f"ld_x{h}") for h in range(2)]
        ld_up, ld_gate, ld_down = map(sem, ("ld_up", "ld_gate", "ld_down"))
        ld_l1, ld_exp, ld_adapt = map(sem, ("ld_l1", "ld_exp", "ld_adapt"))
        ld_sgu = [sem(f"ld_sgu{r}") for r in range(2)]
        ld_sdn = [sem(f"ld_sdn{r}") for r in range(2)]
        filled, fill_set = sem("filled"), sem("fill_set")
        dve_step = sem("dve_step")
        gathered = [sem(f"gathered{i}") for i in range(TILES)]
        yk_loaded = [sem(f"yk_loaded{i}") for i in range(4)]
        wbd_ready, hid_ready, ssq_ready, msq_ready = map(sem, ("wbd_ready", "hid_ready", "ssq_ready", "msq_ready"))
        cond_ready, rms_ready, hn_ready = map(sem, ("cond_ready", "rms_ready", "hn_ready"))
        bf_ready, zero_set, m_zero = sem("bf_ready"), sem("zero_set"), sem("m_zero")
        wqkv_hi, wqkv_lo, wu_hi, wu_lo, wg_hi, wg_scaled, wg_lo, wd_hi, wd_lo, ab_hi, ab_lo = map(
            sem, ("wqkv_hi", "wqkv_lo", "wu_hi", "wu_lo", "wg_hi", "wg_scaled", "wg_lo", "wd_hi", "wd_lo", "ab_hi", "ab_lo"))
        l1_hi, l1_lo, sgu_hi, sgu_lo_dve, sdn_hi, sdn_lo_dve, sh_lo_pool = map(
            sem, ("l1_hi", "l1_lo", "sgu_hi", "sgu_lo_dve", "sdn_hi", "sdn_lo_dve", "sh_lo_pool"))
        hid_kept, hnT_ready, hT_hi, hT_lo = map(sem, ("hid_kept", "hnT_ready", "hT_hi", "hT_lo"))
        k_mm, q_mm, v_mm, k_kept, q_kept, v_kept = map(sem, ("k_mm", "q_mm", "v_mm", "k_kept", "q_kept", "v_kept"))
        kx_act, kx_dve = sem("kx_act"), sem("kx_dve")
        scored, shifted, exped, summed, normed, exT_ready, exd_act, exd_dve, pv_ready, attn_even, attn_ready = map(
            sem, ("scored", "shifted", "exped", "summed", "normed", "exT_ready", "exd_act", "exd_dve", "pv_ready",
                  "attn_even", "attn_ready"))
        woa_mm, woa_ready, up_mm, up_ready, ha_mm, mod_mm, th_ready, m_ready, m_hi, m_lo = map(
            sem, ("woa_mm", "woa_ready", "up_mm", "up_ready", "ha_mm", "mod_mm", "th_ready", "m_ready", "m_hi", "m_lo"))
        gate_mm, silu_ready, act_ready, act_hi, act_lo, down_f, down_mm, x1_ready = map(
            sem, ("gate_mm", "silu_ready", "act_ready", "act_hi", "act_lo", "down_f", "down_mm", "x1_ready"))
        x1T_mm, x1T_hi, x1T_lo, xa_mm, xam_ready, xam_hi, xam_lo, h1_mm, h1_ready = map(
            sem, ("x1T_mm", "x1T_hi", "x1T_lo", "xa_mm", "xam_ready", "xam_hi", "xam_lo", "h1_mm", "h1_ready"))
        h1T_mm, h1T_hi, h1T_lo, lgT_mm, lgT_kept, lg_mm, lg_ready = map(
            sem, ("h1T_mm", "h1T_hi", "h1T_lo", "lgT_mm", "lgT_kept", "lg_mm", "lg_ready"))
        lgx_ready, lge_ready, sg_ready, member_ready, rank_mm, rank_read, slot_ready, who_ready, scattered = map(
            sem, ("lgx_ready", "lge_ready", "sg_ready", "member_ready", "rank_mm", "rank_read", "slot_ready", "who_ready",
                  "scattered"))
        sgu_mm, s_silu_ready, s_act_ready, s_act_hi, s_act_lo, s_zero, sdn_f, sdn_mm, shared_added = map(
            sem, ("sgu_mm", "s_silu_ready", "s_act_ready", "s_act_hi", "s_act_lo", "s_zero", "sdn_f", "sdn_mm",
                  "shared_added"))
        r_loaded = [sem(f"r_loaded{i}") for i in range(RING)]
        r_sent = [sem(f"r_sent{i}") for i in range(RING)]
        r_in, r_hT, r_gu, r_sil, r_act, r_ta, r_actT, r_dn, r_wd, r_y, r_pick = map(
            sem, ("r_in", "r_hT", "r_gu", "r_sil", "r_act", "r_ta", "r_actT", "r_dn", "r_wd", "r_y", "r_pick"))
        out_ready, stored = sem("out_ready"), sem("stored")

        def ring_count(s, r):
            return 4 * (s - r) + 16

        def half(h):
            return slice(HALF * h, HALF * h + HALF)

        def mask_k(op, done, g, c, heads):
            src = kT[:, c, 2 * P * g:2 * P * g + 2 * P].rearrange("p (b k) -> p b k", k=SEQ)
            for e in heads:
                ins = op(kx[:, g % 2, c, :, e, :], src, K["head_of"][:, e:e + 1])
            ins.then_inc(done, 1)

        def on_diagonal(copy, done, u, b4s):
            for b4 in b4s:
                ins = copy(exd[SEQ * b4:SEQ * b4 + SEQ, u % 2, :, SEQ * b4:SEQ * b4 + SEQ],
                           exT[SEQ * b4:SEQ * b4 + SEQ, u % 2, :].rearrange("p (h q) -> p h q", q=SEQ))
            ins.then_inc(done, 1)

        block = ctx.enter_context(nc.Block())

        @block.sync
        def _(sp):
            def halves(name):
                return t[name].rearrange("(k p) n -> p k n", p=P)

            sp.dma_start(cond_b[:, :], t["cond_b"]).then_inc(ld_cond, 16)
            sp.dma_start(consts[:, :], t["consts"]).then_inc(ld_const, 16)
            xt = t["x"].rearrange("(t p) d -> p t d", p=P)
            sp.dma_start(res[:, 0:4, :], xt[:, 0:4, :]).then_inc(ld_x[0], 16)
            sp.dma_start(norm_w[:].rearrange("p i k -> p (i k)"), t["norms"]).then_inc(ld_norm, 16)
            sp.dma_start(res[:, 4:8, :], xt[:, 4:8, :]).then_inc(ld_x[1], 16)
            sp.wait_ge(gathered[TILES // 2 - 1], 16)
            for i, n in enumerate(("WqT", "WkT", "WvT")):
                sp.dma_start(wqkv[:, i], halves(n)).then_inc(ld_wqkv, 16)
            sp.wait_ge(gathered[TILES - 1], 16)
            sp.dma_start(wu[:], halves("WupT")).then_inc(ld_up, 16)
            sp.dma_start(wo[:], halves("Wo")).then_inc(ld_small, 16)
            sp.dma_start(a_raw[:], halves("A")).then_inc(ld_small, 16)
            sp.dma_start(b_raw[:], t["B"]).then_inc(ld_small, 16)
            sp.dma_start(wg[:], halves("WinT")).then_inc(ld_gate, 16)
            sp.dma_start(wd_[:], halves("WdT")).then_inc(ld_down, 16)
            sp.dma_start(adapter_b[:], t["adapter_b"]).then_inc(ld_adapt, 16)
            sp.dma_start(scale_p[:], t["scale_p"]).then_inc(ld_adapt, 16)
            sp.dma_start(rw[:], halves("router")).then_inc(ld_adapt, 16)
            sp.wait_ge(fill_set, 2)
            sp.wait_ge(hid_ready, TILES)
            sp.wait_ge(ld_down, 16)
            for s in range(0, SLOT_TILES, 8):
                n = min(8, SLOT_TILES - s)
                sp.dma_start(slots_d[s * P:(s + n) * P, :].rearrange("(s p) c -> p s c", p=P),
                             spread(fill[:], 1, n)).then_inc(filled, 16)

            def load_sgu(f):
                a, n = SHC[f]
                for m in range(2):
                    w = halves("s_gu")[:, :, SH * m + a:SH * m + a + n]
                    dst = sgu[:, f % 2, m, :, 0:n] if n == P else sgu[:, f % 2, 0, :, n * m:n * m + n]
                    sp.dma_start(dst, w).then_inc(ld_sgu[f % 2], 16)

            def load_sdn(f):
                a, n = SHC[f]
                sp.dma_start(sdn[0:n, f % 4], t["s_dn"][a:a + n, :]).then_inc(ld_sdn[f // 5], 16)

            sp.wait_ge(up_mm, 2 * FC)
            load_sgu(0)
            load_sgu(1)
            for f in range(4):
                load_sdn(f)
            sp.wait_ge(mod_mm, 2)
            sp.dma_start(aT[:], halves("AT")).then_inc(ld_l1, 16)
            sp.dma_start(w1[:], halves("W1T")).then_inc(ld_l1, 16)
            sp.dma_start(bm[:], t["BmT"]).then_inc(ld_l1, 16)
            for e in range(EXP):
                sp.dma_start(e_gu[:, e], t["e_gu"][e].rearrange("(k p) n -> p k n", p=P)).then_inc(ld_exp, 16)
            sp.wait_ge(down_mm, 4)
            for e in range(EXP):
                sp.dma_start(e_dn[:, e], t["e_dn"][e].rearrange("(k p) n -> p k n", p=IH)).then_inc(ld_exp, 16)
            for f in range(2, len(SHC)):
                sp.wait_ge(sgu_mm, 2 * f - 2)
                load_sgu(f)
                if f >= 4:
                    sp.wait_ge(sdn_f, f - 3)
                    load_sdn(f)

            def load(s, r, first_round):
                if not first_round:
                    sp.wait_ge(r_in, s - 3)
                    sp.wait_ge(r_wd, s - 3)
                sp.dma_start(slot_rows[:, r, :], slots_d[bass.ds(s * P, P), :]).then_inc(r_loaded[r], 16)

            sp.wait_ge(scattered, 16 * TILES * TOPK)
            head = 4 + (SLOT_TILES - 4) % RING
            for s in range(head):
                load(s, s % RING, s < RING)
            with sp.Fori(head, SLOT_TILES - RING + 1, RING) as i:
                for j in range(RING):
                    load(i + j, (head + j) % RING, False)
            for r in range(RING):
                sp.wait_ge(r_sent[r], 16 * len(range(r, SLOT_TILES, RING)))
            ykt = yk_d.rearrange("(t p k) d -> p t (k d)", p=P, k=TOPK)
            for i in range(4):
                sp.dma_start(yk[:, 2 * i:2 * i + 2], ykt[:, 2 * i:2 * i + 2]).then_inc(yk_loaded[i], 16)
            ot = t["out"].rearrange("(t p) d -> t p d", p=P)
            for i in range(TILES):
                sp.wait_ge(out_ready, i + 1)
                sp.dma_start(ot[i], res[:, i]).then_inc(stored, 16)
            sp.wait_ge(stored, 16 * TILES)

        @block.gpsimd
        def _(pool):
            G = nc.gpsimd
            pool.wait_ge(cond_ready, 1)
            wrows = t["cond_w"].rearrange("s c d -> (s c) d")
            for i in range(TILES):
                pool.indirect_dma_start(wgath[:, i, :], None, wrows,
                                        bass.IndirectOffsetOnAxis(cond_rows[:, i:i + 1], 0),
                                        bounds_check=COND * SEQ - 1).then_inc(gathered[i], 16)
            G.memset(a_h[:].bitcast(F32), 0.0).then_inc(zero_set, 1)
            G.memset(a_l[:].bitcast(F32), 0.0).then_inc(zero_set, 1)
            G.memset(b_stack[:].bitcast(F32), 0.0).then_inc(zero_set, 1)
            G.memset(exd[:], 0.0).then_inc(zero_set, 1)
            G.memset(fill[:, 0:D + EXP], 0.0).then_inc(fill_set, 1)
            G.memset(fill[:, D + EXP:ROW], NOWHERE).then_inc(fill_set, 1)

            def norm(u):
                pool.wait_ge(summed, u + 1)
                e3 = ex[:, u % 3, :].rearrange("p (a k) -> p a k", k=SEQ)
                G.tensor_tensor(e3, e3, spread(rtotal[:, u, :], 2, SEQ), ALU.mult).then_inc(normed, 1)

            for k in range(KC):
                pool.wait_ge(wg_hi, k + 1)
                G.tensor_tensor(wg_l[:, k], wg[:, k], wg_h[:, k].bitcast(F32), ALU.subtract).then_inc(wg_lo, 1)
            for u in range(TILES):
                norm(u)
                if u % 2:
                    j = u // 2
                    pool.wait_ge(wd_hi, j + 1)
                    G.tensor_tensor(wd_l[:, 2 * j:2 * j + 2], wd_[:, 2 * j:2 * j + 2], wd_h[:, 2 * j:2 * j + 2].bitcast(F32),
                                    ALU.subtract).then_inc(wd_lo, 1)
            pool.wait_ge(pv_ready, TILES)
            G.memset(m_stack[:].bitcast(F32), 0.0).then_inc(m_zero, 1)
            pool.wait_ge(mod_mm, 2)
            G.memset(rw_h[:].bitcast(F32), 0.0).then_inc(m_zero, 1)
            G.memset(rw_l[:].bitcast(F32), 0.0).then_inc(m_zero, 1)
            for f in range(2):
                pool.wait_ge(sgu_hi, f + 1)
                G.tensor_tensor(sgu_l[:, f], sgu[:, f], sgu_h[:, f].bitcast(F32), ALU.subtract).then_inc(sh_lo_pool, 1)
            pool.wait_ge(sdn_hi, 1)
            G.tensor_tensor(sdn_l[:], sdn[:], sdn_h[:].bitcast(F32), ALU.subtract).then_inc(sh_lo_pool, 1)
            for i, (lo, raw, hi) in enumerate(((aT_l, aT, aT_h), (w1_l, w1, w1_h), (bm_l, bm, bm_h))):
                pool.wait_ge(l1_hi, i + 1)
                G.tensor_tensor(lo[:], raw[:], hi[:].bitcast(F32), ALU.subtract).then_inc(l1_lo, 1)
            pool.wait_ge(l1_hi, 4)
            pool.wait_ge(m_zero, 3)
            G.tensor_tensor(rw_l[:, :, 0:EXP + 1], rw[:], rw_h[:, :, 0:EXP + 1].bitcast(F32),
                            ALU.subtract).then_inc(l1_lo, 1)

            pool.wait_ge(filled, 16 * len(range(0, SLOT_TILES, 8)))
            pool.wait_ge(slot_ready, 1)
            pool.wait_ge(h1_ready, 4)
            for i in range(TILES):
                for k in range(TOPK):
                    pool.indirect_dma_start(slots_d, bass.IndirectOffsetOnAxis(slot[:, i * TOPK + k:i * TOPK + k + 1], 0),
                                            rows[:, i, :], None, bounds_check=SLOTS - 1).then_inc(scattered, 16)

            within = pool.to_reg(TOK * TOPK - 1)

            def send(s, r):
                pool.wait_ge(r_y, s + 1)
                pool.indirect_dma_start(yk_d, bass.IndirectOffsetOnAxis(dest[:, r:r + 1], 0), y[:, r, :], None,
                                        bounds_check=within, oob_is_err=False).then_inc(r_sent[r], 16)

            for s in range(SLOT_TILES):
                send(s, s % RING)

        @block.scalar
        def _(act_e):
            A = nc.scalar.activation
            act_e.wait_ge(ld_const, 16)
            A(warm[:], K["ident"][:, 0:1], ACT.Sqrt)
            act_e.wait_ge(ld_norm, 16)

            def keep_hid(h):
                for g in range(2 * h, 2 * h + 2):
                    act_e.wait_ge(hid_ready, 2 * g + 2)
                    A(hn[:, 2 * g:2 * g + 2].rearrange("p t d -> p (t d)"), bank[g][:, :], ACT.Copy).then_inc(hid_kept, 1)
                for i in range(4 * h, 4 * h + 4):
                    act_e.wait_ge(hid_kept, i // 2 + 1)
                    A(hnorm[:, i], hn[:, i], ACT.Square, accum_out=ssq[:, i:i + 1]).then_inc(ssq_ready, 1)

            def root(h):
                act_e.wait_ge(msq_ready, h + 1)
                A(rms[:, 4 * h:4 * h + 4], msq[:, 4 * h:4 * h + 4], ACT.Sqrt).then_inc(rms_ready, 1)

            def keep_hT(h):
                act_e.wait_ge(hnT_ready, 4 * h + 4)
                for k in range(KC):
                    A(hT_h[:, k, half(h)], bank[4 + 2 * h + k][:, :], ACT.Copy).then_inc(hT_hi, 1)

            keep_hid(0)
            root(0)
            keep_hid(1)
            root(1)
            act_e.wait_ge(ld_wqkv, 48)
            for k in range(KC):
                A(wqkv_h[:, :, k], wqkv[:, :, k], ACT.Copy, scale=norm_w[:, 0, k:k + 1]).then_inc(wqkv_hi, 1)
            act_e.wait_ge(ld_up, 16)
            A(wu_h[:, 0], wu[:, 0], ACT.Copy, scale=norm_w[:, 1, 0:1]).then_inc(wu_hi, 1)
            keep_hT(0)
            A(wu_h[:, 1], wu[:, 1], ACT.Copy, scale=norm_w[:, 1, 1:2]).then_inc(wu_hi, 1)
            keep_hT(1)
            act_e.wait_ge(ld_small, 48)
            act_e.wait_ge(zero_set, 3)
            for k in range(KC):
                A(a_h[:, k, 0:RANK], a_raw[:, k], ACT.Copy, scale=norm_w[:, 1, k:k + 1]).then_inc(ab_hi, 1)
            A(b_stack[0:RANK], b_raw[:], ACT.Copy).then_inc(ab_hi, 1)
            A(b_stack[SEQ:SEQ + RANK], b_raw[:], ACT.Copy).then_inc(ab_hi, 1)

            def keep_qv(h):
                for c in range(KC):
                    act_e.wait_ge(q_mm, 2 * h + 1 + c)
                    A(qT[:, c, half(h)], bank[c][:, :], ACT.Copy, scale=HD ** -0.5).then_inc(q_kept, 1)
                for g in range(2 * h, 2 * h + 2):
                    act_e.wait_ge(v_mm, g + 1)
                    A(v_sb[:, 2 * g:2 * g + 2].rearrange("p t d -> p (t d)"), bank[4 + g % 2][:, :],
                      ACT.Copy).then_inc(v_kept, 1)

            def keys(g, c):
                act_e.wait_ge(k_kept, 2 * (g // 2) + 1 + c)
                if g >= 2:
                    act_e.wait_ge(scored, 2 * g - 2)
                mask_k(lambda o, i, m: A(o, i, ACT.Copy, scale=m), kx_act, g, c, range(5, 8))

            def keep_up(i):
                act_e.wait_ge(up_mm, i + 1)
                if i == 12:
                    act_e.wait_ge(kx_dve, 8)
                A(up[:, i // 2, half(i % 2)], bank[6 + i % 2][:, :], ACT.Copy).then_inc(up_ready, 1)

            def exp(u):
                act_e.wait_ge(shifted, u + 1)
                A(ex[:, u % 3, :], ex[:, u % 3, :], ACT.Exp).then_inc(exped, 1)

            def diagonal(u):
                act_e.wait_ge(exT_ready, u + 1)
                if u >= 2:
                    act_e.wait_ge(pv_ready, u - 1)
                else:
                    act_e.wait_ge(zero_set, 4)
                on_diagonal(lambda o, i: A(o, i, ACT.Copy), exd_act, u, (2, 3))

            def even_heads(u):
                act_e.wait_ge(pv_ready, u + 1)
                o = bank[4 + u % 2][:, :].rearrange("p (c e q) -> p c e q", c=KC, e=2)
                A(attnT[:, :, P * u:P * u + P], o[:, :, 0, :], ACT.Copy, scale=K["pair_of"][:, 0:1]).then_inc(attn_even, 1)

            keep_qv(0)
            for g in range(2):
                for c in range(KC):
                    keys(g, c)
            keep_qv(1)
            act_e.wait_ge(woa_mm, 1)
            A(woa[:].rearrange("p k r -> p (k r)"), bank[6][:, 0:KC * RANK], ACT.Copy).then_inc(woa_ready, 1)
            act_e.wait_ge(ld_gate, 16)
            for k in range(KC):
                A(wg[:, k], wg[:, k], ACT.Copy, scale=norm_w[:, 1, k:k + 1]).then_inc(wg_scaled, 1)
                act_e.wait_ge(wg_scaled, k + 1)
                A(wg_h[:, k], wg[:, k], ACT.Copy).then_inc(wg_hi, 1)
            act_e.wait_ge(ld_down, 16)
            for u in range(TILES):
                exp(u)
                keep_up(2 * u)
                if u:
                    diagonal(u - 1)
                keep_up(2 * u + 1)
                if u >= 2:
                    even_heads(u - 2)
                if u == 0:
                    keys(2, 0)
                    keys(2, 1)
                if u in (2, 3):
                    keys(3, u - 2)
                if u % 2:
                    j = u // 2
                    A(wd_h[:, 2 * j:2 * j + 2], wd_[:, 2 * j:2 * j + 2], ACT.Copy).then_inc(wd_hi, 1)
            diagonal(TILES - 1)
            even_heads(TILES - 2)
            even_heads(TILES - 1)
            for h in range(2):
                act_e.wait_ge(mod_mm, h + 1)
                A(thm[:, half(h)], bank[4 + h][SEQ * h:SEQ * h + RANK, :], ACT.Tanh).then_inc(th_ready, 1)
            act_e.wait_ge(m_zero, 1)
            for h in range(2):
                act_e.wait_ge(m_ready, h + 1)
                A(m_stack[0:RANK, half(h)], m_sb[:, half(h)], ACT.Copy).then_inc(m_hi, 1)
                A(m_stack[64:64 + RANK, half(h)], m_sb[:, half(h)], ACT.Copy).then_inc(m_hi, 1)

            def high_parts(i):
                if i < 2:
                    act_e.wait_ge(ld_sgu[i], 32)
                    A(sgu_h[:, i], sgu[:, i], ACT.Copy).then_inc(sgu_hi, 1)
                elif i == 2:
                    act_e.wait_ge(ld_sdn[0], 64)
                    A(sdn_h[:], sdn[:], ACT.Copy).then_inc(sdn_hi, 1)
                elif i < 6:
                    if i == 3:
                        act_e.wait_ge(ld_l1, 48)
                    hi, raw = ((aT_h, aT), (w1_h, w1), (bm_h, bm))[i - 3]
                    A(hi[:], raw[:], ACT.Copy).then_inc(l1_hi, 1)
                elif i == 6:
                    act_e.wait_ge(m_zero, 3)
                    act_e.wait_ge(ld_adapt, 48)
                    A(rw_h[:, :, 0:EXP + 1], rw[:], ACT.Copy).then_inc(l1_hi, 1)

            def act_high(i):
                act_e.wait_ge(act_ready, i + 1)
                A(act_h[:, i // 2, half(i % 2)], g_sb[:, i % 3, :], ACT.Copy).then_inc(act_hi, 1)

            for i in range(2 * FC):
                act_e.wait_ge(gate_mm, i + 1)
                if i >= 3:
                    act_e.wait_ge(act_lo, i - 2)
                A(g_sb[:, i % 3, :], bank[6 + i % 2][:, :], ACT.Silu).then_inc(silu_ready, 1)
                act_high(i)
                if i >= 8:
                    high_parts(i - 8)
            for h in range(2):
                act_e.wait_ge(x1T_mm, 4 * h + 4)
                for k in range(KC):
                    A(x1T_h[:, k, half(h)], bank[4 + 2 * h + k][:, :], ACT.Copy).then_inc(x1T_hi, 1)
            for h in range(2):
                act_e.wait_ge(xam_ready, h + 1)
                A(xam_h[:, half(h)], xam[:, half(h)], ACT.Copy).then_inc(xam_hi, 1)
            for g in range(4):
                act_e.wait_ge(h1_mm, g + 1)
                A(rows[:, 2 * g:2 * g + 2, 0:D], bank[2 + g][:, :].rearrange("p (t d) -> p t d", t=2),
                  ACT.Copy).then_inc(h1_ready, 1)
            for h in range(2):
                act_e.wait_ge(h1T_mm, 4 * h + 4)
                for k in range(KC):
                    A(hT_h[:, k, half(h)], bank[((6, 7), (0, 1))[h][k]][:, :], ACT.Copy).then_inc(h1T_hi, 1)
            for h in range(2):
                act_e.wait_ge(lgT_mm, h + 1)
                A(lgT[:, half(h)], bank[2 + h][0:SEQ, :], ACT.Copy).then_inc(lgT_kept, 1)
            act_e.wait_ge(lgx_ready, 1)
            A(lgx[:], lgx[:], ACT.Exp).then_inc(lge_ready, 1)
            A(sgate[:], lg_sb[:, :, EXP], ACT.Sigmoid).then_inc(sg_ready, 1)

            def s_silu(i):
                f, h = i // 2, i % 2
                act_e.wait_ge(sgu_mm, i + 1)
                if i >= 3:
                    act_e.wait_ge(s_act_lo, i - 2)
                b_ = bank[(6, 0)[h]]
                if SHC[f][1] == P:
                    A(s_g[:, i % 3, :], b_[:, :], ACT.Silu).then_inc(s_silu_ready, 1)
                else:
                    A(s_g[64:128, i % 3, :], b_[0:64, :], ACT.Silu).then_inc(s_silu_ready, 1)

            def s_high(i):
                f, h = i // 2, i % 2
                n = SHC[f][1]
                act_e.wait_ge(s_act_ready, i + 1)
                if f >= 2:
                    act_e.wait_ge(sdn_f, f - 1)
                A(s_act_h[0:n, f % 2, half(h)], s_g[0:n, i % 3, :], ACT.Copy).then_inc(s_act_hi, 1)

            def s_gu_high(f):
                r, m = f % 2, 2 if SHC[f][1] == P else 1
                act_e.wait_ge(ld_sgu[r], 32 * (f // 2 + 1))
                A(sgu_h[:, r, 0:m], sgu[:, r, 0:m], ACT.Copy).then_inc(sgu_hi, 1)

            def s_dn_high(f):
                n = SHC[f][1]
                act_e.wait_ge(ld_sdn[f // 5], (80, 16)[f // 5])
                A(sdn_h[0:n, f % 4], sdn[0:n, f % 4], ACT.Copy).then_inc(sdn_hi, 1)

            for i in range(2 * len(SHC)):
                s_silu(i)
                s_high(i)
                if i % 2 == 0 and 2 <= i < 2 * len(SHC) - 2:
                    s_gu_high(i // 2 + 1)
                if i in (8, 10):
                    s_dn_high(i // 2)

            def keep_in(s, q):
                act_e.wait_ge(r_in, s + 1)
                A(hT[:, q], bank[2 + q][:, 0:D].rearrange("p (k n) -> p k n", k=KC), ACT.Copy).then_inc(r_hT, 1)

            def silu(s, q):
                act_e.wait_ge(r_gu, s + 1)
                A(sil[:, q], bank[q][:, 0:IM], ACT.Silu).then_inc(r_sil, 1)

            def weigh(s, q, r, again):
                act_e.wait_ge(r_dn, s + 1)
                act_e.wait_ge(r_wd, s + 1)
                if again:
                    act_e.wait_ge(r_sent[r], ring_count(s, r) - 16)
                A(y[:, r, :], bank[6 + q][:, 0:D], ACT.Copy, scale=wd[:, r, 0:1]).then_inc(r_y, 1)

            keep_in(0, 0)
            for s in range(PIPE0):
                if s >= 2:
                    act_e.wait_ge(r_act, s - 1)
                silu(s, s % 2)
                keep_in(s + 1, (s + 1) % 2)

            def step(s, j, again):
                q = (PIPE0 + j) % 2
                act_e.wait_ge(r_act, s - 1)
                silu(s, q)
                act_e.wait_ge(r_gu, s)
                keep_in(s + 1, 1 - q)
                weigh(s - 2, q, (PIPE0 + j - 2) % RING, again)

            for j in range(RING):
                step(PIPE0 + j, j, False)
            with act_e.Fori(PIPE0 + RING, SLOT_TILES - RING, RING) as i:
                for j in range(RING):
                    step(i + j, j, True)
            s = SLOT_TILES - 1
            act_e.wait_ge(r_act, s - 1)
            silu(s, s % 2)
            for s in range(SLOT_TILES - 3, SLOT_TILES):
                weigh(s, s % 2, s % RING, True)

        @block.vector
        def _(dve):
            V = nc.vector
            steps = [0]

            def link(ins):
                steps[0] += 1
                ins.then_inc(dve_step, 1)
                dve.wait_ge(dve_step, steps[0])

            dve.wait_ge(ld_cond, 16)
            dve.wait_ge(ld_const, 16)
            V.tensor_scalar(cond_rows[:], cond_b[:], float(SEQ), K["pos_of"], ALU.mult, ALU.add).then_inc(cond_ready, 1)
            V.tensor_copy(ident_b[:], K["ident"]).then_inc(bf_ready, 1)
            V.tensor_copy(causal_b[:], K["causal"]).then_inc(bf_ready, 1)
            V.tensor_copy(before_b[:], K["before"]).then_inc(bf_ready, 1)
            V.memset(ones_b[:], 1.0).then_inc(bf_ready, 1)
            for i in range(TILES):
                dve.wait_ge(gathered[i], 16)
                V.tensor_tensor(wbd[:, i], spread(wgath[:, i], 1, 4), spread(K["batch_of"], 2, SEQ),
                                ALU.mult).then_inc(wbd_ready, 1)
            def normalize(h):
                dve.wait_ge(ssq_ready, 4 * h + 4)
                V.tensor_scalar(msq[:, 4 * h:4 * h + 4], ssq[:, 4 * h:4 * h + 4], 1.0 / D, EPS, ALU.mult, ALU.add).then_inc(msq_ready, 1)
                dve.wait_ge(rms_ready, h + 1)
                link(V.reciprocal(rstd[:, 4 * h:4 * h + 4], rms[:, 4 * h:4 * h + 4]))
                for i in range(4 * h, 4 * h + 4):
                    V.tensor_scalar(hnorm[:, i], hn[:, i], rstd[:, i:i + 1], None, ALU.mult).then_inc(hn_ready, 1)

            def low_hT(h):
                for k in range(KC):
                    dve.wait_ge(hT_hi, 2 * h + k + 1)
                    V.tensor_tensor(hT_l[:, k, half(h)], bank[4 + 2 * h + k][:, :], hT_h[:, k, half(h)].bitcast(F32),
                                    ALU.subtract).then_inc(hT_lo, 1)

            def low_up(k):
                dve.wait_ge(wu_hi, k + 1)
                V.scalar_tensor_tensor(wu_l[:, k], wu[:, k], norm_w[:, 1, k:k + 1], wu_h[:, k].bitcast(F32),
                                       ALU.mult, ALU.subtract).then_inc(wu_lo, 1)

            normalize(0)
            normalize(1)
            dve.wait_ge(ld_norm, 16)
            for k in range(KC):
                dve.wait_ge(wqkv_hi, k + 1)
                V.scalar_tensor_tensor(wqkv_l[:, :, k], wqkv[:, :, k], norm_w[:, 0, k:k + 1],
                                       wqkv_h[:, :, k].bitcast(F32), ALU.mult, ALU.subtract).then_inc(wqkv_lo, 1)

            low_hT(0)
            low_hT(1)
            V.tensor_tensor(res[:], hn[:], res[:], ALU.add)
            low_up(0)
            low_up(1)
            for k in range(KC):
                dve.wait_ge(ab_hi, k + 1)
                V.scalar_tensor_tensor(a_l[:, k, 0:RANK], a_raw[:, k], norm_w[:, 1, k:k + 1],
                                       a_h[:, k, 0:RANK].bitcast(F32), ALU.mult, ALU.subtract).then_inc(ab_lo, 1)
            dve.wait_ge(ab_hi, 4)
            V.tensor_tensor(b_stack[64:64 + RANK], b_raw[:], b_stack[0:RANK].bitcast(F32), ALU.subtract).then_inc(ab_lo, 1)

            def keep_k(h):
                for c in range(KC):
                    dve.wait_ge(k_mm, 2 * h + 1 + c)
                    V.tensor_copy(kT[:, c, half(h)], bank[2 + c][:, :]).then_inc(k_kept, 1)

            def keys(g, c):
                dve.wait_ge(k_kept, 2 * (g // 2) + 1 + c)
                if g >= 2:
                    dve.wait_ge(scored, 2 * g - 2)
                mask_k(lambda o, i, m: V.tensor_scalar(o, i, m, None, ALU.mult), kx_dve, g, c, range(5))

            def shift(u):
                dve.wait_ge(scored, u + 1)
                s3 = bank[u % 4][:, :].rearrange("p (a k) -> p a k", k=SEQ)
                link(V.reduce_max(peak[:, u, :], s3, AX.X))
                V.tensor_tensor(ex[:, u % 3, :].rearrange("p (a k) -> p a k", k=SEQ), s3,
                                spread(peak[:, u, :], 2, SEQ), ALU.subtract).then_inc(shifted, 1)

            def sums(u):
                dve.wait_ge(exped, u + 1)
                link(V.reduce_sum(total[:, u, :], ex[:, u % 3, :].rearrange("p (a k) -> p a k", k=SEQ), AX.X))
                V.reciprocal(rtotal[:, u, :], total[:, u, :]).then_inc(summed, 1)

            def turn(u):
                dve.wait_ge(normed, u + 1)
                if u >= 2:
                    dve.wait_ge(exd_act, u - 1)
                V.transpose(exT[:, u % 2, :], ex[:, u % 3, :]).then_inc(exT_ready, 1)

            def diagonal(u):
                dve.wait_ge(exT_ready, u + 1)
                if u >= 2:
                    dve.wait_ge(pv_ready, u - 1)
                else:
                    dve.wait_ge(zero_set, 4)
                on_diagonal(V.tensor_copy, exd_dve, u, (0, 1))

            def odd_heads(u):
                dve.wait_ge(attn_even, u + 1)
                o = bank[4 + u % 2][:, :].rearrange("p (c e q) -> p c e q", c=KC, e=2)
                a_ = attnT[:, :, P * u:P * u + P]
                V.scalar_tensor_tensor(a_, o[:, :, 1, :], K["pair_of"][:, 1:2], a_, ALU.mult, ALU.add).then_inc(attn_ready, 1)

            keep_k(0)
            for g in range(2):
                for c in range(KC):
                    keys(g, c)
            keep_k(1)
            for u in range(TILES):
                shift(u)
                if u:
                    turn(u - 1)
                    diagonal(u - 1)
                sums(u)
                if u >= 2:
                    odd_heads(u - 2)
                if u == 0:
                    keys(2, 0)
                    keys(2, 1)
                if u in (2, 3):
                    keys(3, u - 2)
            turn(TILES - 1)
            diagonal(TILES - 1)
            odd_heads(TILES - 2)
            odd_heads(TILES - 1)
            for h in range(2):
                dve.wait_ge(th_ready, h + 1)
                dve.wait_ge(ha_mm, h + 1)
                V.scalar_tensor_tensor(m_sb[:, half(h)], thm[:, half(h)], 0.1, bank[h][0:RANK, :],
                                       ALU.mult, ALU.mult).then_inc(m_ready, 1)
            for h in range(2):
                dve.wait_ge(m_hi, 2 * h + 1)
                V.tensor_tensor(m_stack[SEQ:SEQ + RANK, half(h)], m_sb[:, half(h)], m_stack[0:RANK, half(h)].bitcast(F32),
                                ALU.subtract).then_inc(m_lo, 1)

            def act_low(i):
                f = i // 2
                dve.wait_ge(act_hi, i + 1)
                if f >= 2:
                    dve.wait_ge(down_f, f - 1)
                V.tensor_tensor(act_l[:, f % 2, half(i % 2)], g_sb[:, i % 3, :], act_h[:, f, half(i % 2)].bitcast(F32),
                                ALU.subtract).then_inc(act_lo, 1)

            for i in range(2 * FC):
                dve.wait_ge(silu_ready, i + 1)
                dve.wait_ge(up_ready, i + 1)
                V.tensor_tensor(g_sb[:, i % 3, :], g_sb[:, i % 3, :], up[:, i // 2, half(i % 2)],
                                ALU.mult).then_inc(act_ready, 1)
                act_low(i)
            for i in range(4):
                dve.wait_ge(down_mm, i + 1)
                r2 = res[:, 2 * i:2 * i + 2].rearrange("p t d -> p (t d)")
                V.tensor_tensor(r2, bank[i][:, :], r2, ALU.add).then_inc(x1_ready, 1)
            dve.wait_ge(ld_adapt, 48)
            link(V.tensor_scalar(adapter_sel[:], adapter_b[:], K["adapter_of"], scale_p[:, 0:1], ALU.is_equal, ALU.mult))
            for h in range(2):
                for k in range(KC):
                    dve.wait_ge(x1T_hi, 2 * h + k + 1)
                    V.tensor_tensor(x1T_l[:, k, half(h)], bank[4 + 2 * h + k][:, :], x1T_h[:, k, half(h)].bitcast(F32),
                                    ALU.subtract).then_inc(x1T_lo, 1)
            for h in range(2):
                dve.wait_ge(xa_mm, h + 1)
                V.tensor_tensor(xam[:, half(h)].rearrange("p (b s) -> p b s", s=SEQ),
                                bank[h][:, :].rearrange("p (b s) -> p b s", s=SEQ),
                                spread(adapter_sel[:, 16 * h:16 * h + 16], 2, SEQ), ALU.mult).then_inc(xam_ready, 1)
            for h in range(2):
                dve.wait_ge(xam_hi, h + 1)
                V.tensor_tensor(xam_l[:, half(h)], xam[:, half(h)], xam_h[:, half(h)].bitcast(F32),
                                ALU.subtract).then_inc(xam_lo, 1)
            for h in range(2):
                for k in range(KC):
                    dve.wait_ge(h1T_hi, 2 * h + k + 1)
                    V.tensor_tensor(hT_l[:, k, half(h)], bank[((6, 7), (0, 1))[h][k]][:, :],
                                    hT_h[:, k, half(h)].bitcast(F32), ALU.subtract).then_inc(h1T_lo, 1)

            dve.wait_ge(lg_mm, 1)
            V.tensor_copy(lg_sb[:].rearrange("p t e -> p (t e)"), bank[4][:, 0:TILES * SEQ]).then_inc(lg_ready, 1)
            dve.wait_ge(lg_ready, 1)
            lg = lg_sb[:, :, 0:EXP]
            link(V.reduce_max(lgm[:, 0, :], lg, AX.X))
            V.tensor_tensor(lgx[:], lg, spread(lgm[:, 0, :], 2, EXP), ALU.subtract).then_inc(lgx_ready, 1)
            dve.wait_ge(lge_ready, 1)
            link(V.reduce_sum(lgm[:, 1, :], lgx[:], AX.X))
            link(V.reciprocal(lgm[:, 2, :], lgm[:, 1, :]))
            link(V.tensor_tensor(lgx[:], lgx[:], spread(lgm[:, 2, :], 2, EXP), ALU.mult))
            for i in range(TILES):
                ins = V.max(top_v[:, i], lgx[:, i])
            link(ins)
            for i in range(TILES):
                ins = V.max_index(top_i[:, i], top_v[:, i], lgx[:, i])
            link(ins)
            link(V.tensor_copy(top_f[:], top_i[:, :, 0:TOPK]))
            link(V.tensor_tensor(hot[:], spread(top_f[:], 3, EXP),
                                 spread(spread(K["iota_e"], 1, TOPK), 1, TILES), ALU.is_equal))
            with nc.allow_low_precision(reason="zeros and ones"):
                V.tensor_reduce(member[:], hot[:].rearrange("p t k e -> p t e k"), AX.X, ALU.add).then_inc(member_ready, 1)
            def find_slots():
                dve.wait_ge(rank_mm, 1)
                rank = bank[5][:, 0:P].rearrange("p (t e) -> p t e", e=EXP)
                count = bank[5][:, P:P + EXP]
                link(V.tensor_tensor(over[:], spread(count, 2, TILES), spread(K["tile_edge"], 1, EXP), ALU.is_gt))
                link(V.reduce_sum(ntile[:], over[:], AX.X))
                link(V.tensor_tensor(pairs[:], spread(ntile[:], 1, EXP), K["lower_e"].rearrange("p (a b) -> p a b", a=EXP), ALU.mult))
                link(V.reduce_sum(first[:], pairs[:], AX.X))
                V.scalar_tensor_tensor(where[:], spread(first[:], 1, TILES), float(P), rank, ALU.mult, ALU.add).then_inc(rank_read, 1)
                dve.wait_ge(rank_read, 1)
                link(V.tensor_tensor(prod[:], hot[:], spread(where[:], 2, TOPK), ALU.mult))
                link(V.reduce_sum(slot_f[:], prod[:].rearrange("p t k e -> p (t k) e"), AX.X))
                V.tensor_copy(slot[:], slot_f[:]).then_inc(slot_ready, 1)

            def find_experts():
                link(V.tensor_tensor(last[:], first[:], ntile[:], ALU.add))
                link(V.memset(last[:, EXP - 1:EXP], float(SLOT_TILES)))
                link(V.tensor_tensor(hot_s[:], spread(K["iota_s"], 2, EXP), spread(first[:], 1, SLOT_TILES), ALU.is_ge))
                link(V.tensor_tensor(hot_t[:], spread(K["iota_s"], 2, EXP), spread(last[:], 1, SLOT_TILES), ALU.is_lt))
                link(V.tensor_tensor(hot_s[:], hot_s[:], hot_t[:], ALU.mult))
                link(V.tensor_tensor(hot_t[:], hot_s[:], spread(K["iota_e"], 1, SLOT_TILES), ALU.mult))
                link(V.reduce_sum(who_f[:], hot_t[:], AX.X))
                V.tensor_copy(who[:], who_f[:]).then_inc(who_ready, 1)

            def s_mul(i):
                f, h = i // 2, i % 2
                n = SHC[f][1]
                dve.wait_ge(s_silu_ready, i + 1)
                if n == P:
                    V.tensor_tensor(s_g[:, i % 3, :], s_g[:, i % 3, :], bank[(7, 1)[h]][:, :], ALU.mult).then_inc(s_act_ready, 1)
                else:
                    V.tensor_tensor(s_g[0:64, i % 3, :], s_g[64:128, i % 3, :], bank[(6, 0)[h]][64:128, :],
                                    ALU.mult).then_inc(s_act_ready, 1)

            def s_low(i):
                f, h = i // 2, i % 2
                n = SHC[f][1]
                dve.wait_ge(s_act_hi, i + 1)
                V.tensor_tensor(s_act_l[0:n, f % 2, half(h)], s_g[0:n, i % 3, :],
                                s_act_h[0:n, f % 2, half(h)].bitcast(F32), ALU.subtract).then_inc(s_act_lo, 1)

            def s_gu_low(f):
                r, m = f % 2, 2 if SHC[f][1] == P else 1
                dve.wait_ge(sgu_hi, f + 1)
                V.tensor_tensor(sgu_l[:, r, 0:m], sgu[:, r, 0:m], sgu_h[:, r, 0:m].bitcast(F32),
                                ALU.subtract).then_inc(sgu_lo_dve, 1)

            def s_dn_low(f):
                n = SHC[f][1]
                dve.wait_ge(sdn_hi, f - 2)
                V.tensor_tensor(sdn_l[0:n, f % 4], sdn[0:n, f % 4], sdn_h[0:n, f % 4].bitcast(F32),
                                ALU.subtract).then_inc(sdn_lo_dve, 1)

            s_mul(0)
            link(V.reduce_sum(lgm[:, 0, :], top_v[:, :, 0:TOPK], AX.X))
            link(V.tensor_scalar(lgm[:, 1, :], lgm[:, 0, :], 1e-9, None, ALU.max))
            link(V.reciprocal(lgm[:, 2, :], lgm[:, 1, :]))
            link(V.tensor_tensor(wts[:], top_v[:, :, 0:TOPK], spread(lgm[:, 2, :], 2, TOPK), ALU.mult))
            dve.wait_ge(h1_ready, 4)
            link(V.tensor_tensor(prod[:], hot[:], spread(wts[:], 3, EXP), ALU.mult))
            link(V.tensor_reduce(rows[:, :, D:D + EXP], prod[:].rearrange("p t k e -> p t e k"), AX.X, ALU.add))
            s_mul(1)
            s_low(0)
            link(V.tensor_tensor(prod[:], hot[:], spread(K["dest"].rearrange("p (t k) -> p t k", k=TOPK), 3, EXP), ALU.mult))
            link(V.tensor_reduce(rows[:, :, D + EXP:ROW], prod[:].rearrange("p t k e -> p t e k"), AX.X, ALU.add))
            s_low(1)
            for i in range(2, 2 * len(SHC)):
                f = i // 2
                if i == 3:
                    find_slots()
                if i == 2 * len(SHC) - 2:
                    dve.wait_ge(sdn_f, f - 1)
                    V.memset(s_act_h[64:128, f % 2, :].bitcast(F32), 0.0).then_inc(s_zero, 1)
                    V.memset(s_act_l[64:128, f % 2, :].bitcast(F32), 0.0).then_inc(s_zero, 1)
                s_mul(i)
                s_low(i)
                if i % 2 == 0 and i < 2 * len(SHC) - 2:
                    s_gu_low(f + 1)
                if i in (8, 10):
                    s_dn_low(f)
                if i == 5:
                    find_experts()
            dve.wait_ge(sg_ready, 1)
            for i in range(TILES):
                if i % 2 == 0:
                    dve.wait_ge(sdn_mm, i // 2 + 1)
                V.scalar_tensor_tensor(res[:, i], bank[2 + i // 2][:, D * (i % 2):D * (i % 2) + D], sgate[:, i:i + 1],
                                       res[:, i], ALU.mult, ALU.add).then_inc(shared_added, 1)

            def mul(s, q):
                dve.wait_ge(r_sil, s + 1)
                V.tensor_tensor(act[:, q], sil[:, q], bank[q][:, IM:2 * IM], ALU.mult).then_inc(r_act, 1)

            def keep_actT(s, q):
                dve.wait_ge(r_ta, s + 1)
                V.tensor_copy(actT[:, q], bank[4 + q][0:IH, 0:2 * P].rearrange("p (k n) -> p k n", k=2)).then_inc(r_actT, 1)

            def pick_row(s, r, again):
                dve.wait_ge(r_loaded[r], ring_count(s, r))
                V.tensor_tensor(pick[:, r], slot_rows[:, r, D:ROW].rearrange("p (a e) -> p a e", a=2),
                                spread(hot_s[:, bass.ds(s, 1), :].rearrange("p s e -> p (s e)"), 1, 2), ALU.mult).then_inc(r_pick, 1)
                if again:
                    dve.wait_ge(r_sent[r], ring_count(s, r) - 16)
                dve.wait_ge(r_pick, 2 * s + 1)
                V.reduce_sum(wd[:, r, :], pick[:, r], AX.X).then_inc(r_pick, 1)
                dve.wait_ge(r_pick, 2 * s + 2)
                V.tensor_copy(dest[:, r:r + 1], wd[:, r, 1:2]).then_inc(r_wd, 1)

            for s in range(PIPE0):
                mul(s, s % 2)
                if s:
                    keep_actT(s - 1, (s - 1) % 2)
                pick_row(s, s % RING, False)

            def vstep(s, j, again):
                q = (PIPE0 + j) % 2
                dve.wait_ge(r_ta, s - 1)
                mul(s, q)
                if again:
                    dve.wait_ge(r_dn, s - 2)
                keep_actT(s - 1, 1 - q)
                pick_row(s, (PIPE0 + j) % RING, again)

            for j in range(RING):
                vstep(PIPE0 + j, j, j >= 2)
            with dve.Fori(PIPE0 + RING, SLOT_TILES - RING, RING) as i:
                for j in range(RING):
                    vstep(i + j, j, True)
            s = SLOT_TILES - 1
            vstep(s, s - PIPE0, True)
            dve.wait_ge(r_dn, s - 1)
            keep_actT(s, s % 2)

            for i in range(TILES):
                dve.wait_ge(yk_loaded[i // 2], 16)
                link(V.tensor_tensor(ysum[:, i], yk[:, i, 0:2 * D], yk[:, i, 2 * D:4 * D], ALU.add))
                link(V.tensor_tensor(ysum[:, i, 0:D], ysum[:, i, 0:D], ysum[:, i, D:2 * D], ALU.add))
                V.tensor_tensor(res[:, i], ysum[:, i, 0:D], res[:, i], ALU.add).then_inc(out_ready, 1)

        @block.tensor
        def _(pe):
            MM = nc.tensor.matmul
            TR = nc.tensor.transpose
            I = K["ident"]

            def product(out, pairs, start=True, stop=True, **kw):
                parts = [p for (ah, al, bh, bl) in pairs for p in ((ah, bh), (ah, bl), (al, bh))]
                for j, (a_, b_) in enumerate(parts):
                    ins = MM(out, a_, b_, start=start and j == 0, stop=stop and j == len(parts) - 1, **kw)
                return ins

            pe.wait_ge(ld_const, 16)
            for i in range(TILES):
                pe.wait_ge(wbd_ready, i + 1)
                pe.wait_ge(ld_x[i // 4], 16)
                MM(bank[i // 2][:, D * (i % 2):D * (i % 2) + D], wbd[:, i].rearrange("p b d -> p (b d)"), res[:, i],
                   start=True, stop=True).then_inc(hid_ready, 1)
            for i in range(TILES):
                pe.wait_ge(hn_ready, i + 1)
                for k in range(KC):
                    ins = TR(bank[4 + 2 * (i // 4) + k][:, P * (i % 4):P * (i % 4) + P], hnorm[:, i, P * k:P * k + P], I)
                ins.then_inc(hnT_ready, 1)

            def hT_half(h):
                return [(hT_h[:, k, half(h)], hT_l[:, k, half(h)]) for k in range(KC)]

            def hT_tile(i):
                return [(hT_h[:, k, P * i:P * i + P], hT_l[:, k, P * i:P * i + P]) for k in range(KC)]

            def qkv(h):
                pe.wait_ge(hT_hi, 2 * h + 2)
                pe.wait_ge(hT_lo, 2 * h + 2)
                for m, b0, kept, done in ((1, 2, k_kept, k_mm), (0, 0, q_kept, q_mm)):
                    for c in range(KC):
                        if h:
                            pe.wait_ge(kept, c + 1)
                        at = slice(P * c, P * c + P)
                        product(bank[b0 + c][:, :], [(wqkv_h[:, m, k, at], wqkv_l[:, m, k, at]) + hT_half(h)[k]
                                                     for k in range(KC)]).then_inc(done, 1)
                for g in range(2 * h, 2 * h + 2):
                    if g >= 2:
                        pe.wait_ge(v_kept, g - 1)
                    for tt in range(2):
                        ins = product(bank[4 + g % 2][:, D * tt:D * tt + D],
                                      [hT_tile(2 * g + tt)[k] + (wqkv_h[:, 2, k, :], wqkv_l[:, 2, k, :]) for k in range(KC)])
                    ins.then_inc(v_mm, 1)

            pe.wait_ge(wqkv_lo, 2)
            qkv(0)
            qkv(1)
            pe.wait_ge(ld_small, 48)
            pe.wait_ge(hT_lo, 4)
            for c in range(KC):
                for k in range(KC):
                    ins = MM(bank[6][:, RANK * c:RANK * c + RANK], wo[:, k, P * c:P * c + P], a_raw[:, k, :],
                             start=(k == 0), stop=(k == KC - 1))
            ins.then_inc(woa_mm, 1)

            def up_unit(i):
                if i == 0:
                    pe.wait_ge(wu_lo, 2)
                    pe.wait_ge(woa_ready, 1)
                if i >= 2:
                    pe.wait_ge(up_ready, i - 1)
                f, h = i // 2, i % 2
                at = slice(P * f, P * f + P)
                product(bank[6 + i % 2][:, :], [(wu_h[:, k, at], wu_l[:, k, at]) + hT_half(h)[k]
                                                for k in range(KC)]).then_inc(up_mm, 1)

            def scores(u):
                if u == 0:
                    pe.wait_ge(bf_ready, 4)
                    pe.wait_ge(q_kept, 4)
                    pe.wait_ge(k_kept, 4)
                if u % 2 == 0:
                    pe.wait_ge(kx_act, 2 * (u // 2) + 2)
                    pe.wait_ge(kx_dve, 2 * (u // 2) + 2)
                if u >= 4:
                    pe.wait_ge(shifted, u - 3)
                b_ = bank[u % 4]
                MM(b_[:, :], ident_b[:], spread(causal_b[:], 1, HEADS), start=True, stop=False, skip_group_check=True)
                for c in range(KC):
                    for b4 in range(4):
                        ins = MM(b_[SEQ * b4:SEQ * b4 + SEQ, 256 * c:256 * c + 256],
                                 qT[:, c, P * u + SEQ * b4:P * u + SEQ * b4 + SEQ],
                                 kx[:, u // 2 % 2, c, 4 * (u % 2) + b4].rearrange("p e k -> p (e k)"),
                                 start=False, stop=True, skip_group_check=True)
                ins.then_inc(scored, 1)

            def pv(u):
                pe.wait_ge(exd_act, u + 1)
                pe.wait_ge(exd_dve, u + 1)
                pe.wait_ge(v_kept, 4) if u < 2 else pe.wait_ge(attn_ready, u - 1)
                for c in range(KC):
                    for j in range(4):
                        ins = MM(bank[4 + u % 2][SEQ * j:SEQ * j + SEQ, 256 * c:256 * c + 256],
                                 v_sb[:, u, P * c + SEQ * j:P * c + SEQ * j + SEQ],
                                 exd[:, u % 2, 8 * c + 2 * j:8 * c + 2 * j + 2, :].rearrange("p e q -> p (e q)"),
                                 start=True, stop=True)
                ins.then_inc(pv_ready, 1)

            scores(0)
            for u in range(TILES):
                if u + 1 < TILES:
                    scores(u + 1)
                up_unit(2 * u)
                if u >= 2:
                    pv(u - 2)
                up_unit(2 * u + 1)
            pe.wait_ge(ab_hi, 2)
            pe.wait_ge(ab_lo, 2)
            pe.wait_ge(shifted, 6)
            for h in range(2):
                product(bank[h][:, :], [(a_h[:, k, :], a_l[:, k, :]) + hT_half(h)[k] for k in range(KC)]).then_inc(ha_mm, 1)

            def gate_base(i):
                if i == 0:
                    pe.wait_ge(wg_lo, 2)
                pe.wait_ge(up_ready, 2 * FC) if i < 2 else pe.wait_ge(silu_ready, i - 1)
                f, h = i // 2, i % 2
                at = slice(P * f, P * f + P)
                product(bank[6 + i % 2][:, :], [(wg_h[:, k, at], wg_l[:, k, at]) + hT_half(h)[k] for k in range(KC)],
                        stop=False)

            pv(TILES - 2)
            gate_base(0)
            pv(TILES - 1)
            gate_base(1)
            pe.wait_ge(attn_ready, TILES)
            for k in range(KC):
                for h in range(2):
                    ins = MM(bank[4 + h][SEQ * h:SEQ * h + RANK, :], woa[:, k, :], attnT[:, k, half(h)],
                             start=(k == 0), stop=(k == KC - 1))
                    if k == KC - 1:
                        ins.then_inc(mod_mm, 1)

            def gate_unit(i):
                gate_base(i)
                gate_mod(i)

            def gate_mod(i):
                f, h = i // 2, i % 2
                at = slice(P * f, P * f + P)
                if i < 2:
                    pe.wait_ge(ab_lo, 3)
                    pe.wait_ge(m_hi, 2 * h + 2)
                    pe.wait_ge(m_lo, h + 1)
                MM(bank[6 + i % 2][:, :], b_stack[:, at], m_stack[:, half(h)], start=False, stop=True).then_inc(gate_mm, 1)

            def down(f):
                if f % 2 == 0:
                    pe.wait_ge(wd_lo, f // 2 + 1)
                pe.wait_ge(act_lo, 2 * f + 2)
                for i in range(TILES):
                    at = slice(P * i, P * i + P)
                    ins = product(bank[i // 2][:, D * (i % 2):D * (i % 2) + D],
                                  [(act_h[:, f, at], act_l[:, f % 2, at], wd_h[:, f, :], wd_l[:, f, :])],
                                  start=(f == 0 and i % 2 == 0), stop=(f == FC - 1), skip_group_check=True)
                    if f == FC - 1 and i % 2:
                        ins.then_inc(down_mm, 1)
                if f < FC - 1:
                    ins.then_inc(down_f, 1)

            gate_mod(0), gate_mod(1)
            for f in range(FC):
                if f + 1 < FC:
                    gate_unit(2 * f + 2), gate_unit(2 * f + 3)
                down(f)

            for i in range(TILES):
                pe.wait_ge(x1_ready, i // 2 + 1)
                if i == 0:
                    pe.wait_ge(th_ready, 2)
                if i == 4:
                    pe.wait_ge(silu_ready, 2 * FC)
                for k in range(KC):
                    ins = TR(bank[4 + 2 * (i // 4) + k][:, P * (i % 4):P * (i % 4) + P], res[:, i, P * k:P * k + P], I)
                ins.then_inc(x1T_mm, 1)
            pe.wait_ge(l1_lo, 4)
            for h in range(2):
                pe.wait_ge(x1T_lo, 2 * h + 2)
                product(bank[h][:, :], [(aT_h[:, k, :], aT_l[:, k, :], x1T_h[:, k, half(h)], x1T_l[:, k, half(h)])
                                        for k in range(KC)]).then_inc(xa_mm, 1)
            for i in range(TILES):
                at = slice(P * i, P * i + P)
                product(bank[2 + i // 2][:, D * (i % 2):D * (i % 2) + D],
                        [(x1T_h[:, k, at], x1T_l[:, k, at], w1_h[:, k, :], w1_l[:, k, :]) for k in range(KC)],
                        start=(i % 2 == 0), stop=False, skip_group_check=True)
            for i in range(TILES):
                if i % 4 == 0:
                    pe.wait_ge(xam_lo, i // 4 + 1)
                at = slice(P * i, P * i + P)
                ins = product(bank[2 + i // 2][:, D * (i % 2):D * (i % 2) + D],
                              [(xam_h[:, at], xam_l[:, at], bm_h[:, :], bm_l[:, :])], start=False, skip_group_check=True)
                if i % 2:
                    ins.then_inc(h1_mm, 1)
            for i in range(TILES):
                pe.wait_ge(h1_ready, i // 2 + 1)
                for k in range(KC):
                    b_ = bank[((6, 7), (0, 1))[i // 4][k]]
                    ins = TR(b_[:, P * (i % 4):P * (i % 4) + P], rows[:, i, P * k:P * k + P], I)
                ins.then_inc(h1T_mm, 1)
            for h in range(2):
                pe.wait_ge(h1T_lo, 2 * h + 2)
                product(bank[2 + h][:, :], [(rw_h[:, k, :], rw_l[:, k, :]) + hT_half(h)[k] for k in range(KC)]).then_inc(lgT_mm, 1)
            for i in range(TILES):
                pe.wait_ge(lgT_kept, i // 4 + 1)
                ins = TR(bank[4][:, SEQ * i:SEQ * i + SEQ], lgT[:, P * i:P * i + P], I[0:SEQ, 0:SEQ])
            ins.then_inc(lg_mm, 1)

            def ranks():
                pe.wait_ge(member_ready, 1)
                mb = member[:].rearrange("p t e -> p (t e)")
                MM(bank[5][:, 0:P], before_b[:], mb, start=True, stop=False, skip_group_check=True)
                for d in range(1, TILES):
                    MM(bank[5][:, EXP * d:P], ones_b[:], mb[:, 0:P - EXP * d], start=False, stop=False,
                       skip_group_check=True)
                for i in range(TILES):
                    ins = MM(bank[5][:, P:P + EXP], ones_b[:], mb[:, EXP * i:EXP * i + EXP], start=False,
                             stop=(i == TILES - 1), skip_group_check=True)
                ins.then_inc(rank_mm, 1)

            def shared_gu(f):
                r = f % 2
                if f < 2:
                    pe.wait_ge(sh_lo_pool, f + 1)
                else:
                    pe.wait_ge(sgu_lo_dve, f - 1)
                for h in range(2):
                    i = 2 * f + h
                    if i >= 2:
                        pe.wait_ge(s_act_ready, i - 1)
                    for m in range(2 if SHC[f][1] == P else 1):
                        ins = product(bank[((6, 7), (0, 1))[h][m]][:, :],
                                      [(sgu_h[:, r, m, k, :], sgu_l[:, r, m, k, :]) + hT_half(h)[k] for k in range(KC)])
                    ins.then_inc(sgu_mm, 1)

            def shared_down(f):
                last_f = f == len(SHC) - 1
                pe.wait_ge(s_act_lo, 2 * f + 2)
                if f == 0:
                    pe.wait_ge(sh_lo_pool, 3)
                    pe.wait_ge(rank_read, 1)
                if f >= 4:
                    pe.wait_ge(sdn_lo_dve, f - 3)
                if last_f:
                    pe.wait_ge(s_zero, 2)
                for i in range(TILES):
                    at = slice(P * i, P * i + P)
                    ins = product(bank[2 + i // 2][:, D * (i % 2):D * (i % 2) + D],
                                  [(s_act_h[:, f % 2, at], s_act_l[:, f % 2, at], sdn_h[:, f % 4, :], sdn_l[:, f % 4, :])],
                                  start=(f == 0 and i % 2 == 0), stop=last_f, skip_group_check=True)
                    if last_f and i % 2:
                        ins.then_inc(sdn_mm, 1)
                if not last_f:
                    ins.then_inc(sdn_f, 1)

            for f in range(len(SHC)):
                if f == len(SHC) - 1:
                    shared_down(f - 2)
                shared_gu(f)
                if f == 0:
                    ranks()
                if 2 <= f < len(SHC) - 1:
                    shared_down(f - 2)
            shared_down(len(SHC) - 2)
            shared_down(len(SHC) - 1)

            def turn_in(s, q, r, again):
                pe.wait_ge(r_loaded[r], ring_count(s, r))
                if again:
                    pe.wait_ge(r_hT, s - 1)
                for k in range(KC):
                    ins = TR(bank[2 + q][:, P * k:P * k + P], slot_rows[:, r, P * k:P * k + P], I)
                ins.then_inc(r_in, 1)

            def experts_of(s, n):
                return nc.values_load_multi_w_load_instructions(
                    who[0:1, bass.ds(s, n)], engines=[mybir.EngineType.PE], min_val=0, max_val=EXP - 1,
                    skip_runtime_bounds_check_because="one expert's number, picked by a one-hot row of hot_s")[1]

            def gate_up(s, e, q, again):
                pe.wait_ge(r_hT, s + 1)
                if again:
                    pe.wait_ge(r_act, s - 1)
                w = e_gu[:].rearrange("p e k n -> p (e k) n")
                for k in range(KC):
                    ins = MM(bank[q][:, 0:2 * IM], hT[:, q, k, :],
                             w[:, bass.ds(e * KC + k, 1), :].rearrange("p a n -> p (a n)"),
                             start=(k == 0), stop=(k == KC - 1))
                ins.then_inc(r_gu, 1)

            def turn_act(s, q, again):
                pe.wait_ge(r_act, s + 1)
                if again:
                    pe.wait_ge(r_actT, s - 1)
                for k in range(2):
                    ins = TR(bank[4 + q][0:IH, P * k:P * k + P], act[:, q, IH * k:IH * k + IH], I)
                ins.then_inc(r_ta, 1)

            def down_e(s, e, q, again):
                pe.wait_ge(r_actT, s + 1)
                if again:
                    pe.wait_ge(r_y, s - 1)
                w = e_dn[:].rearrange("p e k n -> p (e k) n")
                for k in range(2):
                    ins = MM(bank[6 + q][:, 0:D], actT[:, q, k, :],
                             w[:, bass.ds(e * 2 + k, 1), :].rearrange("p a n -> p (a n)"),
                             start=(k == 0), stop=(k == 1))
                ins.then_inc(r_dn, 1)

            pe.wait_ge(who_ready, 1)
            pe.wait_ge(ld_exp, 32 * EXP)
            pe.wait_ge(shared_added, 4)
            turn_in(0, 0, 0, False)
            experts = experts_of(0, RING + PIPE0)
            gate_up(0, experts[0], 0, False)
            turn_in(1, 1, 1, False)
            gate_up(1, experts[1], 1, False)
            pe.wait_ge(shared_added, 8)
            turn_act(0, 0, False)
            turn_in(2, 0, 2, True)

            def pstep(s, experts, j, again):
                q = (PIPE0 + j) % 2
                gate_up(s, experts[j + PIPE0], q, True)
                turn_act(s - 1, 1 - q, again)
                turn_in(s + 1, 1 - q, (PIPE0 + j + 1) % RING, True)
                down_e(s - 2, experts[j], q, again)

            for j in range(RING):
                pstep(PIPE0 + j, experts, j, j >= 2)
            with pe.Fori(PIPE0 + RING, SLOT_TILES - RING, RING) as i:
                experts = experts_of(i - 2, RING + PIPE0)
                for j in range(RING):
                    pstep(i + j, experts, j, True)
            s = SLOT_TILES - 1
            experts = experts_of(s - 2, 3)
            gate_up(s, experts[2], s % 2, True)
            turn_act(s - 1, (s - 1) % 2, True)
            down_e(s - 2, experts[0], s % 2, True)
            turn_act(s, s % 2, True)
            down_e(s - 1, experts[1], (s - 1) % 2, True)
            down_e(s, experts[2], s % 2, True)


def kernel(**inputs):
    import numpy as _np
    import concourse.bacc as _bacc
    from concourse import mybir as _mybir
    from concourse.bass_utils import run_bass_kernel_spmd as _run

    a = {k: _np.asarray(v) for k, v in inputs.items()}
    flip = lambda w: _np.ascontiguousarray(w.T)
    arrays = {
        "x": a["x"].reshape(TOK, D), "cond": flip(a["itok_B_1_198"].reshape(TILES, 4)), "adapter": a["itok_B_0_6"],
        "cond_w": a["L0_cond_weights"], 
        "norms": flip(_np.concatenate([a["L0_ffn_ln1_w"], a["L0_ffn_ln2_w"]]).reshape(2 * KC, P)),
        "WqT": flip(a["L0_ffn_Wq"]), "WkT": flip(a["L0_ffn_Wk"]), "WvT": flip(a["L0_ffn_Wv"]),
        "Wo": a["L0_ffn_Wo"], "A": a["L0_ffn_A"], "B": a["L0_ffn_B"],
        "WinT": flip(a["L0_ffn_W_in_base"]), "WupT": flip(a["L0_ffn_W_up_base"]), "WdT": flip(a["L0_ffn_W_down"]),
        "W1T": flip(a["L1_cond_W"]), "AT": flip(a["L1_cond_A"].reshape(P, D)),
        "BmT": _np.ascontiguousarray(a["L1_cond_Bm"].transpose(0, 2, 1)).reshape(P, D),
        "scale": a["L1_cond_scalings"],
        "router": _np.concatenate([flip(a["L1_ffn_router_w"]), a["L1_ffn_sh_gate_w"]], axis=1),
        "e_gu": _np.concatenate([a["L1_ffn_w_gate"], a["L1_ffn_w_up"]], axis=2), "e_dn": a["L1_ffn_w_down"],
        "s_gu": _np.concatenate([a["L1_ffn_sh_gate"], a["L1_ffn_sh_up"]], axis=1), "s_dn": a["L1_ffn_sh_down"],
        "consts": constants(),
    }
    arrays = {f"in_{k}": _np.ascontiguousarray(v) for k, v in arrays.items()}
    nc = _bacc.Bacc("TRN2", target_bir_lowering=False, num_devices=1)
    t = {k[3:]: nc.dram_tensor(k, v.shape, _mybir.dt.from_np(v.dtype), kind="ExternalInput").ap()
         for k, v in arrays.items()}
    t["out"] = nc.dram_tensor("out", (TOK, D), F32, kind="ExternalOutput").ap()
    t["cond_b"] = bass.AP(t["cond"].tensor, 0, [[TILES, 4], [0, SEQ], [1, TILES]])
    t["adapter_b"] = bass.AP(t["adapter"].tensor, 0, [[0, P], [1, BATCH]])
    t["scale_p"] = bass.AP(t["scale"].tensor, 0, [[1, ADAPT], [0, RANK], [1, 1]])
    program(nc, t)
    r = _run(nc, [arrays], core_ids=[0])
    return r.results[0]["out"].reshape(BATCH, SEQ, D)
```

```python
from contextlib import ExitStack

import numpy as np

import concourse.bass as bass
from concourse import mybir

F32 = mybir.dt.float32
F32R = mybir.dt.float32r
BF16 = mybir.dt.bfloat16
I32 = mybir.dt.int32
U32 = mybir.dt.uint32
ALU = mybir.AluOpType
ACT = mybir.ActivationFunctionType
AX = mybir.AxisListType

P = 128
BATCH, SEQ, D = 32, 32, 256
TOK = BATCH * SEQ
TILES = TOK // P
HALF = TOK // 2
KC = D // P
HEADS, HD = 16, 16
FF = 1024
FC = FF // P
RANK = 16
COND = 200
EPS = 1e-6
NEG = -3.0e38
ADAPT = 8
EXP, TOPK = 16, 4
IM = 176
IH = IM // 2
SH = 704
SHC = [(f * P, min(P, SH - f * P)) for f in range((SH + P - 1) // P)]
SLOT_TILES = (TOK * TOPK + EXP * (P - 1)) // P
SLOTS = SLOT_TILES * P
ROW = D + 2 * EXP
NOWHERE = 1.0e6
PIPE0, RING = 2, 4
BACK = ((0, 1), (1, 3), (3, 5), (5, 7), (7, 8))
BACK_POOL = (2, 4, 6)
STEADY = range(PIPE0, SLOT_TILES - 1)
assert len(STEADY) % RING == 0 and PIPE0 % RING == 2

CONSTS = {}


def const_columns():
    at = 0
    for name, n in (("ident", P), ("batch_of", 4), ("head_of", 8), ("pair_of", 2), ("causal", 32), ("adapter_of", 1),
                    ("before", P), ("iota_e", EXP), ("tile_edge", TILES),
                    ("lower_e", EXP * EXP), ("iota_s", SLOT_TILES), ("dest", TILES * TOPK)):
        CONSTS[name] = (at, n)
        at += n
    return at


NCONST = const_columns()


def constants():
    p = np.arange(P)
    c = np.zeros((P, NCONST), np.float32)

    def put(name, a):
        at, n = CONSTS[name]
        c[:, at:at + n] = a

    put("ident", np.eye(P))
    put("batch_of", p[:, None] // SEQ == np.arange(4)[None])
    put("head_of", p[:, None] // HD == np.arange(8)[None])
    put("pair_of", p[:, None] // HD % 2 == np.arange(2)[None])
    put("causal", np.where(np.arange(SEQ)[None] <= p[:, None] % SEQ, 0.0, NEG))
    put("adapter_of", p[:, None] // RANK)
    put("before", p[:, None] < p[None])
    put("iota_e", np.arange(EXP)[None])
    put("tile_edge", P * np.arange(TILES)[None])
    put("lower_e", (np.arange(EXP)[None] < np.arange(EXP)[:, None]).reshape(1, -1))
    put("iota_s", np.arange(SLOT_TILES)[None])
    n = np.arange(TILES)[None, :, None] * P + p[:, None, None]
    put("dest", (TOPK * n + np.arange(TOPK)[None, None]).reshape(P, -1))
    return c


def spread(ap, axis, n):
    v = ap.unsqueeze(axis)
    shape = list(v.shape)
    shape[axis] = n
    return v.broadcast_to(shape)


def program(nc, t):
    ctx = ExitStack()
    with ctx:
        top = [0]
        base = (nc.sbuf_base + 63) // 64 * 64
        nbytes = {F32: 4, F32R: 4, BF16: 2, I32: 4, U32: 4}

        def sb(name, shape, dt=F32, at=None):
            size = int(np.prod(shape[1:])) * nbytes[dt]
            size = (size + 31) // 32 * 32
            if at is None:
                at = top[0]
                top[0] += size
            assert base + at + size <= nc.sbuf_usable_end, name
            h = nc.alloc_sbuf_tensor_at(name, shape, dt, offset=base + at)
            h_at[name] = (at, size)
            return h

        h_at = {}

        def after(name):
            return h_at[name][0] + h_at[name][1]

        def sem(name):
            return ctx.enter_context(nc.semaphore(name))

        consts = sb("consts", [P, NCONST])
        K = {n: consts[:, a:a + w] for n, (a, w) in CONSTS.items()}
        ident_b = sb("ident_b", [P, P], BF16)
        causal_b = sb("causal_b", [P, SEQ], BF16)
        before_b = sb("before_b", [P, P], BF16)
        ones_b = sb("ones_b", [P, P], BF16)
        cond_b = sb("cond_b", [P, TILES], I32)
        cond_rows = sb("cond_rows", [P, TILES], I32)
        pos_of = sb("pos_of", [P, 1])
        norm_w = sb("norm_w", [P, 2, KC])
        ssq = sb("ssq", [P, TILES])
        msq = sb("msq", [P, TILES])
        rms = sb("rms", [P, TILES])
        rstd = sb("rstd", [P, TILES])
        warm = sb("warm", [P, 3])
        peak = sb("peak", [P, TILES, HEADS])
        total = sb("total", [P, TILES, HEADS])
        rtotal = sb("rtotal", [P, TILES, HEADS])
        adapter_b = sb("adapter_b", [P, BATCH], I32)
        scale_p = sb("scale_p", [P, 1])
        adapter_sel = sb("adapter_sel", [P, BATCH])
        res = sb("res", [P, TILES, D])
        hT_h = sb("hT_h", [P, KC, TOK], F32R)
        hT_l = sb("hT_l", [P, KC, TOK], F32R)
        wqkv_h = sb("wqkv_h", [P, 3, KC, D], F32R)
        wqkv_l = sb("wqkv_l", [P, 3, KC, D], F32R)
        wqkv = sb("wqkv", [P, 3, KC, D], at=h_at["wqkv_l"][0])
        wg_h = sb("wg_h", [P, KC, FF], F32R)
        wg_l = sb("wg_l", [P, KC, FF], F32R)
        wg = sb("wg", [P, KC, FF], at=h_at["wg_l"][0])
        wd_h = sb("wd_h", [P, FC, D], F32R)
        wd_l = sb("wd_l", [P, FC, D], F32R)
        wd_ = sb("wd_", [P, FC, D], at=h_at["wd_l"][0])
        wu_h = sb("wu_h", [P, KC, FF], F32R)
        wu_l = sb("wu_l", [P, KC, FF], F32R)
        wu = sb("wu", [P, KC, FF], at=h_at["wu_l"][0])
        wo = sb("wo", [P, KC, D])
        a_raw = sb("a_raw", [P, KC, RANK])
        a_h = sb("a_h", [P, KC, P], F32R)
        a_l = sb("a_l", [P, KC, P], F32R)
        woa = sb("woa", [P, KC, RANK])
        b_stack = sb("b_stack", [P, FF], F32R)
        up = sb("up", [P, FC, TOK])
        act_h = sb("act_h", [P, FC, TOK], F32R, at=h_at["up"][0])
        kT = sb("kT", [P, KC, TOK], at=h_at["up"][0] + 3 * FC // 4 * TOK * 4)
        wgath = sb("wgath", [P, TILES, SEQ], at=h_at["up"][0])
        wbd = sb("wbd", [P, TILES, 4, SEQ], at=after("wgath"))
        hnorm = sb("hnorm", [P, TILES, D], at=after("wbd"))
        zone_a = top[0]
        qT = sb("qT", [P, KC, TOK])
        v_sb = sb("v_sb", [P, TILES, D])
        kx = sb("kx", [P, 2, KC, 8, 8, SEQ])
        hn = sb("hn", [P, TILES, D], at=h_at["kx"][0])
        zone_b = top[0]
        exd = sb("exd", [P, 2, HEADS, P])
        ex = sb("ex", [P, 3, 512])
        exT = sb("exT", [P, 2, 512])
        zone_end = top[0]
        b_raw = sb("b_raw", [RANK, FF], at=h_at["up"][0] + FC // 2 * TOK * 4)
        assert after("hnorm") <= h_at["b_raw"][0]
        attnT = sb("attnT", [P, KC, TOK], at=h_at["wqkv_h"][0])
        act_l = sb("act_l", [P, 2, TOK], F32R, at=zone_b)
        g_sb = sb("g_sb", [P, 3, 512], at=after("act_l"))
        m_stack = sb("m_stack", [P, TOK], F32R, at=after("g_sb"))
        thm = sb("thm", [RANK, TOK], at=after("m_stack"))
        m_sb = sb("m_sb", [RANK, TOK], at=after("thm"))
        assert after("m_sb") <= zone_end
        e_gu = sb("e_gu", [P, EXP, KC, 2 * IM], at=zone_a)
        assert after("e_gu") <= zone_b
        e_gu_l = sb("e_gu_l", [P, EXP, KC, 2 * IM], F32R, at=h_at["e_gu"][0])
        e_gu_h = sb("e_gu_h", [P, EXP, KC, 2 * IM], F32R, at=h_at["wqkv_h"][0])
        assert after("e_gu_h") <= after("wd_l")
        w1_h = sb("w1_h", [P, KC, D], F32R, at=h_at["wqkv_h"][0])
        w1_l = sb("w1_l", [P, KC, D], F32R, at=after("w1_h"))
        w1 = sb("w1", [P, KC, D], at=h_at["w1_l"][0])
        bm_h = sb("bm_h", [P, D], F32R, at=after("w1_l"))
        bm_l = sb("bm_l", [P, D], F32R, at=after("bm_h"))
        bm = sb("bm", [P, D], at=h_at["bm_l"][0])
        aT_h = sb("aT_h", [P, KC, P], F32R, at=after("bm_l"))
        aT_l = sb("aT_l", [P, KC, P], F32R, at=after("aT_h"))
        aT = sb("aT", [P, KC, P], at=h_at["aT_l"][0])
        rw_h = sb("rw_h", [P, KC, P], F32R, at=after("aT_l"))
        rw_l = sb("rw_l", [P, KC, P], F32R, at=after("rw_h"))
        assert after("rw_l") <= after("wqkv_l")
        rw = sb("rw", [P, KC, EXP + 1])
        sdn_h = sb("sdn_h", [P, 4, D], F32R, at=h_at["wu_h"][0])
        sdn_l = sb("sdn_l", [P, 4, D], F32R, at=after("sdn_h"))
        sdn = sb("sdn", [P, 4, D], at=h_at["sdn_l"][0])
        sgu_h = sb("sgu_h", [P, 2, 2, KC, P], F32R, at=after("sdn_l"))
        sgu_l = sb("sgu_l", [P, 2, 2, KC, P], F32R, at=after("sgu_h"))
        sgu = sb("sgu", [P, 2, 2, KC, P], at=h_at["sgu_l"][0])
        assert after("sgu_l") <= after("wu_l")
        e_dn = [sb("e_dn0", [IH, EXP, D], at=h_at["hT_h"][0]), sb("e_dn1", [IH, EXP, D], at=h_at["sgu_h"][0])]
        assert after("e_dn0") <= after("hT_l") and after("e_dn1") <= after("b_stack")
        x1T_h = sb("x1T_h", [P, KC, TOK], F32R, at=h_at["up"][0])
        x1T_l = sb("x1T_l", [P, KC, TOK], F32R, at=after("x1T_h"))
        xam = sb("xam", [P, TOK], at=after("x1T_l"))
        xam_h = sb("xam_h", [P, TOK], F32R, at=after("xam"))
        xam_l = sb("xam_l", [P, TOK], F32R, at=after("xam_h"))
        s_act_h = sb("s_act_h", [P, 3, TOK], F32R, at=h_at["up"][0])
        s_act_l = sb("s_act_l", [P, 3, TOK], F32R, at=after("s_act_h"))
        s_g = sb("s_g", [P, 3, 512], at=after("s_act_l"))
        lgT = sb("lgT", [SEQ, TOK], at=h_at["s_act_l"][0] + 2 * 4 * TOK)
        assert after("s_g") <= after("up") and after("xam_l") <= after("up")
        rows = sb("rows", [P, TILES, ROW], at=zone_b)
        lgx = sb("lgx", [P, TILES, EXP], at=after("rows"))
        lgm = sb("lgm", [P, 3, TILES], at=after("lgx"))
        top_v = sb("top_v", [P, TILES, 8], at=after("lgm"))
        top_i = sb("top_i", [P, TILES, 8], U32, at=after("top_v"))
        top_f = sb("top_f", [P, TILES, TOPK], at=after("top_i"))
        wts = sb("wts", [P, TILES, TOPK], at=after("top_f"))
        hot = sb("hot", [P, TILES, TOPK, EXP], at=after("wts"))
        prod = sb("prod", [P, TILES, TOPK, EXP], at=after("hot"))
        member = sb("member", [P, TILES, EXP], BF16, at=after("prod"))
        over = sb("over", [P, EXP, TILES], at=after("member"))
        ntile = sb("ntile", [P, EXP], at=after("over"))
        first = sb("first", [P, EXP], at=after("ntile"))
        last = sb("last", [P, EXP], at=after("first"))
        pairs = sb("pairs", [P, EXP, EXP], at=after("last"))
        where = sb("where", [P, TILES, EXP], at=after("pairs"))
        slot_f = sb("slot_f", [P, TILES * TOPK], at=after("where"))
        slot = sb("slot", [P, TILES * TOPK], I32, at=after("slot_f"))
        hot_s = sb("hot_s", [P, SLOT_TILES, EXP], at=after("slot"))
        hot_t = sb("hot_t", [P, SLOT_TILES, EXP], at=after("hot_s"))
        prod_d = sb("prod_d", [P, TILES, TOPK, EXP], at=h_at["hot_t"][0])
        assert after("prod_d") <= after("hot_t")
        who_f = sb("who_f", [P, SLOT_TILES], at=after("hot_t"))
        who = sb("who", [P, SLOT_TILES], I32, at=after("who_f"))
        lg_sb = sb("lg_sb", [P, TILES, SEQ], at=after("who"))
        sgate = sb("sgate", [P, TILES], at=after("lg_sb"))
        assert after("sgate") <= zone_end, (after("sgate"), zone_end)
        fill = sb("fill", [P, ROW])
        slot_rows = sb("slot_rows", [P, RING, ROW], at=after("sgate"))
        e_in_h = sb("e_in_h", [P, 2, KC, P], F32R, at=h_at["up"][0])
        e_in_l = sb("e_in_l", [P, 2, KC, P], F32R, at=after("e_in_h"))
        sil = sb("sil", [P, 2, IM], at=after("e_in_l"))
        act = sb("act", [P, 2, IM], at=after("sil"))
        actT_h = sb("actT_h", [IH, 2, P], F32R, at=after("act"))
        actT_l = sb("actT_l", [IH, 2, P], F32R, at=after("actT_h"))
        actT = sb("actT", [IH, 2, P], at=after("actT_l"))
        y = sb("y", [P, RING, D], at=after("actT"))
        pick = sb("pick", [P, RING, 2, EXP], at=after("y"))
        wd = sb("wd", [P, RING, 2], at=after("pick"))
        dest = sb("dest", [P, RING], I32, at=after("wd"))
        dn_l = sb("dn_l", [IH, EXP, D], F32R, at=h_at["e_dn0"][0])
        dn_h = sb("dn_h", [IH, EXP, D], F32R, at=h_at["up"][0] + FC // 2 * TOK * 4)
        assert after("dest") <= h_at["dn_h"][0] and after("dn_h") <= after("up")
        yk = sb("yk", [P, TILES, TOPK * D], at=zone_a)
        ysum = sb("ysum", [P, TILES, 2 * D], at=h_at["wg_h"][0])
        assert after("yk") <= zone_b
        bank = [ctx.enter_context(nc.psum_tensor(f"bank{i}", [P, 512], F32)) for i in range(8)]

        slots_d = nc.dram_tensor("slots_d", (SLOTS, ROW), F32).ap()
        yk_d = nc.dram_tensor("yk_d", (TOK * TOPK, D), F32).ap()

        ld_const, ld_cond, ld_wqkv, ld_norm, ld_small = map(sem, ("ld_const", "ld_cond", "ld_wqkv", "ld_norm", "ld_small"))
        ld_x = [sem(f"ld_x{h}") for h in range(2)]
        ld_up, ld_gate, ld_down = map(sem, ("ld_up", "ld_gate", "ld_down"))
        ld_l1, ld_exp, ld_adapt = map(sem, ("ld_l1", "ld_exp", "ld_adapt"))
        ld_sgu = [sem(f"ld_sgu{r}") for r in range(2)]
        ld_sdn = [sem(f"ld_sdn{r}") for r in range(2)]
        filled = sem("filled")
        dve_step = sem("dve_step")
        gathered = [sem(f"gathered{i}") for i in range(TILES)]
        yk_loaded = [sem(f"yk_loaded{i}") for i in range(len(BACK))]
        pool_step, out_pool = sem("pool_step"), sem("out_pool")
        wbd_ready, hid_ready, ssq_ready, msq_ready = map(sem, ("wbd_ready", "hid_ready", "ssq_ready", "msq_ready"))
        cond_ready, rms_ready, hn_ready = map(sem, ("cond_ready", "rms_ready", "hn_ready"))
        bf_ready, zero_set, m_zero = sem("bf_ready"), sem("zero_set"), sem("m_zero")
        wqkv_hi, wqkv_lo, wu_hi, wu_lo, wg_scaled, wgd_hi, wgd_lo, ab_hi, ab_lo = map(
            sem, ("wqkv_hi", "wqkv_lo", "wu_hi", "wu_lo", "wg_scaled", "wgd_hi", "wgd_lo", "ab_hi", "ab_lo"))
        l1_hi, l1_lo, egu_hi, egu_lo, sgu_hi, sgu_lo_dve, sdn_hi, sdn_lo_dve, sh_lo_pool = map(
            sem, ("l1_hi", "l1_lo", "egu_hi", "egu_lo", "sgu_hi", "sgu_lo_dve", "sdn_hi", "sdn_lo_dve", "sh_lo_pool"))
        hid_kept, hnT_ready, hT_hi, hT_lo = map(sem, ("hid_kept", "hnT_ready", "hT_hi", "hT_lo"))
        k_mm, q_mm, v_mm, k_kept, q_kept, v_kept = map(sem, ("k_mm", "q_mm", "v_mm", "k_kept", "q_kept", "v_kept"))
        kx_act, kx_dve = sem("kx_act"), sem("kx_dve")
        scored, shifted, exped, summed, normed, exT_ready, exd_act, exd_dve, pv_ready, attn_even, attn_ready = map(
            sem, ("scored", "shifted", "exped", "summed", "normed", "exT_ready", "exd_act", "exd_dve", "pv_ready",
                  "attn_even", "attn_ready"))
        woa_mm, woa_ready, up_mm, up_ready, ha_mm, mod_mm, mod_act, m_ready, m_lo = map(
            sem, ("woa_mm", "woa_ready", "up_mm", "up_ready", "ha_mm", "mod_mm", "mod_act", "m_ready", "m_lo"))
        gate_mm, silu_ready, act_ready, act_hi, act_lo, down_f, down_mm, x1_ready = map(
            sem, ("gate_mm", "silu_ready", "act_ready", "act_hi", "act_lo", "down_f", "down_mm", "x1_ready"))
        x1T_mm, x1T_hi, x1T_lo, xa_mm, xam_ready, xam_hi, xam_lo, h1_mm, h1_ready = map(
            sem, ("x1T_mm", "x1T_hi", "x1T_lo", "xa_mm", "xam_ready", "xam_hi", "xam_lo", "h1_mm", "h1_ready"))
        h1T_mm, h1T_hi, h1T_lo, lgT_mm, lgT_kept, lg_mm, lg_ready = map(
            sem, ("h1T_mm", "h1T_hi", "h1T_lo", "lgT_mm", "lgT_kept", "lg_mm", "lg_ready"))
        lgx_ready, lge_ready, member_ready, rank_mm, rank_read, slot_ready, who_ready, scattered = map(
            sem, ("lgx_ready", "lge_ready", "member_ready", "rank_mm", "rank_read", "slot_ready", "who_ready",
                  "scattered"))
        sgu_mm, s_silu_ready, s_act_ready, s_act_hi, s_act_lo, sdn_f, sdn_mm, shared_added = map(
            sem, ("sgu_mm", "s_silu_ready", "s_act_ready", "s_act_hi", "s_act_lo", "sdn_f", "sdn_mm",
                  "shared_added"))
        r_loaded = [sem(f"r_loaded{i}") for i in range(RING)]
        r_sent = [sem(f"r_sent{i}") for i in range(RING)]
        r_in, r_hi, r_lo, r_gu, r_sil, r_act, r_ta, r_act_hi, r_actT, r_dn, r_wd, r_y, r_pick = map(
            sem, ("r_in", "r_hi", "r_lo", "r_gu", "r_sil", "r_act", "r_ta", "r_act_hi", "r_actT", "r_dn", "r_wd", "r_y", "r_pick"))
        out_ready, stored = sem("out_ready"), sem("stored")

        def ring_count(s, r):
            return 4 * (s - r) + 16

        split_order = [(EXP // 2 + j) % EXP for j in range(EXP)]
        split_high = {4: (0, 2), 5: (2, 5), 6: (5, 7), 7: (7, 8), 8: (8, 12), 9: (12, 14), 10: (14, 16)}
        split_low = {4: (0, 2), 5: (2, 4), 6: (4, 6), 7: (6, 7), 8: (7, 9), 9: (12, 14), 10: (14, 16)}
        split_pool = range(9, 12)

        def back_group(i):
            return next(j for j, (a, b) in enumerate(BACK) if a <= i < b)

        def add_experts(eng, i, link):
            link(eng.tensor_tensor(ysum[:, i], yk[:, i, 0:2 * D], yk[:, i, 2 * D:4 * D], ALU.add))
            link(eng.tensor_tensor(ysum[:, i, 0:D], ysum[:, i, 0:D], ysum[:, i, D:2 * D], ALU.add))
            return eng.tensor_tensor(res[:, i], ysum[:, i, 0:D], res[:, i], ALU.add)

        def qk_bank(h, m):
            return ((0, 2), (2, 6))[h][m]

        def gate_bank(i):
            return (6, 7, 2, 3)[i] if i < 4 else 6 + i % 2

        def half(h):
            return slice(HALF * h, HALF * h + HALF)

        def mask_k(op, done, g, c, heads):
            src = kT[:, c, 2 * P * g:2 * P * g + 2 * P].rearrange("p (b k) -> p b k", k=SEQ)
            for e in heads:
                ins = op(kx[:, g % 2, c, :, e, :], src, K["head_of"][:, e:e + 1])
            ins.then_inc(done, 1)

        def on_diagonal(copy, done, u, b4s):
            for b4 in b4s:
                ins = copy(exd[SEQ * b4:SEQ * b4 + SEQ, u % 2, :, SEQ * b4:SEQ * b4 + SEQ],
                           exT[SEQ * b4:SEQ * b4 + SEQ, u % 2, :].rearrange("p (h q) -> p h q", q=SEQ))
            ins.then_inc(done, 1)

        block = ctx.enter_context(nc.Block())

        @block.sync
        def _(sp):
            def halves(name):
                return t[name].rearrange("(k p) n -> p k n", p=P)

            sp.dma_start(cond_b[:, :], t["cond_b"]).then_inc(ld_cond, 16)
            sp.dma_start(pos_of[:, :], t["pos"]).then_inc(ld_cond, 16)
            sp.dma_start(consts[:, :], t["consts"]).then_inc(ld_const, 16)
            xt = t["x"].rearrange("(t p) d -> p t d", p=P)
            sp.dma_start(res[:, 0:4, :], xt[:, 0:4, :]).then_inc(ld_x[0], 16)
            sp.dma_start(norm_w[:].rearrange("p i k -> p (i k)"), t["norms"]).then_inc(ld_norm, 16)
            sp.dma_start(res[:, 4:8, :], xt[:, 4:8, :]).then_inc(ld_x[1], 16)
            sp.wait_ge(gathered[TILES // 2 - 1], 16)
            for i, n in enumerate(("WqT", "WkT", "WvT")):
                sp.dma_start(wqkv[:, i], halves(n)).then_inc(ld_wqkv, 16)
            sp.wait_ge(gathered[TILES - 1], 16)
            sp.dma_start(wu[:], halves("WupT")).then_inc(ld_up, 16)
            sp.dma_start(wo[:], halves("Wo")).then_inc(ld_small, 16)
            sp.dma_start(a_raw[:], halves("A")).then_inc(ld_small, 16)
            sp.dma_start(b_raw[:], t["B"]).then_inc(ld_small, 16)
            sp.dma_start(wg[:], halves("WinT")).then_inc(ld_gate, 16)
            sp.dma_start(wd_[:], halves("WdT")).then_inc(ld_down, 16)
            sp.dma_start(adapter_b[:], t["adapter_b"]).then_inc(ld_adapt, 16)
            sp.dma_start(scale_p[:], t["scale_p"]).then_inc(ld_adapt, 16)
            sp.dma_start(rw[:], halves("router")).then_inc(ld_adapt, 16)
            sp.wait_ge(zero_set, 6)
            sp.wait_ge(hid_ready, TILES)
            sp.wait_ge(ld_down, 16)
            for s in range(0, SLOT_TILES, 8):
                n = min(8, SLOT_TILES - s)
                sp.dma_start(slots_d[s * P:(s + n) * P, :].rearrange("(s p) c -> p s c", p=P),
                             spread(fill[:], 1, n)).then_inc(filled, 16)

            def load_sgu(f):
                a, n = SHC[f]
                for m in range(2):
                    w = halves("s_gu")[:, :, SH * m + a:SH * m + a + n]
                    dst = sgu[:, f % 2, m, :, 0:n] if n == P else sgu[:, f % 2, 0, :, n * m:n * m + n]
                    sp.dma_start(dst, w).then_inc(ld_sgu[f % 2], 16)

            def load_sdn(f):
                a, n = SHC[f]
                sp.dma_start(sdn[0:n, f % 4], t["s_dn"][a:a + n, :]).then_inc(ld_sdn[f // 5], 16)

            sp.wait_ge(up_mm, 2 * FC)
            load_sgu(0)
            load_sgu(1)
            for f in range(4):
                load_sdn(f)
            sp.wait_ge(mod_mm, 2)
            sp.dma_start(aT[:], halves("AT")).then_inc(ld_l1, 16)
            sp.dma_start(w1[:], halves("W1T")).then_inc(ld_l1, 16)
            sp.dma_start(bm[:], t["BmT"]).then_inc(ld_l1, 16)
            for k in range(KC):
                for e in range(0, EXP, 4):
                    sp.dma_start(e_gu[:, e:e + 4, k], t["e_gu"][e:e + 4, P * k:P * k + P, :].rearrange(
                        "e p n -> p e n")).then_inc(ld_exp, 16)

            def load_down(k, a, b):
                sp.dma_start(e_dn[k][:, a:b], t["e_dn"][a:b, IH * k:IH * k + IH, :].rearrange(
                    "e p n -> p e n")).then_inc(ld_down, 16)

            sp.wait_ge(down_mm, 4)
            load_down(1, 8, 16)
            for f in range(2, len(SHC)):
                sp.wait_ge(sgu_mm, 2 * f - 2)
                load_sgu(f)
                if f >= 4:
                    sp.wait_ge(sdn_f, f - 3)
                    load_sdn(f)
            sp.wait_ge(sgu_mm, 10)
            load_down(1, 0, 2)
            load_down(1, 4, 6)
            sp.wait_ge(sgu_mm, 12)
            load_down(1, 2, 4)
            load_down(1, 6, 8)
            load_down(0, 0, 8)
            load_down(0, 8, 16)

            def load(s, r, first_round):
                if not first_round:
                    sp.wait_ge(r_in, s - 3)
                    sp.wait_ge(r_wd, s - 3)
                sp.dma_start(slot_rows[:, r, :], slots_d[bass.ds(s * P, P), :]).then_inc(r_loaded[r], 16)

            sp.wait_ge(scattered, 16 * TILES * TOPK)
            head = 4 + (SLOT_TILES - 4) % RING
            for s in range(RING):
                load(s, s, True)
            for s in range(RING, head):
                load(s, s % RING, False)
            with sp.Fori(head, SLOT_TILES - RING + 1, RING) as i:
                for j in range(RING):
                    load(i + j, (head + j) % RING, False)
            for r in range(RING):
                sp.wait_ge(r_sent[r], 16 * len(range(r, SLOT_TILES, RING)))
            ykt = yk_d.rearrange("(t p k) d -> p t (k d)", p=P, k=TOPK)
            for j, (a, b) in enumerate(BACK):
                sp.dma_start(yk[:, a:b], ykt[:, a:b]).then_inc(yk_loaded[j], 16)
            ot = t["out"].rearrange("(t p) d -> t p d", p=P)
            for i in range(TILES):
                on_pool = sum(j in BACK_POOL for j in range(i + 1))
                if i in BACK_POOL:
                    sp.wait_ge(out_pool, on_pool)
                else:
                    sp.wait_ge(out_ready, i + 1 - on_pool)
                sp.dma_start(ot[i], res[:, i]).then_inc(stored, 16)
            sp.wait_ge(stored, 16 * TILES)

        @block.gpsimd
        def _(pool):
            G = nc.gpsimd
            pool.wait_ge(cond_ready, 1)
            wrows = t["cond_w"].rearrange("s c d -> (s c) d")
            for i in range(TILES):
                pool.indirect_dma_start(wgath[:, i, :], None, wrows,
                                        bass.IndirectOffsetOnAxis(cond_rows[:, i:i + 1], 0),
                                        bounds_check=COND * SEQ - 1).then_inc(gathered[i], 16)
            G.memset(a_h[:].bitcast(F32), 0.0).then_inc(zero_set, 1)
            G.memset(a_l[:].bitcast(F32), 0.0).then_inc(zero_set, 1)
            G.memset(b_stack[:].bitcast(F32), 0.0).then_inc(zero_set, 1)
            G.memset(exd[:], 0.0).then_inc(zero_set, 1)
            G.memset(fill[:, 0:D + EXP], 0.0).then_inc(zero_set, 1)
            G.memset(fill[:, D + EXP:ROW], NOWHERE).then_inc(zero_set, 1)

            def norm(u):
                pool.wait_ge(summed, u + 1)
                e3 = ex[:, u % 3, :].rearrange("p (a k) -> p a k", k=SEQ)
                G.tensor_tensor(e3, e3, spread(rtotal[:, u, :], 2, SEQ), ALU.mult).then_inc(normed, 1)

            def low_part(i):
                pool.wait_ge(wgd_hi, i + 1)
                if i in (2, 3):
                    lo, raw, hi = (w[:, i - 2] for w in (wg_l, wg, wg_h))
                else:
                    j = i if i < 2 else i - 2
                    lo, raw, hi = (w[:, 2 * j:2 * j + 2] for w in (wd_l, wd_, wd_h))
                G.tensor_tensor(lo, raw, hi.bitcast(F32), ALU.subtract).then_inc(wgd_lo, 1)

            for u in range(TILES):
                norm(u)
                if u not in (0, 3):
                    low_part({1: 0, 2: 1, 4: 2, 5: 3, 6: 4, 7: 5}[u])
            pool.wait_ge(pv_ready, TILES)
            G.memset(m_stack[:].bitcast(F32), 0.0).then_inc(m_zero, 1)
            pool.wait_ge(mod_mm, 2)
            G.memset(rw_h[:].bitcast(F32), 0.0).then_inc(m_zero, 1)
            G.memset(rw_l[:].bitcast(F32), 0.0).then_inc(m_zero, 1)
            for f in range(2):
                pool.wait_ge(sgu_hi, f + 1)
                G.tensor_tensor(sgu_l[:, f], sgu[:, f], sgu_h[:, f].bitcast(F32), ALU.subtract).then_inc(sh_lo_pool, 1)
            pool.wait_ge(sdn_hi, 1)
            G.tensor_tensor(sdn_l[:], sdn[:], sdn_h[:].bitcast(F32), ALU.subtract).then_inc(sh_lo_pool, 1)
            for i, (lo, raw, hi) in enumerate(((aT_l, aT, aT_h), (w1_l, w1, w1_h), (bm_l, bm, bm_h))):
                pool.wait_ge(l1_hi, i + 1)
                G.tensor_tensor(lo[:], raw[:], hi[:].bitcast(F32), ALU.subtract).then_inc(l1_lo, 1)
            pool.wait_ge(l1_hi, 4)
            pool.wait_ge(m_zero, 3)
            G.tensor_tensor(rw_l[:, :, 0:EXP + 1], rw[:], rw_h[:, :, 0:EXP + 1].bitcast(F32),
                            ALU.subtract).then_inc(l1_lo, 1)

            pool.wait_ge(member_ready, 1)
            dest_k = K["dest"].rearrange("p (t k) -> p t k", k=TOPK)
            G.tensor_tensor(prod_d[:], hot[:], spread(dest_k, 3, EXP), ALU.mult).then_inc(pool_step, 1)
            pool.wait_ge(pool_step, 1)
            G.tensor_tensor(prod_d[:, :, 0:2], prod_d[:, :, 0:2], prod_d[:, :, 2:4], ALU.add).then_inc(pool_step, 1)
            pool.wait_ge(pool_step, 2)
            pool.wait_ge(h1_ready, 4)
            G.tensor_tensor(rows[:, :, D + EXP:ROW], prod_d[:, :, 0], prod_d[:, :, 1], ALU.add).then_inc(pool_step, 1)
            pool.wait_ge(sgu_hi, 3)
            G.tensor_tensor(sgu_l[:, 0], sgu[:, 0], sgu_h[:, 0].bitcast(F32), ALU.subtract).then_inc(sh_lo_pool, 1)

            pool.wait_ge(filled, 16 * len(range(0, SLOT_TILES, 8)))
            pool.wait_ge(pool_step, 3)
            for i in range(TILES):
                pool.wait_ge(slot_ready, 2 + i // 4)
                for k in range(TOPK):
                    pool.indirect_dma_start(slots_d, bass.IndirectOffsetOnAxis(slot[:, i * TOPK + k:i * TOPK + k + 1], 0),
                                            rows[:, i, :], None, bounds_check=SLOTS - 1).then_inc(scattered, 16)

            for j in split_pool:
                e = split_order[j]
                pool.wait_ge(egu_hi, j + 1)
                G.tensor_tensor(e_gu_l[:, e], e_gu[:, e], e_gu_h[:, e].bitcast(F32), ALU.subtract).then_inc(sh_lo_pool, 1)

            for g in range(2, 4):
                pool.wait_ge(egu_hi, EXP + g + 1)
                G.tensor_tensor(dn_l[:, 4 * g:4 * g + 4], e_dn[0][:, 4 * g:4 * g + 4], dn_h[:, 4 * g:4 * g + 4].bitcast(F32),
                                ALU.subtract).then_inc(sh_lo_pool, 1)

            within = pool.to_reg(TOK * TOPK - 1)

            def send(s, r):
                pool.wait_ge(r_y, s + 1)
                pool.indirect_dma_start(yk_d, bass.IndirectOffsetOnAxis(dest[:, r:r + 1], 0), y[:, r, :], None,
                                        bounds_check=within, oob_is_err=False).then_inc(r_sent[r], 16)

            for s in range(SLOT_TILES):
                send(s, s % RING)

            steps = [3]

            def link(ins):
                steps[0] += 1
                ins.then_inc(pool_step, 1)
                pool.wait_ge(pool_step, steps[0])

            for i in BACK_POOL:
                pool.wait_ge(yk_loaded[back_group(i)], 16)
                add_experts(G, i, link).then_inc(out_pool, 1)

        @block.scalar
        def _(act_e):
            A = nc.scalar.activation
            act_e.wait_ge(ld_const, 16)
            A(warm[:, 0:1], K["ident"][:, 0:1], ACT.Sqrt)
            act_e.wait_ge(ld_norm, 16)

            def keep_hid(h):
                for g in range(2 * h, 2 * h + 2):
                    act_e.wait_ge(hid_ready, 2 * g + 2)
                    A(hn[:, 2 * g:2 * g + 2].rearrange("p t d -> p (t d)"), bank[g][:, :], ACT.Copy).then_inc(hid_kept, 1)

            def square_hid(h):
                for i in range(4 * h, 4 * h + 4):
                    act_e.wait_ge(hid_kept, i // 2 + 1)
                    A(hnorm[:, i], hn[:, i], ACT.Square, accum_out=ssq[:, i:i + 1]).then_inc(ssq_ready, 1)

            def root(h):
                act_e.wait_ge(msq_ready, h + 1)
                A(rms[:, 4 * h:4 * h + 4], msq[:, 4 * h:4 * h + 4], ACT.Sqrt).then_inc(rms_ready, 1)

            def keep_hT(h):
                act_e.wait_ge(hnT_ready, 4 * h + 4)
                for k in range(KC):
                    A(hT_h[:, k, half(h)], bank[4 + 2 * h + k][:, :], ACT.Copy).then_inc(hT_hi, 1)

            def qkv_high(k):
                act_e.wait_ge(ld_wqkv, 48)
                A(wqkv_h[:, :, k], wqkv[:, :, k], ACT.Copy, scale=norm_w[:, 0, k:k + 1]).then_inc(wqkv_hi, 1)

            keep_hid(0)
            square_hid(0)
            root(0)
            qkv_high(0)
            qkv_high(1)
            keep_hid(1)
            keep_hT(0)
            square_hid(1)
            root(1)
            act_e.wait_ge(ld_up, 16)
            for k in range(KC):
                A(wu_h[:, k], wu[:, k], ACT.Copy, scale=norm_w[:, 1, k:k + 1]).then_inc(wu_hi, 1)
            keep_hT(1)
            def keep_qv(h):
                for c in range(KC):
                    act_e.wait_ge(q_mm, 2 * h + 1 + c)
                    A(qT[:, c, half(h)], bank[qk_bank(h, 0) + c][:, :], ACT.Copy, scale=HD ** -0.5).then_inc(q_kept, 1)
                for g in range(2 * h, 2 * h + 2):
                    act_e.wait_ge(v_mm, g + 1)
                    A(v_sb[:, 2 * g:2 * g + 2].rearrange("p t d -> p (t d)"), bank[4 + g % 2][:, :],
                      ACT.Copy).then_inc(v_kept, 1)

            def keys(g, c):
                act_e.wait_ge(k_kept, 2 * (g // 2) + 1 + c)
                if g >= 2:
                    act_e.wait_ge(scored, 2 * g - 2)
                mask_k(lambda o, i, m: A(o, i, ACT.Copy, scale=m), kx_act, g, c, range(5, 8))

            def keep_up(i):
                act_e.wait_ge(up_mm, i + 1)
                if i == 12:
                    act_e.wait_ge(kx_dve, 8)
                A(up[:, i // 2, half(i % 2)], bank[6 + i % 2][:, :], ACT.Copy).then_inc(up_ready, 1)

            def exp(u):
                act_e.wait_ge(shifted, u + 1)
                A(ex[:, u % 3, :], ex[:, u % 3, :], ACT.Exp).then_inc(exped, 1)

            def diagonal(u):
                act_e.wait_ge(exT_ready, u + 1)
                if u >= 2:
                    act_e.wait_ge(pv_ready, u - 1)
                else:
                    act_e.wait_ge(zero_set, 4)
                on_diagonal(lambda o, i: A(o, i, ACT.Copy), exd_act, u, (2, 3))

            def even_heads(u):
                act_e.wait_ge(pv_ready, u + 1)
                o = bank[4 + u % 2][:, :].rearrange("p (c e q) -> p c e q", c=KC, e=2)
                A(attnT[:, :, P * u:P * u + P], o[:, :, 0, :], ACT.Copy, scale=K["pair_of"][:, 0:1]).then_inc(attn_even, 1)

            keep_qv(0)
            keys(0, 0)
            keys(0, 1)
            act_e.wait_ge(ld_small, 48)
            act_e.wait_ge(zero_set, 3)
            for k in range(KC):
                A(a_h[:, k, 0:RANK], a_raw[:, k], ACT.Copy, scale=norm_w[:, 1, k:k + 1]).then_inc(ab_hi, 1)
            A(b_stack[0:RANK], b_raw[:], ACT.Copy).then_inc(ab_hi, 1)
            A(b_stack[SEQ:SEQ + RANK], b_raw[:], ACT.Copy).then_inc(ab_hi, 1)
            keep_qv(1)
            keys(1, 0)
            keys(1, 1)
            act_e.wait_ge(woa_mm, 1)
            A(woa[:].rearrange("p k r -> p (k r)"), bank[6][:, 0:KC * RANK], ACT.Copy).then_inc(woa_ready, 1)

            def down_high(j):
                A(wd_h[:, 2 * j:2 * j + 2], wd_[:, 2 * j:2 * j + 2], ACT.Copy).then_inc(wgd_hi, 1)

            def gate_high(k):
                A(wg[:, k], wg[:, k], ACT.Copy, scale=norm_w[:, 1, k:k + 1]).then_inc(wg_scaled, 1)
                act_e.wait_ge(wg_scaled, k + 1)
                A(wg_h[:, k], wg[:, k], ACT.Copy).then_inc(wgd_hi, 1)

            act_e.wait_ge(ld_gate, 16)
            act_e.wait_ge(ld_down, 16)
            for u in range(TILES):
                exp(u)
                keep_up(2 * u)
                if u:
                    diagonal(u - 1)
                keep_up(2 * u + 1)
                if u >= 2:
                    even_heads(u - 2)
                if u == 0:
                    keys(2, 0)
                    keys(2, 1)
                if u in (2, 3):
                    keys(3, u - 2)
                if u == 1:
                    down_high(0)
                    down_high(1)
                if u in (4, 5):
                    gate_high(u - 4)
                if u >= 6:
                    down_high(u - 4)
            diagonal(TILES - 1)
            even_heads(TILES - 2)
            even_heads(TILES - 1)
            A(warm[:, 1:2], K["ident"][:, 0:1], ACT.Tanh)
            for h in range(2):
                act_e.wait_ge(mod_mm, h + 1)
                A(thm[:, half(h)], bank[4 + h][SEQ * h:SEQ * h + RANK, :], ACT.Tanh).then_inc(mod_act, 1)
            A(warm[:, 2:3], K["ident"][:, 0:1], ACT.Silu)
            act_e.wait_ge(m_zero, 1)
            for h in range(2):
                act_e.wait_ge(m_ready, h + 1)
                A(m_stack[64:64 + RANK, half(h)], m_sb[:, half(h)], ACT.Copy).then_inc(mod_act, 1)

            def high_parts(i):
                if i < 2:
                    act_e.wait_ge(ld_sgu[i], 32)
                    A(sgu_h[:, i], sgu[:, i], ACT.Copy).then_inc(sgu_hi, 1)
                elif i == 2:
                    act_e.wait_ge(ld_sdn[0], 64)
                    A(sdn_h[:], sdn[:], ACT.Copy).then_inc(sdn_hi, 1)
                elif i < 6:
                    if i == 3:
                        act_e.wait_ge(ld_l1, 48)
                    hi, raw = ((aT_h, aT), (w1_h, w1), (bm_h, bm))[i - 3]
                    A(hi[:], raw[:], ACT.Copy).then_inc(l1_hi, 1)
                elif i == 6:
                    act_e.wait_ge(m_zero, 3)
                    act_e.wait_ge(ld_adapt, 48)
                    A(rw_h[:, :, 0:EXP + 1], rw[:], ACT.Copy).then_inc(l1_hi, 1)

            def act_high(i):
                act_e.wait_ge(act_ready, i + 1)
                A(act_h[:, i // 2, half(i % 2)], g_sb[:, i % 3, :], ACT.Copy).then_inc(act_hi, 1)

            for i in range(2 * FC):
                act_e.wait_ge(gate_mm, i + 1)
                if i >= 3:
                    act_e.wait_ge(act_lo, i - 2)
                A(g_sb[:, i % 3, :], bank[gate_bank(i)][:, :], ACT.Silu).then_inc(silu_ready, 1)
                act_high(i)
                if i >= 8:
                    high_parts(i - 8)
            for h in range(2):
                act_e.wait_ge(x1T_mm, 4 * h + 4)
                for k in range(KC):
                    A(x1T_h[:, k, half(h)], bank[4 + 2 * h + k][:, :], ACT.Copy).then_inc(x1T_hi, 1)
            for h in range(2):
                act_e.wait_ge(xam_ready, h + 1)
                A(xam_h[:, half(h)], xam[:, half(h)], ACT.Copy).then_inc(xam_hi, 1)
            for g in range(4):
                act_e.wait_ge(h1_mm, g + 1)
                A(rows[:, 2 * g:2 * g + 2, 0:D], bank[2 + g][:, :].rearrange("p (t d) -> p t d", t=2),
                  ACT.Copy).then_inc(h1_ready, 1)
            for h in range(2):
                act_e.wait_ge(h1T_mm, 4 * h + 4)
                for k in range(KC):
                    A(hT_h[:, k, half(h)], bank[((6, 7), (0, 1))[h][k]][:, :], ACT.Copy).then_inc(h1T_hi, 1)
            for h in range(2):
                act_e.wait_ge(lgT_mm, h + 1)
                A(lgT[:, half(h)], bank[2 + h][0:SEQ, :], ACT.Copy).then_inc(lgT_kept, 1)
            act_e.wait_ge(lgx_ready, 1)
            A(lgx[:], lgx[:], ACT.Exp).then_inc(lge_ready, 1)
            A(sgate[:], lg_sb[:, :, EXP], ACT.Sigmoid).then_inc(lge_ready, 1)

            def s_silu(i):
                f, h = i // 2, i % 2
                act_e.wait_ge(sgu_mm, i + 1)
                if i >= 3:
                    act_e.wait_ge(s_act_lo, i - 2)
                b_ = bank[(6, 0)[h]]
                if SHC[f][1] == P:
                    A(s_g[:, i % 3, :], b_[:, :], ACT.Silu).then_inc(s_silu_ready, 1)
                else:
                    A(s_g[64:128, i % 3, :], b_[0:64, :], ACT.Silu).then_inc(s_silu_ready, 1)

            def s_high(i):
                f, h = i // 2, i % 2
                n = SHC[f][1]
                act_e.wait_ge(s_act_ready, i + 1)
                if f >= 3:
                    act_e.wait_ge(sdn_f, f - 2)
                A(s_act_h[0:n, f % 3, half(h)], s_g[0:n, i % 3, :], ACT.Copy).then_inc(s_act_hi, 1)

            def s_gu_high(f):
                r, m = f % 2, 2 if SHC[f][1] == P else 1
                act_e.wait_ge(ld_sgu[r], 32 * (f // 2 + 1))
                A(sgu_h[:, r, 0:m], sgu[:, r, 0:m], ACT.Copy).then_inc(sgu_hi, 1)

            def s_dn_high(f):
                n = SHC[f][1]
                act_e.wait_ge(ld_sdn[f // 5], (80, 16)[f // 5])
                A(sdn_h[0:n, f % 4], sdn[0:n, f % 4], ACT.Copy).then_inc(sdn_hi, 1)

            def expert_high(j):
                e = split_order[j]
                A(e_gu_h[:, e], e_gu[:, e], ACT.Copy).then_inc(egu_hi, 1)

            for i in range(2 * len(SHC)):
                s_silu(i)
                if i % 2 == 0 and 4 <= i < 2 * len(SHC) - 2:
                    s_gu_high(i // 2 + 1)
                split = range(*split_high.get(i, (0, 0)))
                if i == 4:
                    act_e.wait_ge(ld_exp, 16 * 8)
                for j in split[:1]:
                    expert_high(j)
                s_high(i)
                if i == 1:
                    s_gu_high(2)
                if i in (8, 10):
                    s_dn_high(i // 2)
                for j in split[1:]:
                    expert_high(j)

            def keep_in(s, q):
                act_e.wait_ge(r_in, s + 1)
                A(e_in_h[:, q], bank[2 + q][:, 0:D].rearrange("p (k n) -> p k n", k=KC), ACT.Copy).then_inc(r_hi, 1)

            def silu(s, q):
                act_e.wait_ge(r_gu, s + 1)
                A(sil[:, q], bank[q][:, 0:IM], ACT.Silu).then_inc(r_sil, 1)

            def weigh(s, q, r, again):
                act_e.wait_ge(r_dn, s + 1)
                act_e.wait_ge(r_wd, s + 1)
                if again:
                    act_e.wait_ge(r_sent[r], ring_count(s, r) - 16)
                A(y[:, r, :], bank[6 + q][:, 0:D], ACT.Copy, scale=wd[:, r, 0:1]).then_inc(r_y, 1)

            def keep_act(s, q, again):
                act_e.wait_ge(r_ta, s + 1)
                if again:
                    act_e.wait_ge(r_dn, s - 1)
                A(actT_h[:, q], bank[4 + q][0:IH, 0:P], ACT.Copy).then_inc(r_act_hi, 1)

            act_e.wait_ge(ld_down, 16 * (1 + 7))
            act_e.wait_ge(sdn_mm, 4)
            for g in range(4):
                A(dn_h[:, 4 * g:4 * g + 4], e_dn[0][:, 4 * g:4 * g + 4], ACT.Copy).then_inc(egu_hi, 1)
                if g == 2:
                    keep_in(0, 0)
            for s in range(PIPE0):
                if s:
                    act_e.wait_ge(r_gu, s)
                keep_in(s + 1, (s + 1) % 2)
                silu(s, s % 2)
                if s:
                    keep_act(s - 1, (s - 1) % 2, False)

            def step(s, j, again, again_act=True):
                q = (PIPE0 + j) % 2
                act_e.wait_ge(r_gu, s)
                keep_in(s + 1, 1 - q)
                act_e.wait_ge(r_act, s - 1)
                silu(s, q)
                keep_act(s - 1, 1 - q, again_act)
                weigh(s - 2, q, (PIPE0 + j - 2) % RING, again)

            for j in range(RING):
                step(PIPE0 + j, j, False, j >= 1)
            with act_e.Fori(PIPE0 + RING, SLOT_TILES - RING, RING) as i:
                for j in range(RING):
                    step(i + j, j, True)
            s = SLOT_TILES - 1
            act_e.wait_ge(r_act, s - 1)
            silu(s, s % 2)
            keep_act(s - 1, (s - 1) % 2, True)
            weigh(s - 2, (s - 2) % 2, (s - 2) % RING, True)
            keep_act(s, s % 2, True)
            for s in range(SLOT_TILES - 2, SLOT_TILES):
                weigh(s, s % 2, s % RING, True)

        @block.vector
        def _(dve):
            V = nc.vector
            steps = [0]

            def link(ins):
                steps[0] += 1
                ins.then_inc(dve_step, 1)
                dve.wait_ge(dve_step, steps[0])

            dve.wait_ge(ld_cond, 32)
            V.tensor_scalar(cond_rows[:], cond_b[:], float(SEQ), pos_of[:, 0:1], ALU.mult, ALU.add).then_inc(cond_ready, 1)
            dve.wait_ge(ld_const, 16)
            V.tensor_copy(ident_b[:], K["ident"]).then_inc(bf_ready, 1)
            V.tensor_copy(causal_b[:], K["causal"]).then_inc(bf_ready, 1)
            V.tensor_copy(before_b[:], K["before"]).then_inc(bf_ready, 1)
            V.memset(ones_b[:], 1.0).then_inc(bf_ready, 1)
            def on_batches(i):
                dve.wait_ge(gathered[i], 16)
                V.tensor_tensor(wbd[:, i], spread(wgath[:, i], 1, 4), spread(K["batch_of"], 2, SEQ),
                                ALU.mult).then_inc(wbd_ready, 1)

            for i in range(6):
                on_batches(i)
            def mean_square(h):
                dve.wait_ge(ssq_ready, 4 * h + 4)
                V.tensor_scalar(msq[:, 4 * h:4 * h + 4], ssq[:, 4 * h:4 * h + 4], 1.0 / D, EPS, ALU.mult, ALU.add).then_inc(msq_ready, 1)

            def normalize(h):
                dve.wait_ge(rms_ready, h + 1)
                link(V.reciprocal(rstd[:, 4 * h:4 * h + 4], rms[:, 4 * h:4 * h + 4]))
                for i in range(4 * h, 4 * h + 4):
                    V.tensor_scalar(hnorm[:, i], hn[:, i], rstd[:, i:i + 1], None, ALU.mult).then_inc(hn_ready, 1)

            def low_hT(h):
                for k in range(KC):
                    dve.wait_ge(hT_hi, 2 * h + k + 1)
                    V.tensor_tensor(hT_l[:, k, half(h)], bank[4 + 2 * h + k][:, :], hT_h[:, k, half(h)].bitcast(F32),
                                    ALU.subtract).then_inc(hT_lo, 1)

            def low_up(k):
                dve.wait_ge(wu_hi, k + 1)
                V.scalar_tensor_tensor(wu_l[:, k], wu[:, k], norm_w[:, 1, k:k + 1], wu_h[:, k].bitcast(F32),
                                       ALU.mult, ALU.subtract).then_inc(wu_lo, 1)

            def qkv_low(k):
                dve.wait_ge(wqkv_hi, k + 1)
                V.scalar_tensor_tensor(wqkv_l[:, :, k], wqkv[:, :, k], norm_w[:, 0, k:k + 1],
                                       wqkv_h[:, :, k].bitcast(F32), ALU.mult, ALU.subtract).then_inc(wqkv_lo, 1)

            mean_square(0)
            on_batches(6)
            on_batches(7)
            normalize(0)
            dve.wait_ge(ld_norm, 16)
            qkv_low(0)
            qkv_low(1)
            low_hT(0)
            mean_square(1)
            normalize(1)
            low_up(0)
            low_up(1)
            low_hT(1)
            def keep_k(h):
                for c in range(KC):
                    dve.wait_ge(k_mm, 2 * h + 1 + c)
                    V.tensor_copy(kT[:, c, half(h)], bank[qk_bank(h, 1) + c][:, :]).then_inc(k_kept, 1)

            def keys(g, c):
                dve.wait_ge(k_kept, 2 * (g // 2) + 1 + c)
                if g >= 2:
                    dve.wait_ge(scored, 2 * g - 2)
                mask_k(lambda o, i, m: V.tensor_scalar(o, i, m, None, ALU.mult), kx_dve, g, c, range(5))

            def adapter_low():
                for k in range(KC):
                    dve.wait_ge(ab_hi, k + 1)
                    V.scalar_tensor_tensor(a_l[:, k, 0:RANK], a_raw[:, k], norm_w[:, 1, k:k + 1],
                                           a_h[:, k, 0:RANK].bitcast(F32), ALU.mult, ALU.subtract).then_inc(ab_lo, 1)
                dve.wait_ge(ab_hi, 4)
                V.tensor_tensor(b_stack[64:64 + RANK], b_raw[:], b_stack[0:RANK].bitcast(F32), ALU.subtract).then_inc(ab_lo, 1)

            def shift(u):
                dve.wait_ge(scored, u + 1)
                s3 = bank[u % 4][:, :].rearrange("p (a k) -> p a k", k=SEQ)
                link(V.reduce_max(peak[:, u, :], s3, AX.X))
                V.tensor_tensor(ex[:, u % 3, :].rearrange("p (a k) -> p a k", k=SEQ), s3,
                                spread(peak[:, u, :], 2, SEQ), ALU.subtract).then_inc(shifted, 1)

            def sums(u):
                dve.wait_ge(exped, u + 1)
                link(V.reduce_sum(total[:, u, :], ex[:, u % 3, :].rearrange("p (a k) -> p a k", k=SEQ), AX.X))
                V.reciprocal(rtotal[:, u, :], total[:, u, :]).then_inc(summed, 1)

            def turn(u):
                dve.wait_ge(normed, u + 1)
                if u >= 2:
                    dve.wait_ge(exd_act, u - 1)
                V.transpose(exT[:, u % 2, :], ex[:, u % 3, :]).then_inc(exT_ready, 1)

            def diagonal(u):
                dve.wait_ge(exT_ready, u + 1)
                if u >= 2:
                    dve.wait_ge(pv_ready, u - 1)
                else:
                    dve.wait_ge(zero_set, 4)
                on_diagonal(V.tensor_copy, exd_dve, u, (0, 1))

            def odd_heads(u):
                dve.wait_ge(attn_even, u + 1)
                o = bank[4 + u % 2][:, :].rearrange("p (c e q) -> p c e q", c=KC, e=2)
                a_ = attnT[:, :, P * u:P * u + P]
                V.scalar_tensor_tensor(a_, o[:, :, 1, :], K["pair_of"][:, 1:2], a_, ALU.mult, ALU.add).then_inc(attn_ready, 1)

            V.tensor_tensor(res[:], hn[:], res[:], ALU.add)
            keep_k(0)
            keys(0, 0)
            keys(0, 1)
            keep_k(1)
            keys(1, 0)
            keys(1, 1)
            for u in range(TILES):
                shift(u)
                if u:
                    turn(u - 1)
                    diagonal(u - 1)
                if u == 0:
                    adapter_low()
                sums(u)
                if u >= 2:
                    odd_heads(u - 2)
                if u == 0:
                    keys(2, 0)
                    keys(2, 1)
                if u in (2, 3):
                    keys(3, u - 2)
            turn(TILES - 1)
            diagonal(TILES - 1)
            odd_heads(TILES - 2)
            odd_heads(TILES - 1)
            for h in range(2):
                dve.wait_ge(mod_act, h + 1)
                dve.wait_ge(ha_mm, h + 1)
                V.scalar_tensor_tensor(m_sb[:, half(h)], thm[:, half(h)], 0.1, bank[h][0:RANK, :],
                                       ALU.mult, ALU.mult).then_inc(m_ready, 1)
                dve.wait_ge(m_ready, h + 1)
                dve.wait_ge(m_zero, 1)
                link(V.tensor_copy(m_stack[0:RANK, half(h)], m_sb[:, half(h)]))
                V.tensor_tensor(m_stack[SEQ:SEQ + RANK, half(h)], m_sb[:, half(h)], m_stack[0:RANK, half(h)].bitcast(F32),
                                ALU.subtract).then_inc(m_lo, 1)
            dve.wait_ge(ld_adapt, 48)
            link(V.tensor_scalar(adapter_sel[:], adapter_b[:], K["adapter_of"], scale_p[:, 0:1], ALU.is_equal, ALU.mult))

            def act_low(i):
                f = i // 2
                dve.wait_ge(act_hi, i + 1)
                if f >= 2:
                    dve.wait_ge(down_f, f - 1)
                V.tensor_tensor(act_l[:, f % 2, half(i % 2)], g_sb[:, i % 3, :], act_h[:, f, half(i % 2)].bitcast(F32),
                                ALU.subtract).then_inc(act_lo, 1)

            for i in range(2 * FC):
                dve.wait_ge(silu_ready, i + 1)
                dve.wait_ge(up_ready, i + 1)
                V.tensor_tensor(g_sb[:, i % 3, :], g_sb[:, i % 3, :], up[:, i // 2, half(i % 2)],
                                ALU.mult).then_inc(act_ready, 1)
                act_low(i)
            for i in range(4):
                dve.wait_ge(down_mm, i + 1)
                r2 = res[:, 2 * i:2 * i + 2].rearrange("p t d -> p (t d)")
                V.tensor_tensor(r2, bank[i][:, :], r2, ALU.add).then_inc(x1_ready, 1)
            for h in range(2):
                for k in range(KC):
                    dve.wait_ge(x1T_hi, 2 * h + k + 1)
                    V.tensor_tensor(x1T_l[:, k, half(h)], bank[4 + 2 * h + k][:, :], x1T_h[:, k, half(h)].bitcast(F32),
                                    ALU.subtract).then_inc(x1T_lo, 1)
            for h in range(2):
                dve.wait_ge(xa_mm, h + 1)
                V.tensor_tensor(xam[:, half(h)].rearrange("p (b s) -> p b s", s=SEQ),
                                bank[h][:, :].rearrange("p (b s) -> p b s", s=SEQ),
                                spread(adapter_sel[:, 16 * h:16 * h + 16], 2, SEQ), ALU.mult).then_inc(xam_ready, 1)
            for h in range(2):
                dve.wait_ge(xam_hi, h + 1)
                V.tensor_tensor(xam_l[:, half(h)], xam[:, half(h)], xam_h[:, half(h)].bitcast(F32),
                                ALU.subtract).then_inc(xam_lo, 1)
            for h in range(2):
                for k in range(KC):
                    dve.wait_ge(h1T_hi, 2 * h + k + 1)
                    V.tensor_tensor(hT_l[:, k, half(h)], bank[((6, 7), (0, 1))[h][k]][:, :],
                                    hT_h[:, k, half(h)].bitcast(F32), ALU.subtract).then_inc(h1T_lo, 1)

            dve.wait_ge(lg_mm, 1)
            V.tensor_copy(lg_sb[:].rearrange("p t e -> p (t e)"), bank[4][:, 0:TILES * SEQ]).then_inc(lg_ready, 1)
            dve.wait_ge(lg_ready, 1)
            lg = lg_sb[:, :, 0:EXP]
            link(V.reduce_max(lgm[:, 0, :], lg, AX.X))
            V.tensor_tensor(lgx[:], lg, spread(lgm[:, 0, :], 2, EXP), ALU.subtract).then_inc(lgx_ready, 1)
            dve.wait_ge(lge_ready, 1)
            link(V.reduce_sum(lgm[:, 1, :], lgx[:], AX.X))
            link(V.reciprocal(lgm[:, 2, :], lgm[:, 1, :]))
            link(V.tensor_tensor(lgx[:], lgx[:], spread(lgm[:, 2, :], 2, EXP), ALU.mult))
            for i in range(TILES):
                ins = V.max(top_v[:, i], lgx[:, i])
            link(ins)
            for i in range(TILES):
                ins = V.max_index(top_i[:, i], top_v[:, i], lgx[:, i])
            link(ins)
            link(V.tensor_copy(top_f[:], top_i[:, :, 0:TOPK]))
            link(V.tensor_tensor(hot[:], spread(top_f[:], 3, EXP),
                                 spread(spread(K["iota_e"], 1, TOPK), 1, TILES), ALU.is_equal))
            with nc.allow_low_precision(reason="zeros and ones"):
                V.tensor_reduce(member[:], hot[:].rearrange("p t k e -> p t e k"), AX.X, ALU.add).then_inc(member_ready, 1)
            def find_slots():
                dve.wait_ge(rank_mm, 1)
                rank = bank[5][:, 0:P].rearrange("p (t e) -> p t e", e=EXP)
                count = bank[5][:, P:P + EXP]
                link(V.tensor_tensor(over[:], spread(count, 2, TILES), spread(K["tile_edge"], 1, EXP), ALU.is_gt))
                link(V.reduce_sum(ntile[:], over[:], AX.X))
                link(V.tensor_tensor(pairs[:], spread(ntile[:], 1, EXP), K["lower_e"].rearrange("p (a b) -> p a b", a=EXP), ALU.mult))
                link(V.reduce_sum(first[:], pairs[:], AX.X))
                V.scalar_tensor_tensor(where[:], spread(first[:], 1, TILES), float(P), rank, ALU.mult, ALU.add).then_inc(rank_read, 1)
                dve.wait_ge(rank_read, 1)
                link(V.tensor_tensor(prod[:], hot[:], spread(where[:], 2, TOPK), ALU.mult))
                link(V.reduce_sum(slot_f[:], prod[:].rearrange("p t k e -> p (t k) e"), AX.X))
                V.tensor_copy(slot[:], slot_f[:]).then_inc(slot_ready, 1)

            def fill_rows(h):
                t4 = slice(4 * h, 4 * h + 4)
                link(V.tensor_tensor(prod[:, t4], hot[:, t4], spread(wts[:, t4], 3, EXP), ALU.mult))
                V.tensor_reduce(rows[:, t4, D:D + EXP], prod[:, t4].rearrange("p t k e -> p t e k"), AX.X,
                                ALU.add).then_inc(slot_ready, 1)

            def find_experts():
                link(V.tensor_tensor(last[:], first[:], ntile[:], ALU.add))
                link(V.memset(last[:, EXP - 1:EXP], float(SLOT_TILES)))
                dve.wait_ge(pool_step, 3)
                link(V.tensor_tensor(hot_t[:], spread(K["iota_s"], 2, EXP), spread(last[:], 1, SLOT_TILES), ALU.is_ge))
                link(V.reduce_sum(who_f[:], hot_t[:], AX.X))
                V.tensor_tensor(hot_s[:], spread(who_f[:], 2, EXP), spread(K["iota_e"], 1, SLOT_TILES), ALU.is_equal)
                V.tensor_copy(who[:], who_f[:]).then_inc(who_ready, 1)

            def s_mul(i):
                f, h = i // 2, i % 2
                n = SHC[f][1]
                dve.wait_ge(s_silu_ready, i + 1)
                if n == P:
                    V.tensor_tensor(s_g[:, i % 3, :], s_g[:, i % 3, :], bank[(7, 1)[h]][:, :], ALU.mult).then_inc(s_act_ready, 1)
                else:
                    V.tensor_tensor(s_g[0:64, i % 3, :], s_g[64:128, i % 3, :], bank[(6, 0)[h]][64:128, :],
                                    ALU.mult).then_inc(s_act_ready, 1)

            def s_low(i):
                f, h = i // 2, i % 2
                n = SHC[f][1]
                dve.wait_ge(s_act_hi, i + 1)
                V.tensor_tensor(s_act_l[0:n, f % 3, half(h)], s_g[0:n, i % 3, :],
                                s_act_h[0:n, f % 3, half(h)].bitcast(F32), ALU.subtract).then_inc(s_act_lo, 1)

            def s_gu_low(f):
                r, m = f % 2, 2 if SHC[f][1] == P else 1
                dve.wait_ge(sgu_hi, f + 1)
                V.tensor_tensor(sgu_l[:, r, 0:m], sgu[:, r, 0:m], sgu_h[:, r, 0:m].bitcast(F32),
                                ALU.subtract).then_inc(sgu_lo_dve, 1)

            def s_dn_low(f):
                n = SHC[f][1]
                dve.wait_ge(sdn_hi, f - 2)
                V.tensor_tensor(sdn_l[0:n, f % 4], sdn[0:n, f % 4], sdn_h[0:n, f % 4].bitcast(F32),
                                ALU.subtract).then_inc(sdn_lo_dve, 1)

            s_mul(0)
            link(V.reduce_sum(lgm[:, 0, :], top_v[:, :, 0:TOPK], AX.X))
            link(V.tensor_scalar(lgm[:, 1, :], lgm[:, 0, :], 1e-9, None, ALU.max))
            link(V.reciprocal(lgm[:, 2, :], lgm[:, 1, :]))
            link(V.tensor_tensor(wts[:], top_v[:, :, 0:TOPK], spread(lgm[:, 2, :], 2, TOPK), ALU.mult))
            s_mul(1)
            find_slots()
            dve.wait_ge(h1_ready, 4)
            fill_rows(0)
            s_mul(2)
            s_low(0)
            s_low(1)
            s_mul(3)
            fill_rows(1)
            def expert_low(j):
                e = split_order[j]
                dve.wait_ge(egu_hi, j + 1)
                V.tensor_tensor(e_gu_l[:, e], e_gu[:, e], e_gu_h[:, e].bitcast(F32), ALU.subtract).then_inc(egu_lo, 1)

            for i in range(2, 2 * len(SHC)):
                f = i // 2
                if i > 3:
                    s_mul(i)
                if i % 2 == 0 and 2 < i < 2 * len(SHC) - 2:
                    s_gu_low(f + 1)
                split = range(*split_low.get(i, (0, 0)))
                for j in split[:1]:
                    expert_low(j)
                s_low(i)
                if i in (8, 10):
                    s_dn_low(f)
                if i == 10:
                    V.memset(sdn_h[64:128, f % 4].bitcast(F32), 0.0).then_inc(sdn_lo_dve, 1)
                    V.memset(sdn_l[64:128, f % 4].bitcast(F32), 0.0).then_inc(sdn_lo_dve, 1)
                if i == 7:
                    find_experts()
                for j in split[1:]:
                    expert_low(j)
            dve.wait_ge(lge_ready, 2)
            for i in range(TILES):
                if i % 2 == 0:
                    dve.wait_ge(sdn_mm, i // 2 + 1)
                V.scalar_tensor_tensor(res[:, i], bank[2 + i // 2][:, D * (i % 2):D * (i % 2) + D], sgate[:, i:i + 1],
                                       res[:, i], ALU.mult, ALU.add).then_inc(shared_added, 1)

            def low_in(s, q):
                dve.wait_ge(r_hi, s + 1)
                V.tensor_tensor(e_in_l[:, q], bank[2 + q][:, 0:D].rearrange("p (k n) -> p k n", k=KC),
                                e_in_h[:, q].bitcast(F32), ALU.subtract).then_inc(r_lo, 1)

            def mul(s, q):
                dve.wait_ge(r_sil, s + 1)
                V.tensor_tensor(act[:, q], sil[:, q], bank[q][:, IM:2 * IM], ALU.mult).then_inc(r_act, 1)

            def keep_actT(s, q):
                dve.wait_ge(r_act_hi, s + 1)
                V.tensor_copy(actT[:, q], bank[4 + q][0:IH, P:2 * P])
                V.tensor_tensor(actT_l[:, q], bank[4 + q][0:IH, 0:P], actT_h[:, q].bitcast(F32),
                                ALU.subtract).then_inc(r_actT, 1)

            def pick_row(s, r, again):
                dve.wait_ge(r_loaded[r], ring_count(s, r))
                V.tensor_tensor(pick[:, r], slot_rows[:, r, D:ROW].rearrange("p (a e) -> p a e", a=2),
                                spread(hot_s[:, bass.ds(s, 1), :].rearrange("p s e -> p (s e)"), 1, 2), ALU.mult).then_inc(r_pick, 1)
                if again:
                    dve.wait_ge(r_sent[r], ring_count(s, r) - 16)
                dve.wait_ge(r_pick, 2 * s + 1)
                V.reduce_sum(wd[:, r, :], pick[:, r], AX.X).then_inc(r_pick, 1)
                dve.wait_ge(r_pick, 2 * s + 2)
                V.tensor_copy(dest[:, r:r + 1], wd[:, r, 1:2]).then_inc(r_wd, 1)

            def down_low(g):
                dve.wait_ge(egu_hi, EXP + g + 1)
                V.tensor_tensor(dn_l[:, 4 * g:4 * g + 4], e_dn[0][:, 4 * g:4 * g + 4], dn_h[:, 4 * g:4 * g + 4].bitcast(F32),
                                ALU.subtract).then_inc(egu_lo, 1)

            down_low(0)
            low_in(0, 0)
            for s in range(PIPE0):
                low_in(s + 1, (s + 1) % 2)
                if s == 0:
                    down_low(1)
                mul(s, s % 2)
                if s:
                    keep_actT(s - 1, (s - 1) % 2)
                pick_row(s, s % RING, False)

            def vstep(s, j, again, more=True):
                q = (PIPE0 + j) % 2
                if more:
                    low_in(s + 1, 1 - q)
                dve.wait_ge(r_ta, s - 1)
                mul(s, q)
                if again:
                    dve.wait_ge(r_dn, s - 2)
                keep_actT(s - 1, 1 - q)
                pick_row(s, (PIPE0 + j) % RING, again)

            for j in range(RING):
                vstep(PIPE0 + j, j, j >= 2)
            with dve.Fori(PIPE0 + RING, SLOT_TILES - RING, RING) as i:
                for j in range(RING):
                    vstep(i + j, j, True)
            s = SLOT_TILES - 1
            vstep(s, s - PIPE0, True, more=False)
            dve.wait_ge(r_dn, s - 1)
            keep_actT(s, s % 2)

            for i in range(TILES):
                if i not in BACK_POOL:
                    dve.wait_ge(yk_loaded[back_group(i)], 16)
                    add_experts(V, i, link).then_inc(out_ready, 1)

        @block.tensor
        def _(pe):
            MM = nc.tensor.matmul
            TR = nc.tensor.transpose
            I = K["ident"]

            def product(out, pairs, start=True, stop=True, **kw):
                parts = [p for (ah, al, bh, bl) in pairs for p in ((ah, bh), (ah, bl), (al, bh))]
                for j, (a_, b_) in enumerate(parts):
                    ins = MM(out, a_, b_, start=start and j == 0, stop=stop and j == len(parts) - 1, **kw)
                return ins

            pe.wait_ge(ld_const, 16)
            for i in range(TILES):
                pe.wait_ge(wbd_ready, i + 1)
                pe.wait_ge(ld_x[i // 4], 16)
                MM(bank[i // 2][:, D * (i % 2):D * (i % 2) + D], wbd[:, i].rearrange("p b d -> p (b d)"), res[:, i],
                   start=True, stop=True).then_inc(hid_ready, 1)
            def turn_hid(h):
                for i in range(4 * h, 4 * h + 4):
                    pe.wait_ge(hn_ready, i + 1)
                    for k in range(KC):
                        ins = TR(bank[4 + 2 * h + k][:, P * (i % 4):P * (i % 4) + P], hnorm[:, i, P * k:P * k + P], I)
                    ins.then_inc(hnT_ready, 1)

            def hT_half(h):
                return [(hT_h[:, k, half(h)], hT_l[:, k, half(h)]) for k in range(KC)]

            def hT_tile(i):
                return [(hT_h[:, k, P * i:P * i + P], hT_l[:, k, P * i:P * i + P]) for k in range(KC)]

            def qk(h, m):
                done = (q_mm, k_mm)[m]
                for c in range(KC):
                    at = slice(P * c, P * c + P)
                    product(bank[qk_bank(h, m) + c][:, :], [(wqkv_h[:, m, k, at], wqkv_l[:, m, k, at]) + hT_half(h)[k]
                                                            for k in range(KC)]).then_inc(done, 1)

            def values(h):
                for g in range(2 * h, 2 * h + 2):
                    if g >= 2:
                        pe.wait_ge(v_kept, g - 1)
                    for tt in range(2):
                        ins = product(bank[4 + g % 2][:, D * tt:D * tt + D],
                                      [hT_tile(2 * g + tt)[k] + (wqkv_h[:, 2, k, :], wqkv_l[:, 2, k, :]) for k in range(KC)])
                    ins.then_inc(v_mm, 1)

            def scores(u):
                if u == 0:
                    pe.wait_ge(bf_ready, 4)
                    pe.wait_ge(q_kept, 2)
                if u == 2:
                    pe.wait_ge(q_kept, 4)
                if u % 2 == 0:
                    pe.wait_ge(kx_act, 2 * (u // 2) + 2)
                    pe.wait_ge(kx_dve, 2 * (u // 2) + 2)
                if u >= 4:
                    pe.wait_ge(shifted, u - 3)
                b_ = bank[u % 4]
                MM(b_[:, :], ident_b[:], spread(causal_b[:], 1, HEADS), start=True, stop=False, skip_group_check=True)
                for c in range(KC):
                    for b4 in range(4):
                        ins = MM(b_[SEQ * b4:SEQ * b4 + SEQ, 256 * c:256 * c + 256],
                                 qT[:, c, P * u + SEQ * b4:P * u + SEQ * b4 + SEQ],
                                 kx[:, u // 2 % 2, c, 4 * (u % 2) + b4].rearrange("p e k -> p (e k)"),
                                 start=False, stop=True, skip_group_check=True)
                ins.then_inc(scored, 1)

            turn_hid(0)
            pe.wait_ge(wqkv_lo, 2)
            pe.wait_ge(hT_hi, 2)
            pe.wait_ge(hT_lo, 2)
            qk(0, 1)
            turn_hid(1)
            qk(0, 0)
            values(0)
            pe.wait_ge(hT_hi, 4)
            pe.wait_ge(hT_lo, 4)
            qk(1, 1)
            pe.wait_ge(k_kept, 2)
            qk(1, 0)
            scores(0)
            values(1)
            scores(1)
            pe.wait_ge(ld_small, 48)
            pe.wait_ge(hT_lo, 4)
            pe.wait_ge(k_kept, 4)
            for c in range(KC):
                for k in range(KC):
                    ins = MM(bank[6][:, RANK * c:RANK * c + RANK], wo[:, k, P * c:P * c + P], a_raw[:, k, :],
                             start=(k == 0), stop=(k == KC - 1))
            ins.then_inc(woa_mm, 1)

            def up_unit(i):
                if i == 0:
                    pe.wait_ge(wu_lo, 2)
                    pe.wait_ge(woa_ready, 1)
                if i >= 2:
                    pe.wait_ge(up_ready, i - 1)
                f, h = i // 2, i % 2
                at = slice(P * f, P * f + P)
                product(bank[6 + i % 2][:, :], [(wu_h[:, k, at], wu_l[:, k, at]) + hT_half(h)[k]
                                                for k in range(KC)]).then_inc(up_mm, 1)

            def pv(u):
                pe.wait_ge(exd_act, u + 1)
                pe.wait_ge(exd_dve, u + 1)
                pe.wait_ge(v_kept, 4) if u < 2 else pe.wait_ge(attn_ready, u - 1)
                for c in range(KC):
                    for j in range(4):
                        ins = MM(bank[4 + u % 2][SEQ * j:SEQ * j + SEQ, 256 * c:256 * c + 256],
                                 v_sb[:, u, P * c + SEQ * j:P * c + SEQ * j + SEQ],
                                 exd[:, u % 2, 8 * c + 2 * j:8 * c + 2 * j + 2, :].rearrange("p e q -> p (e q)"),
                                 start=True, stop=True)
                ins.then_inc(pv_ready, 1)

            for u in range(TILES):
                if 2 <= u + 1 < TILES:
                    scores(u + 1)
                up_unit(2 * u)
                if u >= 2:
                    pv(u - 2)
                up_unit(2 * u + 1)
            pe.wait_ge(ab_hi, 2)
            pe.wait_ge(ab_lo, 2)
            pe.wait_ge(shifted, 6)
            for h in range(2):
                product(bank[h][:, :], [(a_h[:, k, :], a_l[:, k, :]) + hT_half(h)[k] for k in range(KC)]).then_inc(ha_mm, 1)

            def gate_base(i):
                if i == 0:
                    pe.wait_ge(wgd_lo, 4)
                if i < 2:
                    pe.wait_ge(up_ready, 2 * FC)
                elif i < 4:
                    pe.wait_ge(shifted, TILES)
                else:
                    pe.wait_ge(silu_ready, i - 3 if i < 6 else i - 1)
                f, h = i // 2, i % 2
                at = slice(P * f, P * f + P)
                product(bank[gate_bank(i)][:, :], [(wg_h[:, k, at], wg_l[:, k, at]) + hT_half(h)[k] for k in range(KC)],
                        stop=False)

            pv(TILES - 2)
            gate_base(0)
            pv(TILES - 1)
            gate_base(1)
            gate_base(2)
            pe.wait_ge(attn_ready, TILES)
            for k in range(KC):
                for h in range(2):
                    ins = MM(bank[4 + h][SEQ * h:SEQ * h + RANK, :], woa[:, k, :], attnT[:, k, half(h)],
                             start=(k == 0), stop=(k == KC - 1))
                    if k == KC - 1:
                        ins.then_inc(mod_mm, 1)
            gate_base(3)

            def gate_unit(i):
                gate_base(i)
                gate_mod(i)

            def gate_mod(i):
                f, h = i // 2, i % 2
                at = slice(P * f, P * f + P)
                if i < 2:
                    pe.wait_ge(ab_lo, 3)
                    pe.wait_ge(mod_act, h + 3)
                    pe.wait_ge(m_lo, h + 1)
                MM(bank[gate_bank(i)][:, :], b_stack[:, at], m_stack[:, half(h)], start=False, stop=True).then_inc(gate_mm, 1)

            def down(f):
                if f % 2 == 0:
                    pe.wait_ge(wgd_lo, 4 if f < 4 else f // 2 + 3)
                pe.wait_ge(act_lo, 2 * f + 2)
                if f == 0:
                    pe.wait_ge(silu_ready, 4)
                for i in range(TILES):
                    at = slice(P * i, P * i + P)
                    ins = product(bank[i // 2][:, D * (i % 2):D * (i % 2) + D],
                                  [(act_h[:, f, at], act_l[:, f % 2, at], wd_h[:, f, :], wd_l[:, f, :])],
                                  start=(f == 0 and i % 2 == 0), stop=(f == FC - 1), skip_group_check=True)
                    if f == FC - 1 and i % 2:
                        ins.then_inc(down_mm, 1)
                if f < FC - 1:
                    ins.then_inc(down_f, 1)

            for i in range(4):
                gate_mod(i)
            for f in range(FC):
                if f + 2 < FC:
                    gate_unit(2 * f + 4), gate_unit(2 * f + 5)
                down(f)

            for i in range(TILES):
                pe.wait_ge(x1_ready, i // 2 + 1)
                if i == 0:
                    pe.wait_ge(mod_act, 2)
                if i == 4:
                    pe.wait_ge(silu_ready, 2 * FC)
                for k in range(KC):
                    ins = TR(bank[4 + 2 * (i // 4) + k][:, P * (i % 4):P * (i % 4) + P], res[:, i, P * k:P * k + P], I)
                ins.then_inc(x1T_mm, 1)
            pe.wait_ge(l1_lo, 4)
            for h in range(2):
                pe.wait_ge(x1T_lo, 2 * h + 2)
                product(bank[h][:, :], [(aT_h[:, k, :], aT_l[:, k, :], x1T_h[:, k, half(h)], x1T_l[:, k, half(h)])
                                        for k in range(KC)]).then_inc(xa_mm, 1)
            for i in range(TILES):
                at = slice(P * i, P * i + P)
                product(bank[2 + i // 2][:, D * (i % 2):D * (i % 2) + D],
                        [(x1T_h[:, k, at], x1T_l[:, k, at], w1_h[:, k, :], w1_l[:, k, :]) for k in range(KC)],
                        start=(i % 2 == 0), stop=False, skip_group_check=True)
            for i in range(TILES):
                if i % 4 == 0:
                    pe.wait_ge(xam_lo, i // 4 + 1)
                at = slice(P * i, P * i + P)
                ins = product(bank[2 + i // 2][:, D * (i % 2):D * (i % 2) + D],
                              [(xam_h[:, at], xam_l[:, at], bm_h[:, :], bm_l[:, :])], start=False, skip_group_check=True)
                if i % 2:
                    ins.then_inc(h1_mm, 1)
            for i in range(TILES):
                pe.wait_ge(h1_ready, i // 2 + 1)
                for k in range(KC):
                    b_ = bank[((6, 7), (0, 1))[i // 4][k]]
                    ins = TR(b_[:, P * (i % 4):P * (i % 4) + P], rows[:, i, P * k:P * k + P], I)
                ins.then_inc(h1T_mm, 1)
            for h in range(2):
                pe.wait_ge(h1T_lo, 2 * h + 2)
                product(bank[2 + h][:, :], [(rw_h[:, k, :], rw_l[:, k, :]) + hT_half(h)[k] for k in range(KC)]).then_inc(lgT_mm, 1)
            for i in range(TILES):
                pe.wait_ge(lgT_kept, i // 4 + 1)
                ins = TR(bank[4][:, SEQ * i:SEQ * i + SEQ], lgT[:, P * i:P * i + P], I[0:SEQ, 0:SEQ])
            ins.then_inc(lg_mm, 1)

            def ranks():
                pe.wait_ge(member_ready, 1)
                mb = member[:].rearrange("p t e -> p (t e)")
                MM(bank[5][:, 0:P], before_b[:], mb, start=True, stop=False, skip_group_check=True)
                for d in range(1, TILES):
                    MM(bank[5][:, EXP * d:P], ones_b[:], mb[:, 0:P - EXP * d], start=False, stop=False,
                       skip_group_check=True)
                for i in range(TILES):
                    ins = MM(bank[5][:, P:P + EXP], ones_b[:], mb[:, EXP * i:EXP * i + EXP], start=False,
                             stop=(i == TILES - 1), skip_group_check=True)
                ins.then_inc(rank_mm, 1)

            def shared_gu(f):
                r = f % 2
                if f < 3:
                    pe.wait_ge(sh_lo_pool, (1, 2, 4)[f])
                else:
                    pe.wait_ge(sgu_lo_dve, f - 2)
                for h in range(2):
                    i = 2 * f + h
                    if i >= 2:
                        pe.wait_ge(s_act_ready, i - 1)
                    for m in range(2 if SHC[f][1] == P else 1):
                        ins = product(bank[((6, 7), (0, 1))[h][m]][:, :],
                                      [(sgu_h[:, r, m, k, :], sgu_l[:, r, m, k, :]) + hT_half(h)[k] for k in range(KC)])
                    ins.then_inc(sgu_mm, 1)

            def shared_down(f):
                last_f = f == len(SHC) - 1
                pe.wait_ge(s_act_lo, 2 * f + 2)
                if f == 0:
                    pe.wait_ge(sh_lo_pool, 3)
                    pe.wait_ge(rank_read, 1)
                if f >= 4:
                    pe.wait_ge(sdn_lo_dve, 4 if last_f else 1)
                for i in range(TILES):
                    at = slice(P * i, P * i + P)
                    ins = product(bank[2 + i // 2][:, D * (i % 2):D * (i % 2) + D],
                                  [(s_act_h[:, f % 3, at], s_act_l[:, f % 3, at], sdn_h[:, f % 4, :], sdn_l[:, f % 4, :])],
                                  start=(f == 0 and i % 2 == 0), stop=last_f, skip_group_check=True)
                    if last_f and i % 2:
                        ins.then_inc(sdn_mm, 1)
                if not last_f:
                    ins.then_inc(sdn_f, 1)

            for f in range(len(SHC)):
                shared_gu(f)
                if f == 0:
                    ranks()
                if f >= 2:
                    shared_down(f - 2)
            shared_down(len(SHC) - 2)
            shared_down(len(SHC) - 1)

            def turn_in(s, q, r, again):
                pe.wait_ge(r_loaded[r], ring_count(s, r))
                if again:
                    pe.wait_ge(r_lo, s - 1)
                for k in range(KC):
                    ins = TR(bank[2 + q][:, P * k:P * k + P], slot_rows[:, r, P * k:P * k + P], I)
                ins.then_inc(r_in, 1)

            def experts_of(s, n):
                return nc.values_load_multi_w_load_instructions(
                    who[0:1, bass.ds(s, n)], engines=[mybir.EngineType.PE], min_val=0, max_val=EXP - 1,
                    skip_runtime_bounds_check_because="one expert's number, picked by a one-hot row of hot_s")[1]

            def gate_up(s, e, q, again):
                pe.wait_ge(r_lo, s + 1)
                if again:
                    pe.wait_ge(r_act, s - 1)
                hi, lo = ([w[:].rearrange("p e k n -> p (e k) n")[:, bass.ds(e * KC + k, 1), :].rearrange("p a n -> p (a n)")
                           for k in range(KC)] for w in (e_gu_h, e_gu_l))
                product(bank[q][:, 0:2 * IM], [(e_in_h[:, q, k, :], e_in_l[:, q, k, :], hi[k], lo[k])
                                               for k in range(KC)]).then_inc(r_gu, 1)

            def turn_act(s, q, again):
                pe.wait_ge(r_act, s + 1)
                if again:
                    pe.wait_ge(r_actT, s - 1)
                for k in range(2):
                    ins = TR(bank[4 + q][0:IH, P * k:P * k + P], act[:, q, IH * k:IH * k + IH], I)
                ins.then_inc(r_ta, 1)

            def down_e(s, e, q, again):
                pe.wait_ge(r_actT, s + 1)
                if again:
                    pe.wait_ge(r_y, s - 1)
                hi, lo, rest = (w[:, bass.ds(e, 1), :].rearrange("p a n -> p (a n)") for w in (dn_h, dn_l, e_dn[1]))
                product(bank[6 + q][:, 0:D], [(actT_h[:, q, :], actT_l[:, q, :], hi, lo)], stop=False)
                MM(bank[6 + q][:, 0:D], actT[:, q, :], rest, start=False, stop=True).then_inc(r_dn, 1)

            pe.wait_ge(who_ready, 1)
            pe.wait_ge(shared_added, 4)
            experts = experts_of(0, RING + PIPE0)
            turn_in(0, 0, 0, False)
            turn_in(1, 1, 1, False)
            pe.wait_ge(egu_lo, EXP - len(split_pool))
            pe.wait_ge(sh_lo_pool, 4 + len(split_pool))
            gate_up(0, experts[0], 0, False)
            turn_in(2, 0, 2, True)
            gate_up(1, experts[1], 1, False)
            pe.wait_ge(shared_added, 8)
            turn_act(0, 0, False)
            pe.wait_ge(ld_down, 16 * (1 + 7))
            pe.wait_ge(egu_lo, EXP - len(split_pool) + 2)
            pe.wait_ge(sh_lo_pool, 4 + len(split_pool) + 2)

            def pstep(s, experts, j, again):
                q = (PIPE0 + j) % 2
                turn_in(s + 1, 1 - q, (PIPE0 + j + 1) % RING, True)
                gate_up(s, experts[j + PIPE0], q, True)
                turn_act(s - 1, 1 - q, again)
                down_e(s - 2, experts[j], q, again)

            for j in range(RING):
                pstep(PIPE0 + j, experts, j, j >= 2)
            with pe.Fori(PIPE0 + RING, SLOT_TILES - RING, RING) as i:
                experts = experts_of(i - 2, RING + PIPE0)
                for j in range(RING):
                    pstep(i + j, experts, j, True)
            s = SLOT_TILES - 1
            experts = experts_of(s - 2, 3)
            gate_up(s, experts[2], s % 2, True)
            turn_act(s - 1, (s - 1) % 2, True)
            down_e(s - 2, experts[0], s % 2, True)
            turn_act(s, s % 2, True)
            down_e(s - 1, experts[1], (s - 1) % 2, True)
            down_e(s, experts[2], s % 2, True)


def kernel(**inputs):
    import numpy as _np
    import concourse.bacc as _bacc
    from concourse import mybir as _mybir
    from concourse.bass_utils import run_bass_kernel_spmd as _run

    a = {k: _np.asarray(v) for k, v in inputs.items()}
    flip = lambda w: _np.ascontiguousarray(w.T)
    arrays = {
        "x": a["x"].reshape(TOK, D), "cond": flip(a["itok_B_1_198"].reshape(TILES, 4)), "adapter": a["itok_B_0_6"],
        "cond_w": a["L0_cond_weights"], 
        "norms": flip(_np.concatenate([a["L0_ffn_ln1_w"], a["L0_ffn_ln2_w"]]).reshape(2 * KC, P)),
        "WqT": flip(a["L0_ffn_Wq"]), "WkT": flip(a["L0_ffn_Wk"]), "WvT": flip(a["L0_ffn_Wv"]),
        "Wo": a["L0_ffn_Wo"], "A": a["L0_ffn_A"], "B": a["L0_ffn_B"],
        "WinT": flip(a["L0_ffn_W_in_base"]), "WupT": flip(a["L0_ffn_W_up_base"]), "WdT": flip(a["L0_ffn_W_down"]),
        "W1T": flip(a["L1_cond_W"]), "AT": flip(a["L1_cond_A"].reshape(P, D)),
        "BmT": _np.ascontiguousarray(a["L1_cond_Bm"].transpose(0, 2, 1)).reshape(P, D),
        "scale": a["L1_cond_scalings"],
        "router": _np.concatenate([flip(a["L1_ffn_router_w"]), a["L1_ffn_sh_gate_w"]], axis=1),
        "e_gu": _np.concatenate([a["L1_ffn_w_gate"], a["L1_ffn_w_up"]], axis=2), "e_dn": a["L1_ffn_w_down"],
        "s_gu": _np.concatenate([a["L1_ffn_sh_gate"], a["L1_ffn_sh_up"]], axis=1), "s_dn": a["L1_ffn_sh_down"],
        "consts": constants(), "pos": _np.arange(P, dtype=_np.float32).reshape(P, 1) % SEQ,
    }
    arrays = {f"in_{k}": _np.ascontiguousarray(v) for k, v in arrays.items()}
    nc = _bacc.Bacc("TRN2", target_bir_lowering=False, num_devices=1)
    t = {k[3:]: nc.dram_tensor(k, v.shape, _mybir.dt.from_np(v.dtype), kind="ExternalInput").ap()
         for k, v in arrays.items()}
    t["out"] = nc.dram_tensor("out", (TOK, D), F32, kind="ExternalOutput").ap()
    t["cond_b"] = bass.AP(t["cond"].tensor, 0, [[TILES, 4], [0, SEQ], [1, TILES]])
    t["adapter_b"] = bass.AP(t["adapter"].tensor, 0, [[0, P], [1, BATCH]])
    t["scale_p"] = bass.AP(t["scale"].tensor, 0, [[1, ADAPT], [0, RANK], [1, 1]])
    program(nc, t)
    r = _run(nc, [arrays], core_ids=[0])
    return r.results[0]["out"].reshape(BATCH, SEQ, D)
```
